# Optimizing a Trainium2 kernel written in Bass

```python
import numpy as np
import jax
import jax.numpy as jnp

def _softmax(x, axis=-1):
    return jax.nn.softmax(x, axis=axis)

def _gelu(x):
    return jax.nn.gelu(x, approximate=True)

def _silu(x):
    return jax.nn.silu(x)

def _sigmoid(x):
    return jax.nn.sigmoid(x)

def _layernorm(x, axis=-1, eps=1e-05):
    m = jnp.mean(x, axis=axis, keepdims=True)
    v = jnp.var(x, axis=axis, keepdims=True)
    return (x - m) / jnp.sqrt(v + eps)

def _scatter_add(tgt, idx, src, axis=0):
    return tgt.at[idx].add(src)

def _segment_sum(src, seg, n):
    return jax.ops.segment_sum(src, seg, n)
kernel_name = 'mk_macaron_d2_jaxref_r8_5fa341'

def setup_inputs(seed: int=0):
    np.random.seed(seed)
    _w = jnp.asarray

    def _L0_attn_setup():
        import jax, jax.numpy as jnp
        import numpy as np
        EPS = 1e-15
        HEAD_DIM = 32
        PAD_VAL = 1.0
        key = jax.random.key(seed)
        k1, k2, k3, k4 = jax.random.split(key, 4)
        B, N, C = (2, 512, 256)
        s = 1.0 / np.sqrt(C).astype(np.float32)
        x = jax.random.normal(k1, (B, N, C), jnp.float32)
        w_qkv = jax.random.normal(k2, (3 * C, C), jnp.float32) * s
        w_proj = jax.random.normal(k3, (C, C), jnp.float32) * s
        b_proj = jax.random.normal(k4, (C,), jnp.float32) * 0.01
        return {'x': x, 'w_qkv': w_qkv, 'w_proj': w_proj, 'b_proj': b_proj}
    _L0_attn_in = _L0_attn_setup()

    def _L0_ffn_setup():
        import jax, jax.numpy as jnp
        import numpy as np
        E, K, H, I = (64, 6, 256, 176)
        NS = 2
        IS = NS * I
        CAP = 32
        T_TOKENS = (1, 128)
        SCALE = 0.02

        def _moe_infer(x, gate_w, w_gate, w_up, w_down):
            T = x.shape[0]
            TK = T * K
            logits = x @ gate_w.T
            scores = jax.nn.softmax(logits, axis=-1)
            topk_w, topk_i = jax.lax.top_k(scores, K)
            flat_i = topk_i.reshape(-1)
            flat_w = topk_w.reshape(-1)
            token_ids = jnp.arange(TK, dtype=jnp.int32) // K
            order = jnp.argsort(flat_i)
            sorted_e = flat_i[order]
            counts = jnp.bincount(flat_i, length=E)
            starts = jnp.concatenate([jnp.zeros((1,), counts.dtype), jnp.cumsum(counts)[:-1]])
            pos_sorted = jnp.arange(TK) - starts[sorted_e]
            pos = jnp.zeros((TK,), jnp.int32).at[order].set(pos_sorted.astype(jnp.int32))
            valid = pos < CAP
            slot = jnp.where(valid, pos, CAP)
            buf = jnp.zeros((E, CAP + 1, H), x.dtype).at[flat_i, slot].set(x[token_ids])
            g = jnp.einsum('ech,ehi->eci', buf, w_gate)
            u = jnp.einsum('ech,ehi->eci', buf, w_up)
            y = jnp.einsum('eci,eih->ech', jax.nn.silu(g) * u, w_down)
            out_slots = y[flat_i, slot] * (flat_w * valid)[:, None]
            return out_slots.reshape(T, K, H).sum(axis=1)
        key = jax.random.key(seed)
        ks = jax.random.split(key, 8)
        f32 = jnp.float32
        return {'hidden_states': jax.random.normal(ks[0], (*T_TOKENS, H), f32), 'gate_w': jax.random.normal(ks[1], (E, H), f32) * SCALE, 'w_gate': jax.random.normal(ks[2], (E, H, I), f32) * SCALE, 'w_up': jax.random.normal(ks[3], (E, H, I), f32) * SCALE, 'w_down': jax.random.normal(ks[4], (E, I, H), f32) * SCALE, 'sw_gate': jax.random.normal(ks[5], (H, IS), f32) * SCALE, 'sw_up': jax.random.normal(ks[6], (H, IS), f32) * SCALE, 'sw_down': jax.random.normal(ks[7], (IS, H), f32) * SCALE}
    _L0_ffn_in = _L0_ffn_setup()

    def _L1_attn_setup():
        import jax, jax.numpy as jnp
        import numpy as np
        HIDDEN = 256
        N_HEADS = 16
        HEAD_DIM = HIDDEN // N_HEADS

        def rotate_half(x):
            x1, x2 = jnp.split(x, 2, axis=-1)
            return jnp.concatenate([-x2, x1], axis=-1)
        key = jax.random.key(seed)
        k0, k1, k2, k3, k4 = jax.random.split(key, 5)
        B, S = (1, 256)
        scale = 1.0 / np.sqrt(HIDDEN)
        return {'hidden_states': jax.random.normal(k0, (B, S, HIDDEN), dtype=jnp.float32), 'Wq': jax.random.normal(k1, (HIDDEN, HIDDEN), dtype=jnp.float32) * scale, 'Wk': jax.random.normal(k2, (HIDDEN, HIDDEN), dtype=jnp.float32) * scale, 'Wv': jax.random.normal(k3, (HIDDEN, HIDDEN), dtype=jnp.float32) * scale, 'Wo': jax.random.normal(k4, (HIDDEN, HIDDEN), dtype=jnp.float32) * scale, 'gate': jnp.zeros((1, N_HEADS, 1, 1), dtype=jnp.float32)}
    _L1_attn_in = _L1_attn_setup()

    def _L1_ffn_setup():
        import jax, jax.numpy as jnp
        import numpy as np
        B, S, D, E, TOPK, H = (8, 256, 256, 8, 2, 16)
        DH = D // H
        FH = D // H
        ROUTE_LEN = 256
        key = jax.random.key(seed)
        ks = jax.random.split(key, 8)
        s = 0.02
        return {'x': jax.random.normal(ks[0], (B, S, D), jnp.float32), 'switch_w': jax.random.normal(ks[1], (E, D * ROUTE_LEN), jnp.float32) * s, 'switch_b': jnp.zeros((E,), jnp.float32), 'w1': jax.random.normal(ks[2], (E, FH, DH), jnp.float32) * s, 'b1': jnp.zeros((E, FH), jnp.float32), 'w2': jax.random.normal(ks[3], (E, DH, FH), jnp.float32) * s, 'b2': jnp.zeros((E, DH), jnp.float32), 'w3': jax.random.normal(ks[4], (D, D), jnp.float32) * s, 'b3': jnp.zeros((D,), jnp.float32)}
    _L1_ffn_in = _L1_ffn_setup()
    _d = {'L0_attn_x': _L0_attn_in['x'], 'L0_attn_w_qkv': _L0_attn_in['w_qkv'], 'L0_attn_w_proj': _L0_attn_in['w_proj'], 'L0_attn_b_proj': _L0_attn_in['b_proj'], 'L0_ffn_gate_w': _L0_ffn_in['gate_w'], 'L0_ffn_w_gate': _L0_ffn_in['w_gate'], 'L0_ffn_w_up': _L0_ffn_in['w_up'], 'L0_ffn_w_down': _L0_ffn_in['w_down'], 'L0_ffn_sw_gate': _L0_ffn_in['sw_gate'], 'L0_ffn_sw_up': _L0_ffn_in['sw_up'], 'L0_ffn_sw_down': _L0_ffn_in['sw_down'], 'L1_attn_Wq': _L1_attn_in['Wq'], 'L1_attn_Wk': _L1_attn_in['Wk'], 'L1_attn_Wv': _L1_attn_in['Wv'], 'L1_attn_Wo': _L1_attn_in['Wo'], 'L1_attn_gate': _L1_attn_in['gate'], 'L1_ffn_switch_w': _L1_ffn_in['switch_w'], 'L1_ffn_switch_b': _L1_ffn_in['switch_b'], 'L1_ffn_w1': _L1_ffn_in['w1'], 'L1_ffn_b1': _L1_ffn_in['b1'], 'L1_ffn_w2': _L1_ffn_in['w2'], 'L1_ffn_b2': _L1_ffn_in['b2'], 'L1_ffn_w3': _L1_ffn_in['w3'], 'L1_ffn_b3': _L1_ffn_in['b3']}
    _x0 = _d['L0_attn_x']
    _d['L0_attn_x'] = jax.random.normal(jax.random.fold_in(jax.random.key(seed), 1), (1, 2048, 256), dtype=_x0.dtype)
    del _x0
    return _d

def reference(L0_attn_x, L0_attn_w_qkv, L0_attn_w_proj, L0_attn_b_proj, L0_ffn_gate_w, L0_ffn_w_gate, L0_ffn_w_up, L0_ffn_w_down, L0_ffn_sw_gate, L0_ffn_sw_up, L0_ffn_sw_down, L1_attn_Wq, L1_attn_Wk, L1_attn_Wv, L1_attn_Wo, L1_attn_gate, L1_ffn_switch_w, L1_ffn_switch_b, L1_ffn_w1, L1_ffn_b1, L1_ffn_w2, L1_ffn_b2, L1_ffn_w3, L1_ffn_b3):

    def _L0_attn_ref(x, w_qkv, w_proj, b_proj):
        import jax, jax.numpy as jnp
        import numpy as np
        EPS = 1e-15
        HEAD_DIM = 32
        PAD_VAL = 1.0
        B, N, C = x.shape
        d = HEAD_DIM
        h = C // d
        qkv = (x @ w_qkv.T).reshape(B, N, 3, C)
        q, k, v = (qkv[:, :, 0], qkv[:, :, 1], qkv[:, :, 2])

        def to_heads(t):
            return t.reshape(B, N, h, d).transpose(0, 2, 3, 1)
        q = jax.nn.relu(to_heads(q))
        k = jax.nn.relu(to_heads(k))
        v = to_heads(v)
        v_pad = jnp.pad(v, ((0, 0), (0, 0), (0, 1), (0, 0)), constant_values=PAD_VAL)
        vk = jnp.einsum('bhen,bhdn->bhed', v_pad, k)
        out = jnp.einsum('bhed,bhdn->bhen', vk, q)
        out = out[:, :, :-1] / (out[:, :, -1:] + EPS)
        out = out.reshape(B, C, N).transpose(0, 2, 1)
        return out @ w_proj.T + b_proj

    def _L0_ffn_ref(hidden_states, gate_w, w_gate, w_up, w_down, sw_gate, sw_up, sw_down):
        import jax, jax.numpy as jnp
        import numpy as np
        E, K, H, I = (64, 6, 256, 176)
        NS = 2
        IS = NS * I
        CAP = 32
        T_TOKENS = (1, 128)
        SCALE = 0.02

        def _moe_infer(x, gate_w, w_gate, w_up, w_down):
            T = x.shape[0]
            TK = T * K
            logits = x @ gate_w.T
            scores = jax.nn.softmax(logits, axis=-1)
            topk_w, topk_i = jax.lax.top_k(scores, K)
            flat_i = topk_i.reshape(-1)
            flat_w = topk_w.reshape(-1)
            token_ids = jnp.arange(TK, dtype=jnp.int32) // K
            order = jnp.argsort(flat_i)
            sorted_e = flat_i[order]
            counts = jnp.bincount(flat_i, length=E)
            starts = jnp.concatenate([jnp.zeros((1,), counts.dtype), jnp.cumsum(counts)[:-1]])
            pos_sorted = jnp.arange(TK) - starts[sorted_e]
            pos = jnp.zeros((TK,), jnp.int32).at[order].set(pos_sorted.astype(jnp.int32))
            valid = pos < CAP
            slot = jnp.where(valid, pos, CAP)
            buf = jnp.zeros((E, CAP + 1, H), x.dtype).at[flat_i, slot].set(x[token_ids])
            g = jnp.einsum('ech,ehi->eci', buf, w_gate)
            u = jnp.einsum('ech,ehi->eci', buf, w_up)
            y = jnp.einsum('eci,eih->ech', jax.nn.silu(g) * u, w_down)
            out_slots = y[flat_i, slot] * (flat_w * valid)[:, None]
            return out_slots.reshape(T, K, H).sum(axis=1)
        orig_shape = hidden_states.shape
        x = hidden_states.reshape(-1, orig_shape[-1])
        y = _moe_infer(x, gate_w, w_gate, w_up, w_down).reshape(orig_shape)
        shared = jax.nn.silu(hidden_states @ sw_gate) * (hidden_states @ sw_up) @ sw_down
        return y + shared

    def _L1_attn_ref(hidden_states, Wq, Wk, Wv, Wo, gate):
        import jax, jax.numpy as jnp
        import numpy as np
        HIDDEN = 256
        N_HEADS = 16
        HEAD_DIM = HIDDEN // N_HEADS

        def rotate_half(x):
            x1, x2 = jnp.split(x, 2, axis=-1)
            return jnp.concatenate([-x2, x1], axis=-1)
        B, S, H = hidden_states.shape
        q = hidden_states @ Wq.T
        k = hidden_states @ Wk.T
        v = hidden_states @ Wv.T
        inv_freq = 1.0 / 10000.0 ** (jnp.arange(0, H, 2, dtype=jnp.float32) / H)
        t = jnp.arange(S, dtype=jnp.float32)
        freqs = t[:, None] * inv_freq[None, :]
        emb = jnp.concatenate([freqs, freqs], axis=-1)[None]
        cos, sin = (jnp.cos(emb), jnp.sin(emb))
        q = q * cos + rotate_half(q) * sin
        k = k * cos + rotate_half(k) * sin

        def split_heads(x):
            return x.reshape(B, S, N_HEADS, HEAD_DIM).transpose(0, 2, 1, 3)
        q, k, v = (split_heads(q), split_heads(k), split_heads(v))
        k_feat = jax.nn.elu(k) + 1.0
        memory = jnp.einsum('bhsd,bhse->bhde', k_feat, v)
        norm_term = k_feat.sum(axis=2)
        q_feat = jax.nn.elu(q) + 1.0
        mem_out = jnp.einsum('bhsd,bhde->bhse', q_feat, memory)
        denom = jnp.einsum('bhsd,bhd->bhs', q_feat, norm_term)[..., None]
        mem_out = mem_out / denom
        scale = 1.0 / jnp.sqrt(jnp.float32(HEAD_DIM))
        scores = jnp.einsum('bhqd,bhkd->bhqk', q, k) * scale
        attn = jnp.einsum('bhqk,bhkd->bhqd', jax.nn.softmax(scores, axis=-1), v)
        g = jax.nn.sigmoid(gate)
        combined = g * mem_out + (1.0 - g) * attn
        combined = combined.transpose(0, 2, 1, 3).reshape(B, S, H)
        return combined @ Wo.T

    def _L1_ffn_ref(x, switch_w, switch_b, w1, b1, w2, b2, w3, b3):
        import jax, jax.numpy as jnp
        import numpy as np
        B, S, D, E, TOPK, H = (8, 256, 256, 8, 2, 16)
        DH = D // H
        FH = D // H
        ROUTE_LEN = 256
        b, s, d = x.shape
        x0 = x[:, :ROUTE_LEN].reshape(b, -1)
        logits = x0 @ switch_w.T + switch_b
        probs = jax.nn.softmax(logits, axis=-1)
        gate, top_idx = jax.lax.top_k(probs, TOPK)
        xh = x.reshape(b, s, H, DH).transpose(0, 2, 1, 3)
        w1s, b1s = (w1[top_idx], b1[top_idx])
        w2s, b2s = (w2[top_idx], b2[top_idx])
        h = jnp.einsum('bhsd,bkfd->bkhsf', xh, w1s) + b1s[:, :, None, None, :]
        h = jax.nn.gelu(h, approximate=False)
        o = jnp.einsum('bkhsf,bkdf->bkhsd', h, w2s) + b2s[:, :, None, None, :]
        o = (o * gate[:, :, None, None, None]).sum(axis=1)
        o = o.transpose(0, 2, 1, 3).reshape(b, s, d)
        out = x + o
        return out @ w3.T + b3
    x = L0_attn_x
    x = x + 0.5 * _L0_ffn_ref(_layernorm(x, axis=-1), L0_ffn_gate_w, L0_ffn_w_gate, L0_ffn_w_up, L0_ffn_w_down, L0_ffn_sw_gate, L0_ffn_sw_up, L0_ffn_sw_down)
    x = x + _L0_attn_ref(_layernorm(x, axis=-1), L0_attn_w_qkv, L0_attn_w_proj, L0_attn_b_proj)
    x = x + 0.5 * _L0_ffn_ref(_layernorm(x, axis=-1), L0_ffn_gate_w, L0_ffn_w_gate, L0_ffn_w_up, L0_ffn_w_down, L0_ffn_sw_gate, L0_ffn_sw_up, L0_ffn_sw_down)
    x = x + 0.5 * _L1_ffn_ref(_layernorm(x, axis=-1), L1_ffn_switch_w, L1_ffn_switch_b, L1_ffn_w1, L1_ffn_b1, L1_ffn_w2, L1_ffn_b2, L1_ffn_w3, L1_ffn_b3)
    x = x + _L1_attn_ref(_layernorm(x, axis=-1), L1_attn_Wq, L1_attn_Wk, L1_attn_Wv, L1_attn_Wo, L1_attn_gate)
    x = x + 0.5 * _L1_ffn_ref(_layernorm(x, axis=-1), L1_ffn_switch_w, L1_ffn_switch_b, L1_ffn_w1, L1_ffn_b1, L1_ffn_w2, L1_ffn_b2, L1_ffn_w3, L1_ffn_b3)
    return x

_drawn_inputs = setup_inputs


def setup_inputs(seed=0):
    import zlib

    import numpy as np

    out = dict(_drawn_inputs(seed))
    spreads = {'L1_attn_gate': (0.0, 2.0),
     'L1_ffn_switch_b': (0.0, 0.1),
     'L1_ffn_b1': (0.0, 0.8),
     'L1_ffn_b2': (0.0, 0.447),
     'L1_ffn_b3': (0.0, 0.1)}
    factors = {'L0_attn_b_proj': 4.364,
     'L0_ffn_gate_w': 8.0,
     'L0_ffn_w_gate': 8.0,
     'L0_ffn_w_up': 8.0,
     'L0_ffn_w_down': 8.0,
     'L0_ffn_sw_gate': 2.892,
     'L0_ffn_sw_up': 2.864,
     'L0_ffn_sw_down': 2.849,
     'L1_ffn_w1': 8.0,
     'L1_ffn_w2': 8.0,
     'L1_attn_Wq': 4.525,
     'L1_attn_Wk': 4.393}
    for name, (base, spread) in spreads.items():
        noise = np.random.default_rng([zlib.crc32(name.encode()), seed]).standard_normal(out[name].shape)
        drawn = base * np.exp(spread * noise) if base else spread * noise
        out[name] = jnp.asarray(drawn.astype(out[name].dtype))
    for name, factor in factors.items():
        out[name] = (out[name] * factor).astype(out[name].dtype)
    return out
```

```python
from contextlib import ExitStack

import numpy as np

import concourse.bass as bass
from concourse import mybir

F32 = mybir.dt.float32
BF16 = mybir.dt.bfloat16
U32 = mybir.dt.uint32
ACT = mybir.ActivationFunctionType
ALU = mybir.AluOpType
AX_X = mybir.AxisListType.X

P = 128
TOKENS = 2048
DIM = 256
TILES = TOKENS // P
CHUNKS = DIM // P
EPS = 1e-5

EXPERTS = 64
TOPK = 6
CAP = 32
INNER = 176
HALF = INNER // 2
SHARED = 352
EPG = P // CAP
GROUPS = EXPERTS // EPG
ROW = DIM + EXPERTS
SHARED_CHUNKS = [(0, 128), (128, 128), (256, 96)]
BIG = 3.0e38
WBUFS = 3

LHEADS, LHD = 8, 32
MIX_EXPERTS = 8
HEADS, HD = 16, 16
BLOCK = 512
BLOCKS = TOKENS // BLOCK
HPG = 4
HGROUPS = HEADS // HPG
STEPS = HGROUPS * BLOCKS
STACK = 6 * HD
STACK_M = STACK + 3
Q_PARTS = [0, 0, 1, 1, 0, 2]
K_PARTS = [0, 1, 0, 1, 2, 0]


class Chain:

    def __init__(self, eng, sem):
        self.eng, self.sem, self.n, self.turn = eng, sem, 0, None

    def at(self):
        return self.n if self.turn is None else self.n + self.turn[0] * self.turn[1]

    def __call__(self, ins):
        ins.then_inc(self.sem, 1)
        self.n += 1
        self.eng.wait_ge(self.sem, self.at())

    def enter(self, i, per):
        self.turn, self.start = (i, per), self.n

    def leave(self, trips):
        per = self.turn[1]
        assert self.n - self.start == per, (self.n - self.start, per)
        self.turn, self.n = None, self.start + per * trips


def build(nc, a, out, stages=6):
    ctx = ExitStack()
    with ctx:
        _program(nc, ctx, a, out, stages)


def _program(nc, ctx, a, out, stages):
    def sem(name):
        return ctx.enter_context(nc.semaphore(name))

    def sems(tag, names):
        return {n: sem(f"{tag}_{n}") for n in names.split()}

    made, calls = {}, {}

    def shared_sems(kind, totals):
        if kind not in made:
            made[kind] = sems(kind, " ".join(totals))
        n = calls[kind] = calls.get(kind, -1) + 1
        return made[kind], {k: n * v for k, v in totals.items()}

    def sb(name, shape, dt=F32):
        return ctx.enter_context(nc.sbuf_tensor(name, shape, dt))

    def dram(name, shape, dt=F32):
        return nc.dram_tensor(name, shape, dt, kind="Internal").ap()

    x = sb("x_res", [P, TILES, DIM])
    xn = sb("xn", [P, TILES, DIM])
    xnT = sb("xnT", [P, CHUNKS, TOKENS])
    stats = sb("stats", [P, TILES, 6])
    mv = sb("mv", [P, TILES, 2])
    rstd = sb("rstd", [P, 4, TILES])
    ident = sb("ident_sb", [P, P])
    ident_bf = sb("ident_bf", [P, P], BF16)
    AREA = 40400
    area = sb("area", [P, AREA])
    psum = ctx.enter_context(nc.psum_tensor("psum", [P, 8 * 512], F32))
    bank = [psum[:, 512 * i:512 * (i + 1)] for i in range(8)]

    class Carve:
        def __init__(self):
            self.at = 0

        def __call__(self, words, dt=F32, parts=P):
            v = area[0:parts, self.at:self.at + words]
            self.at += words
            assert self.at <= AREA, self.at
            return v if dt is F32 else v.bitcast(dt)

    s_const = sem("const_loaded")
    s_const2 = sem("const_made")
    s_x = sem("x_loaded")
    chain_sems = {e: sem(f"chain_{e}") for e in ("dve", "act", "pool")}
    chains = {}

    def layer_norm(tag, s_ready, n_ready):
        s, base = shared_sems("ln", dict(var=1, root=1, xn=TILES, tr=TILES // 2, xnT=TILES // 2))

        def dve(v):
            link = chains["dve"]
            v.wait_ge(s_ready, n_ready)
            for t in range(TILES):
                ins = nc.vector.bn_stats(stats[:, t, :], x[:, t, :])
            link(ins)
            for t in range(TILES):
                ins = nc.vector.bn_aggr(mv[:, t, :], stats[:, t, :])
            link(ins)
            var, r = rstd[:, 0, :], rstd[:, 2, :]
            nc.vector.tensor_scalar(var, mv[:, :, 1], EPS, None, ALU.add).then_inc(s["var"], 1)
            v.wait_ge(s["root"], base["root"] + 1)
            link(nc.vector.reciprocal(r, rstd[:, 1, :]))
            link(nc.vector.tensor_tensor(rstd[:, 3, :], r, r, ALU.mult))
            link(nc.vector.tensor_tensor(rstd[:, 3, :], rstd[:, 3, :], var, ALU.mult))
            link(nc.vector.tensor_scalar(rstd[:, 3, :], rstd[:, 3, :], -0.5, 1.5, ALU.mult, ALU.add))
            link(nc.vector.tensor_tensor(r, r, rstd[:, 3, :], ALU.mult))
            for t in range(TILES):
                nc.vector.tensor_scalar(xn[:, t, :], x[:, t, :], mv[:, t, 0:1], rstd[:, 2, t:t + 1],
                                        ALU.subtract, ALU.mult).then_inc(s["xn"], 1)

        def act(e):
            e.wait_ge(s["var"], base["var"] + 1)
            nc.scalar.activation(rstd[:, 1, :], rstd[:, 0, :], ACT.Sqrt).then_inc(s["root"], 1)
            for t2 in range(TILES // 2):
                e.wait_ge(s["tr"], base["tr"] + t2 + 1)
                nc.scalar.copy(xnT[:, :, 2 * P * t2:2 * P * (t2 + 1)].rearrange("p c (t n) -> p t c n", t=2),
                               bank[t2 % 2][:].rearrange("p (t c n) -> p t c n", t=2, c=CHUNKS)
                               ).then_inc(s["xnT"], 1)

        def pe(e):
            for t in range(TILES):
                e.wait_ge(s["xn"], base["xn"] + t + 1)
                if t % 2 == 0 and t >= 4:
                    e.wait_ge(s["xnT"], base["xnT"] + t // 2 - 1)
                for c in range(CHUNKS):
                    o = (t % 2) * 2 * P + c * P
                    ins = nc.tensor.transpose(bank[t // 2 % 2][:, o:o + P], xn[:, t, c * P:(c + 1) * P], ident[:])
                if t % 2:
                    ins.then_inc(s["tr"], 1)

        return (s, base), dve, act, pe

    table = dram("dispatch_table", [TOKENS + 1, ROW])
    slot_dram = dram("slot_tokens", [EXPERTS, CAP])

    def moe(tag, s_ready, n_ready):
        (ln, ln_base), ln_dve, ln_act, ln_pe = layer_norm(tag + "ln", s_ready, n_ready)
        s, base = shared_sems("moe", dict(
            w=96, wsh=64, rows=48, halfin=16, tokrow=32, logit=4, shmm=12, mt=2, tokt=1, xgt=GROUPS, gu=GROUPS, ht=GROUPS,
            y=GROUPS, mix=TILES, lgsb=5, exp=1, shg=12, shu=12, bufT=GROUPS, sg=GROUPS, hTsb=GROUPS, ysc=GROUPS, expin=1,
            msk=1, prob=2, key=2, half=1, tok=1, idx=1, sel=1, h=GROUPS, comb=TILES, out=TILES, hs=12, ysplit=GROUPS,
            gat0=64, gat1=64, gat2=64, gat3=64, wb0=48 * 6, wb1=48 * 5, wb2=48 * 5))
        s_w = [s[f"wb{b}"] for b in range(WBUFS)]
        s_gat = [s[f"gat{b}"] for b in range(4)]
        c = Carve()
        gu_w = [c(EPG * CHUNKS * SHARED).rearrange("p (e k i) -> p e k i", e=EPG, k=CHUNKS) for _ in range(WBUFS)]
        dn_w = [c(EPG * 2 * DIM).rearrange("p (e k d) -> p e k d", e=EPG, k=2) for _ in range(WBUFS)]
        hsT = c(3 * TOKENS).rearrange("p (c n) -> p c n", c=3)
        top = c.at
        lg = c(TILES * 66).rearrange("p (t e) -> p t e", t=TILES)
        rep = c(TILES * 66).rearrange("p (t e) -> p t e", t=TILES)
        msk = c(TILES * EXPERTS).rearrange("p (t h e) -> p t h e", t=TILES // 2, h=2)
        keyA = c(TOKENS // 2)
        keyB = c(TOKENS // 2)
        end = c.at
        c.at = top
        yp = c(3 * GROUPS * DIM // 2, BF16).rearrange("p (k g d) -> p k g d", k=3, g=GROUPS)
        c.at = max(c.at, end)
        top = c.at
        xg = c(GROUPS * ROW).rearrange("p (g r) -> p g r", g=GROUPS)
        end = c.at
        c.at = top
        prob = c(TILES * EXPERTS).rearrange("p (t e) -> p t e", t=TILES)
        sg_sh = [c(512) for _ in range(2)]
        su_sh = [c(512) for _ in range(2)]
        assert c.at <= end
        c.at = end
        top = c.at
        oneh = [c(GROUPS * P // 2, BF16).rearrange("p (g n) -> p g n", g=GROUPS) for _ in range(2)]
        c.at = top
        bufT = [c(DIM).rearrange("p (k n) -> p k n", k=2) for _ in range(2)]
        sg = [c(INNER) for _ in range(2)]
        hh = [c(INNER) for _ in range(2)]
        hT = [c(DIM).rearrange("p (k n) -> p k n", k=2) for _ in range(2)]
        ysc = [c(DIM) for _ in range(2)]
        yres = [c(DIM) for _ in range(1)]
        c.at = max(c.at, top + GROUPS * P)
        gate = c(2 * P).rearrange("p (k e) -> p k e", k=2)
        sh_w = c(CHUNKS * 2 * SHARED).rearrange("p (k g i) -> p k g i", k=CHUNKS, g=2)
        sh_d = c(3 * DIM).rearrange("p (c d) -> p c d", c=3)
        v8 = c(TILES * 8).rearrange("p (t e) -> p t e", t=TILES)
        r8 = c(TILES * 8).rearrange("p (t e) -> p t e", t=TILES)
        esum = c(TILES)
        einv = c(TILES)
        top32 = c(64)
        best = c(CAP)
        bestB = c(64)
        tok = c(CAP)
        tokrow = c(P, parts=GROUPS)
        tokp = c(GROUPS)
        idx = c(GROUPS, U32)
        rel = c(TILES * GROUPS // 2, BF16).rearrange("p (t g) -> p t g", t=TILES)
        wsel = c(GROUPS)
        junk = c(EPG)
        iota_n = c(TOKENS // 2)
        iota_bf = c(P // 2, BF16)
        tile_off = c(TILES)
        key_off = c(1)
        jmask = c(EPG)
        zrow = c(ROW, parts=1)
        w_gate, w_up, w_down = a["L0_ffn_w_gate"], a["L0_ffn_w_up"], a["L0_ffn_w_down"]

        def load_group(e, g):
            b = g % WBUFS
            if g >= WBUFS:
                e.wait_ge(s["y"], base["y"] + g - WBUFS + 1)
            es = slice(EPG * g, EPG * (g + 1))
            e.dma_start(gu_w[b][:, :, :, 0:INNER], w_gate[es].rearrange("e (k p) i -> p e k i", p=P)).then_inc(s_w[b], 16)
            e.dma_start(gu_w[b][:, :, :, INNER:SHARED], w_up[es].rearrange("e (k p) i -> p e k i", p=P)).then_inc(s_w[b], 16)
            e.dma_start(dn_w[b][0:HALF], w_down[es].rearrange("e (k p) d -> p e k d", p=HALF)).then_inc(s_w[b], 16)

        def sync(e):
            e.wait_ge(s_ready, n_ready)
            e.dma_start(gate[:, :, 0:EXPERTS], a["gate_T"].rearrange("(k p) e -> p k e", p=P)).then_inc(s["w"], 16)
            for dst, src in ((iota_n, "iota_row"), (iota_bf, "iota_bf"), (tile_off, "tile_off"),
                             (key_off, "key_off"), (jmask, "slot_mask")):
                e.dma_start(dst, a[src]).then_inc(s["w"], 16)
            e.dma_start(sh_w[:, :, 0, :], a["L0_ffn_sw_gate"].rearrange("(k p) i -> p k i", p=P)).then_inc(s["wsh"], 16)
            e.dma_start(sh_w[:, :, 1, :], a["L0_ffn_sw_up"].rearrange("(k p) i -> p k i", p=P)).then_inc(s["wsh"], 16)
            e.dma_start(sh_d[:, 0:2, :], a["L0_ffn_sw_down"][0:2 * P].rearrange("(c p) d -> p c d", p=P)).then_inc(s["wsh"], 16)
            e.dma_start(sh_d[0:96, 2, :], a["L0_ffn_sw_down"][2 * P:SHARED]).then_inc(s["wsh"], 16)
            for g in range(WBUFS):
                load_group(e, g)
            e.wait_ge(ln["xn"], ln_base["xn"] + TILES)
            body = table[0:TOKENS].rearrange("(t p) r -> p t r", p=P)
            e.dma_start(body[:, :, 0:DIM], xn[:]).then_inc(s["rows"], 16)
            e.wait_ge(s["prob"], base["prob"] + 2)
            e.dma_start(body[:, :, DIM:ROW], prob).then_inc(s["rows"], 16)
            e.dma_start(table[TOKENS:TOKENS + 1], zrow).then_inc(s["rows"], 16)
            e.wait_ge(s["half"], base["half"] + 1)
            e.dma_start(top32[0:64, CAP:2 * CAP], top32[64:128, 0:CAP]).then_inc(s["halfin"], 16)
            e.wait_ge(s["tok"], base["tok"] + 1)
            e.dma_start(slot_dram, tok[0:EXPERTS]).then_inc(s["tokrow"], 16)
            e.wait_ge(s["tokrow"], base["tokrow"] + 16)
            e.dma_start(tokrow, slot_dram.rearrange("(g j) c -> g (j c)", j=EPG)).then_inc(s["tokrow"], 16)
            for g in range(WBUFS, GROUPS):
                load_group(e, g)

        def pe(e):
            ln_pe(e)
            e.wait_ge(s["w"], base["w"] + 6 * 16)
            e.wait_ge(s["lgsb"], base["lgsb"] + 1)
            for t in range(TILES):
                e.wait_ge(ln["xnT"], ln_base["xnT"] + t // 2 + 1)
                b = bank[2 + t // 4 % 2]
                if t % 4 == 0 and t >= 8:
                    e.wait_ge(s["lgsb"], base["lgsb"] + 1 + t // 4 - 1)
                for k in range(CHUNKS):
                    ins = nc.tensor.matmul(b[:, (t % 4) * P:(t % 4 + 1) * P], xnT[:, k, t * P:(t + 1) * P],
                                           gate[:, k, :], start=(k == 0), stop=(k == CHUNKS - 1))
                if t % 4 == 3:
                    ins.then_inc(s["logit"], 1)
            e.wait_ge(s["wsh"], base["wsh"] + 64)

            def shared_up(n):
                blk, ch = n // 3, n % 3
                lo, w = SHARED_CHUNKS[ch]
                if n >= 2:
                    e.wait_ge(s["shu"], base["shu"] + n - 1)
                for gu in range(2):
                    for k in range(CHUNKS):
                        ins = nc.tensor.matmul(bank[4 + 2 * (n % 2) + gu][0:w, :], sh_w[:, k, gu, lo:lo + w],
                                               xnT[:, k, blk * BLOCK:(blk + 1) * BLOCK],
                                               start=(k == 0), stop=(k == CHUNKS - 1))
                ins.then_inc(s["shmm"], 1)

            for n in range(5):
                shared_up(n)
            e.wait_ge(s["msk"], base["msk"] + 1)
            e.wait_ge(s["lgsb"], base["lgsb"] + 5)
            for i in range(TILES // 2):
                ins = nc.tensor.transpose(bank[2 + i // 4][:, (i % 4) * P:(i % 4 + 1) * P],
                                          msk[:, i, :, :].rearrange("p h e -> p (h e)"), ident[:])
                if i % 4 == 3:
                    ins.then_inc(s["mt"], 1)
            for n in range(5, 12):
                shared_up(n)
            e.wait_ge(s["tokrow"], base["tokrow"] + 32)
            e.wait_ge(s["key"], base["key"] + 2)
            nc.tensor.transpose(bank[2][:, 0:GROUPS], tokrow, ident[0:GROUPS, 0:GROUPS]).then_inc(s["tokt"], 1)

            def rows_T(g):
                e.wait_ge(s_gat[g // 4], base["gat0"] + 64)
                if g >= 2:
                    e.wait_ge(s["bufT"], base["bufT"] + g - 1)
                for k in range(CHUNKS):
                    ins = nc.tensor.transpose(bank[g % 2][:, k * P:(k + 1) * P], xg[:, g, k * P:(k + 1) * P], ident[:])
                ins.then_inc(s["xgt"], 1)

            def gate_up(g):
                e.wait_ge(s_w[g % WBUFS], base[f"wb{g % WBUFS}"] + 48 * (g // WBUFS + 1))
                e.wait_ge(s["bufT"], base["bufT"] + g + 1)
                if g >= 2:
                    e.wait_ge(s["h"], base["h"] + g - 1)
                else:
                    e.wait_ge(s["idx"], base["idx"] + 1)
                for k in range(CHUNKS):
                    for j in range(EPG):
                        ins = nc.tensor.matmul(bank[2 + g % 2][CAP * j:CAP * (j + 1), 0:SHARED],
                                               bufT[g % 2][:, k, CAP * j:CAP * (j + 1)], gu_w[g % WBUFS][:, j, k, :],
                                               start=(k == 0), stop=(k == CHUNKS - 1))
                ins.then_inc(s["gu"], 1)

            def hidden_T(g):
                e.wait_ge(s["h"], base["h"] + g + 1)
                if g >= 2:
                    e.wait_ge(s["hTsb"], base["hTsb"] + g - 1)
                else:
                    e.wait_ge(s["shu"], base["shu"] + 12)
                for k in range(2):
                    ins = nc.tensor.transpose(bank[4 + g % 2][0:HALF, k * P:(k + 1) * P],
                                              hh[g % 2][:, k * HALF:(k + 1) * HALF], ident[:])
                ins.then_inc(s["ht"], 1)

            def down(g):
                e.wait_ge(s["hTsb"], base["hTsb"] + g + 1)
                if g >= 2:
                    e.wait_ge(s["ysc"], base["ysc"] + g - 1)
                for k in range(2):
                    for j in range(EPG):
                        ins = nc.tensor.matmul(bank[6 + g % 2][CAP * j:CAP * (j + 1), 0:DIM],
                                               hT[g % 2][0:HALF, k, CAP * j:CAP * (j + 1)],
                                               dn_w[g % WBUFS][0:HALF, j, k, :], start=(k == 0), stop=(k == 1))
                ins.then_inc(s["y"], 1)

            rows_T(0)
            for g in range(GROUPS + 1):
                if g < GROUPS:
                    gate_up(g)
                if g >= 1:
                    hidden_T(g - 1)
                if g + 1 < GROUPS:
                    rows_T(g + 1)
                if g >= 1:
                    down(g - 1)
            e.wait_ge(s["hs"], base["hs"] + 12)
            for t in range(TILES):
                if t >= 2:
                    e.wait_ge(s["out"], base["out"] + t - 1)
                b = bank[t % 2][:, 0:DIM]
                for ch, (lo, w) in enumerate(SHARED_CHUNKS):
                    nc.tensor.matmul(b, hsT[0:w, ch, t * P:(t + 1) * P], sh_d[0:w, ch, :], start=(ch == 0), stop=False)
                e.wait_ge(s["comb"], base["comb"] + t + 1)
                if t == 0:
                    e.wait_ge(s["ysplit"], base["ysplit"] + GROUPS)
                for g in range(GROUPS):
                    for k in range(3):
                        last = g == GROUPS - 1 and k == 2
                        ins = nc.tensor.matmul(b, oneh[t % 2][:, g, :], yp[:, k, g, :], start=False, stop=last)
                ins.then_inc(s["mix"], 1)

        def act(e):
            ln_act(e)
            for q in range(TILES // 4):
                e.wait_ge(s["logit"], base["logit"] + q + 1)
                nc.scalar.copy(lg[:, 4 * q:4 * q + 4, 0:EXPERTS],
                               bank[2 + q % 2][:].rearrange("p (t e) -> p t e", t=4)[:, :, 0:EXPERTS]
                               ).then_inc(s["lgsb"], 1)

            def shared(n):
                w = SHARED_CHUNKS[n % 3][1]
                e.wait_ge(s["shmm"], base["shmm"] + n + 1)
                if n >= 2:
                    e.wait_ge(s["hs"], base["hs"] + n - 1)
                nc.scalar.activation(sg_sh[n % 2][0:w], bank[4 + 2 * (n % 2)][0:w, :], ACT.Silu).then_inc(s["shg"], 1)
                nc.scalar.copy(su_sh[n % 2][0:w], bank[5 + 2 * (n % 2)][0:w, :]).then_inc(s["shu"], 1)

            e.wait_ge(s["expin"], base["expin"] + 1)
            nc.scalar.activation(prob, prob, ACT.Exp).then_inc(s["exp"], 1)
            for n in range(12):
                shared(n)
            for g in range(GROUPS + 2):
                if g < GROUPS:
                    e.wait_ge(s["xgt"], base["xgt"] + g + 1)
                    if g >= 2:
                        e.wait_ge(s["gu"], base["gu"] + g - 1)
                    nc.scalar.copy(bufT[g % 2], bank[g % 2][:, 0:DIM].rearrange("p (k n) -> p k n", k=2)
                                   ).then_inc(s["bufT"], 1)
                    e.wait_ge(s["gu"], base["gu"] + g + 1)
                    if g >= 2:
                        e.wait_ge(s["h"], base["h"] + g - 1)
                    nc.scalar.activation(sg[g % 2], bank[2 + g % 2][:, 0:INNER], ACT.Silu).then_inc(s["sg"], 1)
                if 1 <= g <= GROUPS:
                    e.wait_ge(s["ht"], base["ht"] + g)
                    if g >= 3:
                        e.wait_ge(s["y"], base["y"] + g - 2)
                    nc.scalar.copy(hT[(g - 1) % 2][0:HALF], bank[4 + (g - 1) % 2][0:HALF, 0:DIM]
                                   .rearrange("p (k n) -> p k n", k=2)).then_inc(s["hTsb"], 1)
                if g >= 2:
                    e.wait_ge(s["y"], base["y"] + g - 1)
                    e.wait_ge(s["sel"], base["sel"] + 1)
                    if g >= 4:
                        e.wait_ge(s["ysplit"], base["ysplit"] + g - 3)
                    nc.scalar.activation(ysc[g % 2], bank[6 + g % 2][:, 0:DIM], ACT.Copy,
                                         scale=wsel[:, g - 2:g - 1]).then_inc(s["ysc"], 1)

        def dve(v):
            link = chains["dve"]
            ln_dve(v)
            v.wait_ge(s_ready, n_ready)
            nc.vector.memset(gate[:, :, EXPERTS:P], 0.0)
            nc.vector.memset(lg[:, :, EXPERTS:66], -BIG)
            nc.vector.memset(zrow, 0.0)
            nc.vector.memset(r8[:, :, TOPK:8], -BIG).then_inc(s["lgsb"], 1)
            for t in range(TILES):
                if t % 4 == 0:
                    v.wait_ge(s["lgsb"], base["lgsb"] + 2 + t // 4)
                ins = nc.vector.max(v8[:, t, :], lg[:, t, 0:EXPERTS])
            link(ins)
            nc.vector.tensor_tensor(prob, lg[:, :, 0:EXPERTS], v8[:, :, 0:1].to_broadcast([P, TILES, EXPERTS]),
                                    ALU.subtract).then_inc(s["expin"], 1)
            link(nc.vector.tensor_copy(r8[:, :, 0:TOPK], v8[:, :, 0:TOPK]))
            for t in range(TILES):
                ins = nc.vector.match_replace(rep[:, t, :], r8[:, t, :], lg[:, t, :], BIG)
            link(ins)
            for h in range(2):
                ins = nc.vector.tensor_scalar(msk[:, :, h, :], rep[:, h * 8:(h + 1) * 8, 0:EXPERTS], 1.0e38, None, ALU.is_gt)
            ins.then_inc(s["msk"], 1)
            v.wait_ge(s["exp"], base["exp"] + 1)
            link(nc.vector.tensor_reduce(esum, prob, AX_X, ALU.add))
            link(nc.vector.reciprocal(einv, esum))
            nc.vector.tensor_tensor(prob, prob, einv.rearrange("p (t o) -> p t o", o=1).to_broadcast([P, TILES, EXPERTS]),
                                    ALU.mult).then_inc(s["prob"], 2)
            for i in range(2):
                v.wait_ge(s["mt"], base["mt"] + i + 1)
                ins = nc.vector.scalar_tensor_tensor(out=keyA[:, 512 * i:512 * (i + 1)], in0=iota_n[:, 512 * i:512 * (i + 1)],
                                                     scalar=key_off, in1=bank[2 + i][:], op0=ALU.add, op1=ALU.mult)
                ins.then_inc(s["key"], 1)
            v.wait_ge(s["key"], base["key"] + 2)
            src, dst = keyA, keyB
            for r in range(CAP // 8):
                ins = nc.vector.max(top32[:, 8 * r:8 * r + 8], src)
                if r == CAP // 8 - 1:
                    ins.then_inc(s["half"], 1)
                else:
                    link(ins)
                    link(nc.vector.match_replace(dst, top32[:, 8 * r:8 * r + 8], src, 0.0))
                    src, dst = dst, src
            v.wait_ge(s["halfin"], base["halfin"] + 16)
            v.wait_ge(s["half"], base["half"] + 1)
            src, dst = top32[0:EXPERTS], bestB[0:EXPERTS]
            for r in range(CAP // 8):
                link(nc.vector.max(best[0:EXPERTS, 8 * r:8 * r + 8], src))
                if r < CAP // 8 - 1:
                    link(nc.vector.match_replace(dst, best[0:EXPERTS, 8 * r:8 * r + 8], src, 0.0))
                    src, dst = dst, src
            nc.vector.tensor_scalar(tok[0:EXPERTS], best[0:EXPERTS], -1.0, float(TOKENS), ALU.mult, ALU.add
                                    ).then_inc(s["tok"], 1)
            v.wait_ge(s["tokt"], base["tokt"] + 1)
            nc.vector.tensor_copy(tokp, bank[2][:, 0:GROUPS])
            nc.vector.tensor_copy(idx, bank[2][:, 0:GROUPS]).then_inc(s["idx"], 1)
            v.wait_ge(s["idx"], base["idx"] + 1)
            link(nc.vector.tensor_tensor(rel, tokp.rearrange("p (o g) -> p o g", o=1).to_broadcast([P, TILES, GROUPS]),
                                         tile_off.rearrange("p (t o) -> p t o", o=1).to_broadcast([P, TILES, GROUPS]),
                                         ALU.subtract))
            for b in range(4):
                v.wait_ge(s_gat[b], base["gat0"] + 64)
            for g in range(GROUPS):
                o = DIM + EPG * g
                ins = nc.vector.tensor_tensor_reduce(out=junk, in0=xg[:, g, o:o + EPG], in1=jmask, scale=1.0,
                                                     scalar=0.0, op0=ALU.mult, op1=ALU.add, accum_out=wsel[:, g:g + 1])
                if g < GROUPS - 1:
                    link(ins)
                else:
                    ins.then_inc(s["sel"], 1)
            for g in range(GROUPS):
                v.wait_ge(s["sg"], base["sg"] + g + 1)
                if g >= 2:
                    v.wait_ge(s["ht"], base["ht"] + g - 1)
                nc.vector.tensor_tensor(hh[g % 2], sg[g % 2], bank[2 + g % 2][:, INNER:SHARED], ALU.mult
                                        ).then_inc(s["h"], 1)
            v.wait_ge(s["ysplit"], base["ysplit"] + GROUPS)
            for t in range(TILES + 1):
                if t < TILES:
                    if t >= 2:
                        v.wait_ge(s["mix"], base["mix"] + t - 1)
                    nc.vector.tensor_tensor(oneh[t % 2],
                                            rel[:, t, :].rearrange("p (g o) -> p g o", o=1).to_broadcast([P, GROUPS, P]),
                                            iota_bf.rearrange("p (o n) -> p o n", o=1).to_broadcast([P, GROUPS, P]),
                                            ALU.is_equal).then_inc(s["comb"], 1)
                if t >= 1:
                    v.wait_ge(s["mix"], base["mix"] + t)
                    nc.vector.scalar_tensor_tensor(out=x[:, t - 1, :], in0=bank[(t - 1) % 2][:, 0:DIM], scalar=0.5,
                                                   in1=x[:, t - 1, :], op0=ALU.mult, op1=ALU.add).then_inc(s["out"], 1)

        def pool(e):
            link = chains["pool"]
            for n in range(12):
                blk, ch = n // 3, n % 3
                w = SHARED_CHUNKS[ch][1]
                e.wait_ge(s["shg"], base["shg"] + n + 1)
                e.wait_ge(s["shu"], base["shu"] + n + 1)
                nc.gpsimd.tensor_tensor(hsT[0:w, ch, blk * BLOCK:(blk + 1) * BLOCK], sg_sh[n % 2][0:w], su_sh[n % 2][0:w],
                                        ALU.mult).then_inc(s["hs"], 1)
            e.wait_ge(s["idx"], base["idx"] + 1)
            e.wait_ge(s["rows"], base["rows"] + 48)
            e.wait_ge(s["hs"], base["hs"] + 12)
            for g in range(GROUPS):
                e.indirect_dma_start(xg[:, g, :], None, table, bass.IndirectOffsetOnAxis(ap=idx[:, g:g + 1], axis=0)
                                     ).then_inc(s_gat[g // 4], 16)
            for g in range(GROUPS):
                e.wait_ge(s["ysc"], base["ysc"] + g + 1)
                y, r = ysc[g % 2], yres[0]
                link(nc.gpsimd.tensor_copy(yp[:, 0, g, :], y))
                link(nc.gpsimd.tensor_tensor(r, y, yp[:, 0, g, :], ALU.subtract))
                link(nc.gpsimd.tensor_copy(yp[:, 1, g, :], r))
                link(nc.gpsimd.tensor_tensor(r, r, yp[:, 1, g, :], ALU.subtract))
                nc.gpsimd.tensor_copy(yp[:, 2, g, :], r).then_inc(s["ysplit"], 1)
                e.wait_ge(s["ysplit"], base["ysplit"] + g + 1)

        return (s["out"], base["out"] + TILES), dict(sync=sync, tensor=pe, scalar=act, vector=dve, gpsimd=pool)

    def linear_attention(tag, s_ready, n_ready):
        (ln, ln_base), ln_dve, ln_act, ln_pe = layer_norm(tag + "ln", s_ready, n_ready)
        s = sems(tag, "w kv kr vv vk mem qmm qT o on ot oT pj xb out")
        c = Carve()
        wq = c(CHUNKS * DIM).rearrange("p (k e) -> p k e", k=CHUNKS)
        wkv = c(CHUNKS * 2 * DIM).rearrange("p (k e) -> p k e", k=CHUNKS)
        wp = c(CHUNKS * DIM).rearrange("p (k e) -> p k e", k=CHUNKS)
        bp = c(DIM)
        hmask = c(4)
        kr = [c(DIM) for _ in range(2)]
        vv = [c(2 * 129).rearrange("p (c n) -> p c n", c=2) for _ in range(2)]
        qT = c(CHUNKS * TOKENS).rearrange("p (c n) -> p c n", c=CHUNKS)
        W33 = 4 * (LHD + 1)
        mem = c(2 * W33).rearrange("p (c h n) -> p c h n", c=2, h=4)
        den = [c(LHEADS) for _ in range(2)]
        on = [c(DIM) for _ in range(2)]
        oT = [c(DIM).rearrange("p (c n) -> p c n", c=2) for _ in range(2)]

        def sync(e):
            e.wait_ge(s_ready, n_ready)
            e.dma_start(wkv, a["wkv_T"].rearrange("(k p) e -> p k e", p=P)).then_inc(s["w"], 16)
            e.dma_start(wq, a["wq_T"].rearrange("(k p) e -> p k e", p=P)).then_inc(s["w"], 16)
            e.dma_start(wp, a["wproj_T"].rearrange("(k p) e -> p k e", p=P)).then_inc(s["w"], 16)
            e.dma_start(hmask, a["mask32"]).then_inc(s["w"], 16)
            e.dma_start(bp, a["L0_attn_b_proj"].rearrange("(o d) -> o d", o=1).to_broadcast([P, DIM])).then_inc(s["w"], 16)

        def pe(e):
            ln_pe(e)
            e.wait_ge(s["w"], 80)
            for t in range(TILES):
                e.wait_ge(ln["xnT"], ln_base["xnT"] + t // 2 + 1)
                if t >= 2:
                    e.wait_ge(s["kr"], t - 1)
                    e.wait_ge(s["vv"], t - 1)
                for half in range(2):
                    for k in range(CHUNKS):
                        ins = nc.tensor.matmul(bank[2 + 4 * half + t % 2][:, 0:DIM], xnT[:, k, t * P:(t + 1) * P],
                                               wkv[:, k, half * DIM:(half + 1) * DIM], start=(k == 0), stop=(k == 1))
                ins.then_inc(s["kv"], 1)
                if t >= 1:
                    memory(e, t - 1)
            memory(e, TILES - 1)
            for n in range(CHUNKS * BLOCKS):
                ch, blk = n // BLOCKS, n % BLOCKS
                if n >= 2:
                    e.wait_ge(s["qT"], n - 1)
                for k in range(CHUNKS):
                    ins = nc.tensor.matmul(bank[6 + n % 2][:], wq[:, k, ch * P:(ch + 1) * P],
                                           xnT[:, k, blk * BLOCK:(blk + 1) * BLOCK], start=(k == 0), stop=(k == 1))
                ins.then_inc(s["qmm"], 1)
            e.wait_ge(s["qT"], CHUNKS * BLOCKS)
            e.wait_ge(s["mem"], 2)
            for t in range(TILES + 1):
                if t < TILES:
                    if t >= 2:
                        e.wait_ge(s["on"], t - 1)
                    for ch in range(CHUNKS):
                        ins = nc.tensor.matmul(bank[t % 2][:, ch * W33:(ch + 1) * W33], qT[:, ch, t * P:(t + 1) * P],
                                               mem[:, ch], start=True, stop=True)
                    ins.then_inc(s["o"], 1)
                if t >= 1:
                    u = t - 1
                    e.wait_ge(s["on"], u + 1)
                    if u >= 2:
                        e.wait_ge(s["oT"], u - 1)
                    for ch in range(CHUNKS):
                        ins = nc.tensor.transpose(bank[2 + u % 2][:, ch * P:(ch + 1) * P], on[u % 2][:, ch * P:(ch + 1) * P], ident[:])
                    ins.then_inc(s["ot"], 1)
                    e.wait_ge(s["oT"], u + 1)
                    if u >= 2:
                        e.wait_ge(s["out"], u - 1)
                    for ch in range(CHUNKS):
                        ins = nc.tensor.matmul(bank[6 + u % 2][:, 0:DIM], oT[u % 2][:, ch], wp[:, ch], start=(ch == 0), stop=(ch == 1))
                    ins.then_inc(s["pj"], 1)

        def memory(e, t):
            e.wait_ge(s["kr"], t + 1)
            e.wait_ge(s["vv"], t + 1)
            for ch in range(CHUNKS):
                ins = nc.tensor.matmul(bank[4 + ch][:, 0:129], kr[t % 2][:, ch * P:(ch + 1) * P], vv[t % 2][:, ch, :],
                                       start=(t == 0), stop=(t == TILES - 1))
            ins.then_inc(s["vk"], 1)

        def act(e):
            ln_act(e)
            for t in range(TILES):
                e.wait_ge(s["kv"], t + 1)
                if t >= 2:
                    e.wait_ge(s["vk"], t - 1)
                nc.scalar.activation(kr[t % 2], bank[2 + t % 2][:, 0:DIM], ACT.Relu).then_inc(s["kr"], 1)
            for n in range(CHUNKS * BLOCKS):
                ch, blk = n // BLOCKS, n % BLOCKS
                e.wait_ge(s["qmm"], n + 1)
                nc.scalar.activation(qT[:, ch, blk * BLOCK:(blk + 1) * BLOCK], bank[6 + n % 2][:], ACT.Relu).then_inc(s["qT"], 1)
            for u in range(TILES):
                e.wait_ge(s["ot"], u + 1)
                if u >= 2:
                    e.wait_ge(s["pj"], u - 1)
                nc.scalar.copy(oT[u % 2], bank[2 + u % 2][:, 0:DIM].rearrange("p (c n) -> p c n", c=2)).then_inc(s["oT"], 1)

        def dve(v):
            link = chains["dve"]
            ln_dve(v)
            nc.vector.memset(vv[0][:, :, P:P + 1], 1.0)
            link(nc.vector.memset(vv[1][:, :, P:P + 1], 1.0))
            for t in range(TILES):
                v.wait_ge(s["kv"], t + 1)
                if t >= 2:
                    v.wait_ge(s["vk"], t - 1)
                nc.vector.tensor_copy(vv[t % 2][:, :, 0:P], bank[6 + t % 2][:, 0:DIM].rearrange("p (c n) -> p c n", c=2)
                                      ).then_inc(s["vv"], 1)
            v.wait_ge(s["vk"], TILES)
            v.wait_ge(s["w"], 80)
            hm = hmask.rearrange("p (h o) -> p h o", o=1)
            for ch in range(CHUNKS):
                b = bank[4 + ch]
                nc.vector.tensor_tensor(mem[:, ch, :, 0:LHD], b[:, 0:P].rearrange("p (h n) -> p h n", h=4),
                                        hm.to_broadcast([P, 4, LHD]), ALU.mult)
                nc.vector.tensor_scalar(mem[:, ch, :, LHD], hmask, b[:, P:P + 1], None, ALU.mult).then_inc(s["mem"], 1)
            for t in range(TILES + 2):
                if t < TILES:
                    v.wait_ge(s["o"], t + 1)
                    o = bank[t % 2][:, 0:2 * W33].rearrange("p (h n) -> p h n", h=LHEADS)
                    link(nc.vector.tensor_scalar(den[t % 2], o[:, :, LHD], 1e-15, None, ALU.add))
                    link(nc.vector.reciprocal(den[t % 2], den[t % 2]))
                    if t >= 2:
                        v.wait_ge(s["ot"], t - 1)
                    nc.vector.tensor_tensor(on[t % 2].rearrange("p (h n) -> p h n", h=LHEADS), o[:, :, 0:LHD],
                                            den[t % 2].rearrange("p (h o) -> p h o", o=1).to_broadcast([P, LHEADS, LHD]),
                                            ALU.mult).then_inc(s["on"], 1)
                if t >= 2:
                    u = t - 2
                    if u == 0:
                        v.wait_ge(s["xb"], 1)
                    v.wait_ge(s["pj"], u + 1)
                    nc.vector.tensor_tensor(x[:, u, :], bank[6 + u % 2][:, 0:DIM], x[:, u, :], ALU.add).then_inc(s["out"], 1)

        def pool(e):
            e.wait_ge(ln["xn"], ln_base["xn"] + TILES)
            e.wait_ge(s["w"], 80)
            nc.gpsimd.tensor_tensor(x[:], x[:], bp.rearrange("p (o d) -> p o d", o=1).to_broadcast([P, TILES, DIM]),
                                    ALU.add).then_inc(s["xb"], 1)

        return (s["out"], TILES), dict(sync=sync, tensor=pe, scalar=act, vector=dve, gpsimd=pool)

    def head_mixer(tag, s_ready, n_ready):
        (ln, ln_base), ln_dve, ln_act, ln_pe = layer_norm(tag + "ln", s_ready, n_ready)
        NW = 16 * (32 + 5)
        s, base = shared_sems("mix", dict(
            sw=16 * MIX_EXPERTS, w=NW, lg=1, h=16, o=8, f=TILES, ex=1, g=16, part=1, ein=1, wb=1, bd=4, z=8, out=TILES, xb=1))
        E = MIX_EXPERTS
        c = Carve()
        sw = c(E * 2 * DIM).rearrange("p (e c d) -> p e c d", e=E, c=2)
        w3 = c(CHUNKS * DIM).rearrange("p (k e) -> p k e", k=CHUNKS)
        b3 = c(DIM)
        w1 = c(E * HD).rearrange("p (e f) -> p e f", e=E)
        w2 = c(E * HD).rearrange("p (e f) -> p e f", e=E)
        b1, b2, sbias, iota8 = c(E), c(E), c(E), c(E)
        hmask = c(8)
        ones = c(P)
        junk = c(2 * DIM).rearrange("p (c d) -> p c d", c=2)
        part, logit, m8, e8, esum = c(E), c(E), c(E), c(E), c(1)
        mi = c(E, U32)
        mif = c(E)
        oh = c(4 * E).rearrange("p (k e) -> p k e", k=4)
        tmp = c(E * HD)
        sel = c(4 * HD).rearrange("p (k f) -> p k f", k=4)
        bsel = c(4)
        tmpb = c(4 * E).rearrange("p (k e) -> p k e", k=4)
        b2s = c(1)
        bd = [[c(P) for _ in range(2)] for _ in range(2)]
        ht = [c(BLOCK) for _ in range(4)]
        z = [c(CHUNKS * BLOCK).rearrange("p (c n) -> p c n", c=2) for _ in range(2)]

        def sync(e):
            e.wait_ge(s_ready, n_ready)
            for ex in range(E):
                e.dma_start(sw[:, ex], a["L1_ffn_switch_w"][ex:ex + 1].rearrange("e (c p d) -> p (e c) d", p=P, c=2)).then_inc(s["sw"], 16)
            for h in range(8):
                hp = slice(HD * h, HD * (h + 1))
                e.dma_start(w1[hp], a["w1_T"].rearrange("e d f -> d e f")).then_inc(s["w"], 16)
                e.dma_start(w2[hp], a["w2_T"].rearrange("e d f -> d e f")).then_inc(s["w"], 16)
                e.dma_start(b1[hp], a["b1_T"]).then_inc(s["w"], 16)
                e.dma_start(b2[hp], a["b2_T"]).then_inc(s["w"], 16)
            row = lambda v: v.rearrange("(o d) -> o d", o=1)
            e.dma_start(sbias, row(a["L1_ffn_switch_b"]).to_broadcast([P, E])).then_inc(s["w"], 16)
            e.dma_start(b3, row(a["L1_ffn_b3"]).to_broadcast([P, DIM])).then_inc(s["w"], 16)
            e.dma_start(iota8, a["iota8"]).then_inc(s["w"], 16)
            e.dma_start(hmask, a["mask16"]).then_inc(s["w"], 16)
            e.dma_start(w3, a["w3_T"].rearrange("(k p) e -> p k e", p=P)).then_inc(s["w"], 16)

        def pe(e):
            ln_pe(e)
            e.wait_ge(s["part"], base["part"] + 1)
            nc.tensor.matmul(bank[2][:, 0:E], ones, part, start=True, stop=True).then_inc(s["lg"], 1)
            e.wait_ge(s["bd"], base["bd"] + 4)
            e.wait_ge(ln["xnT"], ln_base["xnT"] + TILES // 2)
            U = 2 * BLOCKS

            def second(u):
                if u >= 2:
                    e.wait_ge(s["z"], base["z"] + u - 1)
                for k in range(2):
                    e.wait_ge(s["g"], base["g"] + 2 * u + k + 1)
                    ins = nc.tensor.matmul(bank[4 + u % 2][:], bd[1][k], ht[(2 * u + k) % 4], start=(k == 0), stop=(k == 1))
                ins.then_inc(s["o"], 1)

            def final(blk):
                e.wait_ge(s["z"], base["z"] + 2 * blk + 2)
                for q in range(4):
                    t = 4 * blk + q
                    if t >= 2:
                        e.wait_ge(s["out"], base["out"] + t - 1)
                    for k in range(CHUNKS):
                        ins = nc.tensor.matmul(bank[6 + t % 2][:, 0:DIM], z[blk % 2][:, k, q * P:(q + 1) * P], w3[:, k, :],
                                               start=(k == 0), stop=(k == 1))
                    ins.then_inc(s["f"], 1)

            for u in range(U):
                blk, ch = u // 2, u % 2
                for k in range(2):
                    n = 2 * u + k
                    if n >= 4:
                        e.wait_ge(s["g"], base["g"] + n - 3)
                    nc.tensor.matmul(bank[n % 4][:], bd[0][k], xnT[:, ch, blk * BLOCK:(blk + 1) * BLOCK],
                                     start=True, stop=True).then_inc(s["h"], 1)
                if u >= 1:
                    second(u - 1)
                if u >= 3 and u % 2:
                    final(u // 2 - 1)
            second(U - 1)
            final(BLOCKS - 1)

        def act(e):
            ln_act(e)
            e.wait_ge(s["ein"], base["ein"] + 1)
            nc.scalar.activation(e8, e8, ACT.Exp).then_inc(s["ex"], 1)
            e.wait_ge(s["wb"], base["wb"] + 1)
            for n in range(4 * BLOCKS):
                e.wait_ge(s["h"], base["h"] + n + 1)
                if n >= 4:
                    e.wait_ge(s["o"], base["o"] + n // 2 - 1)
                nc.scalar.activation(ht[n % 4], bank[n % 4][:], ACT.Gelu, bias=bsel[:, n % 2:n % 2 + 1]).then_inc(s["g"], 1)

        def dve(v):
            link = chains["dve"]
            ln_dve(v)
            v.wait_ge(ln["xn"], ln_base["xn"] + TILES)
            link(nc.vector.memset(ones, 1.0))
            v.wait_ge(s["sw"], base["sw"] + 16 * E)
            for ex in range(E):
                ins = nc.vector.tensor_tensor_reduce(out=junk, in0=xn[:, 0:2, :], in1=sw[:, ex], scale=1.0, scalar=0.0,
                                                     op0=ALU.mult, op1=ALU.add, accum_out=part[:, ex:ex + 1])
                if ex < E - 1:
                    link(ins)
            ins.then_inc(s["part"], 1)
            v.wait_ge(s["w"], base["w"] + NW)
            v.wait_ge(s["lg"], base["lg"] + 1)
            link(nc.vector.tensor_tensor(logit, bank[2][:, 0:E], sbias, ALU.add))
            link(nc.vector.max(m8, logit))
            nc.vector.max_index(mi, m8, logit)
            nc.vector.tensor_scalar(e8, m8, m8[:, 0:1], None, ALU.subtract).then_inc(s["ein"], 1)
            v.wait_ge(s["ein"], base["ein"] + 1)
            link(nc.vector.tensor_copy(mif, mi))
            for k in range(2):
                ins = nc.vector.tensor_scalar(oh[:, k, :], iota8, mif[:, k:k + 1], None, ALU.is_equal)
            link(ins)
            v.wait_ge(s["ex"], base["ex"] + 1)
            link(nc.vector.tensor_reduce(esum, e8, AX_X, ALU.add))
            link(nc.vector.reciprocal(esum, esum))
            link(nc.vector.tensor_scalar(e8, e8, esum, None, ALU.mult))
            for k in range(2):
                ins = nc.vector.tensor_scalar(oh[:, 2 + k, :], oh[:, k, :], e8[:, k:k + 1], None, ALU.mult)
            link(ins)
            for k in range(4):
                w, b = (w1, b1) if k < 2 else (w2, b2)
                t3 = tmp.rearrange("p (e f) -> p e f", e=E)
                link(nc.vector.tensor_tensor(t3, w, oh[:, k, :].rearrange("p (e o) -> p e o", o=1).to_broadcast([P, E, HD]), ALU.mult))
                link(nc.vector.tensor_reduce(sel[:, k, :], tmp.rearrange("p (e f) -> p f e", e=E), AX_X, ALU.add))
                link(nc.vector.tensor_tensor(tmpb[:, k, :], b, oh[:, k, :], ALU.mult))
                link(nc.vector.tensor_reduce(bsel[:, k:k + 1], tmpb[:, k, :], AX_X, ALU.add))
            nc.vector.tensor_tensor(b2s, bsel[:, 2:3], bsel[:, 3:4], ALU.add).then_inc(s["wb"], 1)
            v.wait_ge(s["wb"], base["wb"] + 1)
            for k in range(4):
                nc.vector.tensor_tensor(bd[k // 2][k % 2].rearrange("p (h f) -> p h f", h=8),
                                        sel[:, k, :].rearrange("p (o f) -> p o f", o=1).to_broadcast([P, 8, HD]),
                                        hmask.rearrange("p (h o) -> p h o", o=1).to_broadcast([P, 8, HD]),
                                        ALU.mult).then_inc(s["bd"], 1)
            v.wait_ge(s["xb"], base["xb"] + 1)
            v.wait_ge(ln["xnT"], ln_base["xnT"] + TILES // 2)

            def outs(blk):
                for q in range(4):
                    t = 4 * blk + q
                    v.wait_ge(s["f"], base["f"] + t + 1)
                    nc.vector.scalar_tensor_tensor(out=x[:, t, :], in0=bank[6 + t % 2][:, 0:DIM], scalar=0.5, in1=x[:, t, :],
                                                   op0=ALU.mult, op1=ALU.add).then_inc(s["out"], 1)
            for u in range(2 * BLOCKS):
                blk, ch = u // 2, u % 2
                v.wait_ge(s["o"], base["o"] + u + 1)
                if blk >= 2 and ch == 0:
                    v.wait_ge(s["f"], base["f"] + 4 * (blk - 1))
                nc.vector.scalar_tensor_tensor(out=z[blk % 2][:, ch, :], in0=bank[4 + u % 2][:], scalar=b2s,
                                               in1=xnT[:, ch, blk * BLOCK:(blk + 1) * BLOCK], op0=ALU.add, op1=ALU.add
                                               ).then_inc(s["z"], 1)
                if u >= 2 and u % 2 == 0:
                    outs(u // 2 - 1)
            outs(BLOCKS - 1)

        def pool(e):
            link = chains["pool"]
            e.wait_ge(ln["xn"], ln_base["xn"] + TILES)
            e.wait_ge(s["w"], base["w"] + NW)
            link(nc.gpsimd.tensor_scalar(b3, b3, 0.5, None, ALU.mult))
            nc.gpsimd.tensor_tensor(x[:], x[:], b3.rearrange("p (o d) -> p o d", o=1).to_broadcast([P, TILES, DIM]),
                                    ALU.add).then_inc(s["xb"], 1)

        return (s["out"], base["out"] + TILES), dict(sync=sync, tensor=pe, scalar=act, vector=dve, gpsimd=pool)
    q_dram = dram("q_parts", [3, DIM, TOKENS], BF16)
    k_dram = dram("k_parts", [3, DIM, TOKENS], BF16)
    v_dram = dram("v_ones", [P, HGROUPS * TILES, HPG * 2 * HD])

    def softmax_attention(tag, s_ready, n_ready):
        (ln, ln_base), ln_dve, ln_act, ln_pe = layer_norm(tag + "ln", s_ready, n_ready)
        s = sems(tag, "w wg qk v va rm ra kf kfT kft mem memo comb gex split part2 part3 exk kmax qkd "
                 "vd onesr st exp pv raw mx mxd nm nmt nms mrow rt rc cadd ot oT pj out")
        s_ld = [sem(f"{tag}_step{b}") for b in range(3)]
        VW = 2 * HD
        MW = HD + 1
        c = Carve()
        wqk = c(2 * CHUNKS * DIM).rearrange("p (w k e) -> p w k e", w=2, k=CHUNKS)
        wv = c(CHUNKS * DIM).rearrange("p (k e) -> p k e", k=CHUNKS)
        cs = c(2 * TOKENS).rearrange("p (w n) -> p w n", w=2)
        va = c(TILES * HEADS * VW).rearrange("p (t h n) -> p t h n", t=TILES, h=HEADS)
        qk = [c(CHUNKS * TOKENS).rearrange("p (c n) -> p c n", c=CHUNKS) for _ in range(2)]
        rope = [c(4 * BLOCK).rearrange("p (u n) -> p u n", u=4) for _ in range(2)]
        parts = [c(CHUNKS * TOKENS // 2, BF16).rearrange("p (c n) -> p c n", c=CHUNKS) for _ in range(3)]
        end = c.at
        res = cs
        kfT = c(TILES * DIM).rearrange("p (t d) -> p t d", t=TILES)
        feat = rope[0]
        memb = c(CHUNKS * 8 * MW).rearrange("p (c h n) -> p c h n", c=CHUNKS, h=8)
        c = Carve()
        KS = [c(HPG * TOKENS // 2, BF16).rearrange("p (h n) -> p h n", h=HPG) for _ in range(3)]
        QS = [c(HPG * BLOCK // 2, BF16).rearrange("p (h n) -> p h n", h=HPG) for _ in range(3)]
        VS = [c(TILES * HPG * VW).rearrange("p (t n) -> p t n", t=TILES) for _ in range(3)]
        PT = [c(HPG * BLOCK).rearrange("p (h n) -> p h n", h=HPG) for _ in range(2)]
        raw = xnT[:].rearrange("p c n -> p (c n)")
        raw = c(STEPS * BLOCK).rearrange("p (s n) -> p s n", s=STEPS)
        mx = c(16 * 4).rearrange("p (i k) -> p i k", i=16)
        m16, mr, mr2 = c(16), c(16), c(16)
        nmx = c(P // 2, BF16)
        nm3 = nmx[:, 0:48].rearrange("p (r i) -> p r i", r=3)
        nmT = c(P // 2, BF16, parts=48)
        assert c.at <= AREA - 2000
        c.at = AREA - 2000
        hmask, gate, gexp, gp, omg = c(8), c(HEADS), c(HEADS), c(HEADS), c(HEADS)
        den = [c(HEADS) for _ in range(2)]
        wo = c(CHUNKS * DIM).rearrange("p (k e) -> p k e", k=CHUNKS)
        oT = [c(DIM).rearrange("p (c n) -> p c n", c=2) for _ in range(2)]
        tmp = [c(DIM).rearrange("p (t n) -> p t n", t=16) for _ in range(1)]
        comb = xn

        def sync(e):
            e.wait_ge(s_ready, n_ready)
            for w, name in enumerate(("Wq_T", "Wk_T")):
                e.dma_start(wqk[:, w], a[name].rearrange("(k p) e -> p k e", p=P)).then_inc(s["w"], 16)
            e.dma_start(wv, a["Wv_T"].rearrange("(k p) e -> p k e", p=P)).then_inc(s["w"], 16)
            e.dma_start(cs, a["rope"].rearrange("w p n -> p w n")).then_inc(s["w"], 16)
            e.dma_start(gate, a["L1_attn_gate"].rearrange("a h b c -> a (h b c)").to_broadcast([P, HEADS])).then_inc(s["wg"], 16)
            e.dma_start(hmask, a["mask16"]).then_inc(s["wg"], 16)
            e.dma_start(wo, a["Wo_T"].rearrange("(k p) e -> p k e", p=P)).then_inc(s["wg"], 16)
            e.wait_ge(s["va"], TILES)
            e.wait_ge(s["onesr"], 1)
            for g in range(HGROUPS):
                e.dma_start(v_dram[:, TILES * g:TILES * (g + 1), :],
                            va[:, :, HPG * g:HPG * (g + 1), :].rearrange("p t h n -> p t (h n)")).then_inc(s["vd"], 16)
            for w, d in enumerate((q_dram, k_dram)):
                for r, need in ((0, "split"), (1, "part2"), (2, "part3")):
                    e.wait_ge(s[need], w + 1)
                    e.dma_start(d[r].rearrange("(c p) n -> p c n", p=P), parts[r]).then_inc(s["qkd"], 16)
                e.wait_ge(s["qkd"], 48 * (w + 1))
            e.wait_ge(s["vd"], 16 * HGROUPS)

            def load(b, st):
                g, q = st // BLOCKS, st % BLOCKS
                rows, col, tile = g * HPG * HD, q * BLOCK, g * TILES
                for d, dst, ps, cols in ((q_dram, QS[b], Q_PARTS, bass.ds(col, BLOCK)),
                                         (k_dram, KS[b], K_PARTS, slice(0, TOKENS))):
                    for i, part in enumerate(ps):
                        src = d[part, bass.ds(rows, HPG * HD), cols].rearrange("(h r) n -> r h n", r=HD)
                        e.dma_start(dst[HD * i:HD * (i + 1)], src).then_inc(s_ld[b], 16)
                e.dma_start(VS[b], v_dram[:, bass.ds(tile, TILES), :]).then_inc(s_ld[b], 16)

            def store_max(b, st):
                e.wait_ge(s["nms"], st + 1)
                e.dma_start(QS[b][STACK:STACK_M].rearrange("r h n -> r (h n)").rearrange("r (i n) -> r i n", n=P),
                            nmT).then_inc(s["mrow"], 16)

            e.wait_ge(s["memo"], TILES)
            e.wait_ge(s["comb"], TILES)
            for b in range(3):
                load(b, b)
            store_max(0, 0)
            for st in range(STEPS - 1):
                store_max((st + 1) % 3, st + 1)
                if st + 3 < STEPS:
                    e.wait_ge(s["pv"], (st + 1) * 16)
                    load(st % 3, st + 3)

        def pe(e):
            ln_pe(e)
            e.wait_ge(s["w"], 64)
            e.wait_ge(ln["xnT"], ln_base["xnT"] + TILES // 2)
            for t in range(TILES):
                if t >= 2:
                    e.wait_ge(s["va"], t - 1)
                for k in range(CHUNKS):
                    ins = nc.tensor.matmul(bank[6 + t % 2][:, 0:DIM], xnT[:, k, t * P:(t + 1) * P], wv[:, k], start=(k == 0), stop=(k == 1))
                ins.then_inc(s["v"], 1)
                if t % 2 == 0:
                    n = t // 2
                    w, blk = n // BLOCKS, n % BLOCKS
                    if n >= 2:
                        e.wait_ge(s["rm"], n - 1)
                    for ch in range(CHUNKS):
                        for k in range(CHUNKS):
                            ins = nc.tensor.matmul(bank[2 + 2 * (n % 2) + ch][:], wqk[:, w, k, ch * P:(ch + 1) * P],
                                                   xnT[:, k, blk * BLOCK:(blk + 1) * BLOCK], start=(k == 0), stop=(k == 1))
                    ins.then_inc(s["qk"], 1)
            e.wait_ge(s["kf"], 2)
            for t in range(TILES):
                if t >= 2:
                    e.wait_ge(s["kfT"], t - 1)
                for ch in range(CHUNKS):
                    ins = nc.tensor.transpose(bank[t % 2][:, ch * P:(ch + 1) * P], qk[1][:, ch, t * P:(t + 1) * P], ident[:])
                ins.then_inc(s["kft"], 1)
            e.wait_ge(s["rm"], 2 * BLOCKS)
            for t in range(TILES):
                e.wait_ge(s["kfT"], t + 1)
                for ch in range(CHUNKS):
                    ins = nc.tensor.matmul(bank[4 + ch][:, 0:8 * MW], kfT[:, t, ch * P:(ch + 1) * P], va[:, t, 8 * ch:8 * ch + 8, 0:MW],
                                           start=(t == 0), stop=(t == TILES - 1))
            ins.then_inc(s["mem"], 1)
            e.wait_ge(s["kf"], 4)
            e.wait_ge(s["mem"], 2)
            for t in range(TILES):
                if t >= 2:
                    e.wait_ge(s["comb"], t - 1)
                else:
                    e.wait_ge(s["va"], TILES)
                for ch in range(CHUNKS):
                    ins = nc.tensor.matmul(bank[6 + t % 2][:, ch * 8 * MW:(ch + 1) * 8 * MW], qk[0][:, ch, t * P:(t + 1) * P],
                                           memb[:, ch], start=True, stop=True)
                ins.then_inc(s["memo"], 1)
            e.wait_ge(s["comb"], TILES)

            def max_scores(b, m, j):
                h, qt, kc = j // 16, j // 4 % 4, j % 4
                if isinstance(m, int) and m == 0:
                    if j >= 2:
                        e.wait_ge(s["mxd"], j - 1)
                else:
                    e.wait_ge(s["mxd"], m * 64 + (j - 1))
                nc.tensor.matmul(bank[5 + j % 2][:], QS[b][0:STACK, h, qt * P:(qt + 1) * P],
                                 KS[b][0:STACK, h, kc * BLOCK:(kc + 1) * BLOCK], start=True, stop=True).then_inc(s["mx"], 1)

            def max_rows(b, m):
                e.wait_ge(s["nm"], m + 1)
                nc.tensor.transpose(bank[7][:].bitcast(BF16)[:, 0:P], nmx, ident_bf[:]).then_inc(s["nmt"], 1)

            def step(b, st, ahead):
                nb = (b + 1) % 3
                e.wait_ge(s["mrow"], (st + 1) * 16)
                j = 0
                for kt in range(TILES + 1):
                    for pair in range(2):
                        if kt < TILES:
                            e.wait_ge(s["exp"], st * 32 + (2 * kt + pair + 1))
                            for h in (2 * pair, 2 * pair + 1):
                                ins = nc.tensor.matmul(bank[h][:], KS[b][0:STACK_M, h, kt * P:(kt + 1) * P],
                                                       QS[b][0:STACK_M, h, :], start=True, stop=True)
                            ins.then_inc(s["st"], 1)
                        for _ in range(3 if pair == 0 else 2):
                            if ahead and j < 64:
                                if j == 0:
                                    e.wait_ge(s_ld[nb], ((st + 1 + 2 - nb) // 3 if isinstance(st, int) else turn_of(st, b)) * 208)
                                max_scores(nb, st + 1, j)
                                j += 1
                    if ahead and kt == 14:
                        max_rows(nb, st + 1)
                    if kt >= 1:
                        if kt == 1:
                            e.wait_ge(s["raw"], st + 1)
                        e.wait_ge(s["exp"], st * 32 + (2 * kt + 2))
                        for h in range(HPG):
                            ins = nc.tensor.matmul(bank[4][VW * h:VW * (h + 1), :], VS[b][:, kt - 1, VW * h:VW * (h + 1)],
                                                   PT[(kt - 1) % 2][:, h, :], start=(kt == 1), stop=(kt == TILES))
                        ins.then_inc(s["pv"], 1)

            turn = [None]

            def turn_of(st, b):
                return turn[0] + (1 if b < 2 else 2)

            e.wait_ge(s_ld[0], 208)
            e.wait_ge(s["onesr"], 2)
            for j in range(64):
                max_scores(0, 0, j)
            max_rows(0, 0)
            with e.Fori(0, 5) as i:
                turn[0] = i
                for b in range(3):
                    step(b, i * 3 + b, True)
            step(0, 15, False)

            for st in range(STEPS):
                if st == 0:
                    e.wait_ge(s["exp"], 2 + 32 * STEPS)
                if st >= 2:
                    e.wait_ge(s["rc"], st - 1)
                e.wait_ge(s["raw"], st + 2)
                for q in range(4):
                    ins = nc.tensor.transpose(bank[st % 2][:, q * P:(q + 1) * P], raw[:, st, q * P:(q + 1) * P], ident[:])
                ins.then_inc(s["rt"], 1)
            e.wait_ge(s["cadd"], STEPS)
            e.wait_ge(s["wg"], 48)
            for t in range(TILES):
                if t >= 2:
                    e.wait_ge(s["oT"], t - 1)
                for ch in range(CHUNKS):
                    ins = nc.tensor.transpose(bank[2 + t % 2][:, ch * P:(ch + 1) * P], comb[:, t, ch * P:(ch + 1) * P], ident[:])
                ins.then_inc(s["ot"], 1)
                e.wait_ge(s["oT"], t + 1)
                if t >= 2:
                    e.wait_ge(s["out"], t - 1)
                for ch in range(CHUNKS):
                    ins = nc.tensor.matmul(bank[6 + t % 2][:, 0:DIM], oT[t % 2][:, ch], wo[:, ch], start=(ch == 0), stop=(ch == 1))
                ins.then_inc(s["pj"], 1)

        def act(e):
            ln_act(e)
            for t in range(TILES):
                e.wait_ge(s["v"], t + 1)
                nc.scalar.copy(va[:, t, :, 0:HD], bank[6 + t % 2][:, 0:DIM].rearrange("p (h n) -> p h n", h=HEADS)).then_inc(s["va"], 1)
            for w in range(2):
                e.wait_ge(s["ra"], BLOCKS * (w + 1))
                if w:
                    e.wait_ge(s["qkd"], 48)
                nc.scalar.activation(parts[0], qk[w], ACT.Copy, scale=(0.25 if w == 0 else 1.0)).then_inc(s["split"], 1)
                e.wait_ge(s["exk"], w + 1)
                nc.scalar.copy(parts[1], res).then_inc(s["part2"], 1)
            for n, w in enumerate((1, 0)):
                for ch in range(CHUNKS):
                    i = 2 * n + ch
                    if i >= 1:
                        e.wait_ge(s["kf"], i)
                    else:
                        e.wait_ge(s["part3"], 2)
                    nc.scalar.activation(feat, qk[w][:, ch, :].rearrange("p (u n) -> p u n", u=4), ACT.Exp).then_inc(s["kmax"], 1)
                if n == 0:
                    for t in range(TILES):
                        e.wait_ge(s["kft"], t + 1)
                        nc.scalar.copy(kfT[:, t, :], bank[t % 2][:, 0:DIM]).then_inc(s["kfT"], 1)
            e.wait_ge(s["wg"], 48)
            nc.scalar.activation(gexp, gate, ACT.Exp, scale=-1.0).then_inc(s["gex"], 1)
            e.wait_ge(s["gex"], 1)
            nc.scalar.copy(tmp[0][:, 0, 0:1], gexp[:, 0:1]).then_inc(s["exp"], 2)
            nc.scalar.copy(tmp[0][:, 1, 0:1], gexp[:, 0:1]).then_inc(s["raw"], 1)

            def step(st):
                for kt in range(TILES):
                    for pair in range(2):
                        e.wait_ge(s["st"], st * 32 + (2 * kt + pair + 1))
                        nc.scalar.activation(PT[kt % 2][:, 2 * pair:2 * pair + 2, :],
                                             psum[:, 2 * pair * 512:(2 * pair + 2) * 512].rearrange("p (h n) -> p h n", h=2),
                                             ACT.Exp).then_inc(s["exp"], 1)
                e.wait_ge(s["pv"], st * 16 + 16)
                nc.scalar.copy(raw[:, st, :] if isinstance(st, int) else raw[:, bass.ds(st, 1), :].rearrange("p s n -> p (s n)"),
                               bank[4][:]).then_inc(s["raw"], 1)

            with e.Fori(0, STEPS) as st:
                step(st)
            for t in range(TILES):
                e.wait_ge(s["ot"], t + 1)
                if t >= 2:
                    e.wait_ge(s["pj"], t - 1)
                nc.scalar.copy(oT[t % 2], bank[2 + t % 2][:, 0:DIM].rearrange("p (c n) -> p c n", c=2)).then_inc(s["oT"], 1)

        def dve(v):
            link = chains["dve"]
            ln_dve(v)
            v.wait_ge(s["w"], 64)
            for n in range(2 * BLOCKS):
                blk = n % BLOCKS
                v.wait_ge(s["qk"], n + 1)
                if n >= 2:
                    v.wait_ge(s["ra"], n - 1)
                cols = slice(blk * BLOCK, (blk + 1) * BLOCK)
                for u, (ch, w) in enumerate(((0, 0), (1, 1), (1, 0), (0, 1))):
                    ins = nc.vector.tensor_tensor(rope[n % 2][:, u, :], bank[2 + 2 * (n % 2) + ch][:], cs[:, w, cols], ALU.mult)
                ins.then_inc(s["rm"], 1)
            v.wait_ge(s["ra"], 2 * BLOCKS)
            for w in range(2):
                v.wait_ge(s["split"], w + 1)
                nc.vector.scalar_tensor_tensor(out=res, in0=qk[w], scalar=(0.25 if w == 0 else 1.0), in1=parts[0],
                                               op0=ALU.mult, op1=ALU.subtract).then_inc(s["exk"], 1)
                v.wait_ge(s["part2"], w + 1)
                nc.vector.tensor_tensor(parts[2], res, parts[1], ALU.subtract).then_inc(s["part3"], 1)
            v.wait_ge(s["part3"], 2)
            for i in range(4):
                w, ch = 1 - i // 2, i % 2
                if i == 2:
                    memory_mask(v)
                v.wait_ge(s["kmax"], i + 1)
                f = qk[w][:, ch, :]
                link(nc.vector.tensor_scalar(f, f, 0.0, None, ALU.max))
                nc.vector.scalar_tensor_tensor(out=f, in0=feat.rearrange("p u n -> p (u n)"), scalar=1.0, in1=f,
                                               op0=ALU.min, op1=ALU.add).then_inc(s["kf"], 1)
            v.wait_ge(s["gex"], 1)
            link(nc.vector.tensor_scalar(gp, gexp, 1.0, None, ALU.add))
            link(nc.vector.reciprocal(gp, gp))
            link(nc.vector.tensor_scalar(omg, gp, -1.0, 1.0, ALU.mult, ALU.add))
            for t in range(TILES):
                v.wait_ge(s["memo"], t + 1)
                o = bank[6 + t % 2][:, 0:HEADS * MW].rearrange("p (h n) -> p h n", h=HEADS)
                link(nc.vector.reciprocal(den[t % 2], o[:, :, HD]))
                link(nc.vector.tensor_tensor(den[t % 2], den[t % 2], gp, ALU.mult))
                nc.vector.tensor_tensor(comb[:, t, :].rearrange("p (h n) -> p h n", h=HEADS), o[:, :, 0:HD],
                                        den[t % 2].rearrange("p (h o) -> p h o", o=1).to_broadcast([P, HEADS, HD]),
                                        ALU.mult).then_inc(s["comb"], 1)
            v.wait_ge(s["comb"], TILES)
            v.wait_ge(s["qkd"], 96)
            v.wait_ge(s["vd"], 16 * HGROUPS)
            nc.vector.memset(nmx, 0.0)
            for b in range(3):
                ins = nc.vector.memset(KS[b][STACK:STACK_M], 1.0)
            ins.then_inc(s["onesr"], 1)

            def maxima(m):
                for j in range(64):
                    v.wait_ge(s["mx"], m * 64 + (j + 1))
                    nc.vector.tensor_reduce(mx[:, j // 4, j % 4:j % 4 + 1], bank[5 + j % 2][:], AX_X, ALU.max).then_inc(s["mxd"], 1)
                v.wait_ge(s["mxd"], m * 64 + 64)
                link(nc.vector.tensor_reduce(m16, mx, AX_X, ALU.max))
                link(nc.vector.tensor_scalar(nm3[:, 0, :], m16, -1.0, None, ALU.mult))
                link(nc.vector.scalar_tensor_tensor(out=mr, in0=m16, scalar=-1.0, in1=nm3[:, 0, :], op0=ALU.mult, op1=ALU.subtract))
                link(nc.vector.tensor_copy(nm3[:, 1, :], mr))
                link(nc.vector.tensor_tensor(mr2, mr, nm3[:, 1, :], ALU.subtract))
                nc.vector.tensor_copy(nm3[:, 2, :], mr2).then_inc(s["nm"], 1)
                v.wait_ge(s["nmt"], m + 1)
                if isinstance(m, int):
                    if m:
                        v.wait_ge(s["mrow"], 16 * m)
                else:
                    v.wait_ge(s["mrow"], m * 16)
                nc.vector.tensor_copy(nmT, bank[7][:].bitcast(BF16)[0:48, 0:P]).then_inc(s["nms"], 1)

            maxima(0)
            with v.Fori(1, STEPS) as m:
                link.enter(m - 1, 5)
                maxima(m)
                link.leave(STEPS - 1)
            for st in range(STEPS):
                g, qb = st // BLOCKS, st % BLOCKS
                v.wait_ge(s["rt"], st + 1)
                o = bank[st % 2][:].rearrange("p (q h n) -> p q h n", q=4, h=HPG)
                d = den[st % 2].rearrange("p (q h) -> p q h", q=4)
                if st >= 1:
                    v.wait_ge(s["cadd"], st)
                link(nc.vector.reciprocal(d, o[:, :, :, HD]))
                link(nc.vector.tensor_tensor(d, d, omg[:, HPG * g:HPG * (g + 1)].rearrange("p (o h) -> p o h", o=1).to_broadcast([P, 4, HPG]), ALU.mult))
                t4 = tmp[0].rearrange("p (q h) n -> p q h n", q=4)
                for q in range(4):
                    ins = nc.vector.tensor_tensor(t4[:, q], o[:, q, :, 0:HD],
                                                  d[:, q, :].rearrange("p (h o) -> p h o", o=1).to_broadcast([P, HPG, HD]), ALU.mult)
                ins.then_inc(s["rc"], 1)
                v.wait_ge(s["rc"], st + 1)
                cv = comb[:, 4 * qb:4 * qb + 4, HPG * HD * g:HPG * HD * (g + 1)]
                nc.vector.tensor_tensor(cv, cv, tmp[0].rearrange("p (q h) n -> p q (h n)", q=4), ALU.add).then_inc(s["cadd"], 1)
            for t in range(TILES):
                v.wait_ge(s["pj"], t + 1)
                nc.vector.tensor_tensor(x[:, t, :], bank[6 + t % 2][:, 0:DIM], x[:, t, :], ALU.add).then_inc(s["out"], 1)

        def memory_mask(v):
            v.wait_ge(s["mem"], 1)
            v.wait_ge(s["wg"], 48)
            for ch in range(CHUNKS):
                ins = nc.vector.tensor_tensor(memb[:, ch], bank[4 + ch][:, 0:8 * MW].rearrange("p (h n) -> p h n", h=8),
                                              hmask.rearrange("p (h o) -> p h o", o=1).to_broadcast([P, 8, MW]), ALU.mult)
            ins.then_inc(s["mem"], 1)

        def pool(e):
            e.wait_ge(s["w"], 64)
            e.wait_ge(s_ready, n_ready)
            nc.gpsimd.memset(va[:, :, :, HD:VW], 1.0).then_inc(s["onesr"], 1)
            for n in range(2 * BLOCKS):
                w, blk = n // BLOCKS, n % BLOCKS
                cols = slice(blk * BLOCK, (blk + 1) * BLOCK)
                e.wait_ge(s["rm"], n + 1)
                r = rope[n % 2]
                nc.gpsimd.tensor_tensor(qk[w][:, 0, cols], r[:, 0, :], r[:, 1, :], ALU.subtract)
                nc.gpsimd.tensor_tensor(qk[w][:, 1, cols], r[:, 2, :], r[:, 3, :], ALU.add).then_inc(s["ra"], 1)

        return (s["out"], TILES), dict(sync=sync, tensor=pe, scalar=act, vector=dve, gpsimd=pool)

    layers = []
    ready = (s_x, 16)
    makers = [moe, linear_attention, moe, head_mixer, softmax_attention, head_mixer]
    from_ = [m for m in makers]
    for n, mk in enumerate(from_[:stages]):
        ready, progs = mk(f"l{n}", *ready)
        layers.append(progs)

    block = ctx.enter_context(nc.Block())
    s_out = sem("stored")

    @block.sync
    def _(e):
        e.dma_start(x[:], a["L0_attn_x"][0].rearrange("(t p) d -> p t d", p=P)).then_inc(s_x, 16)
        e.dma_start(ident[:], a["ident"]).then_inc(s_const, 16)
        for pr in layers:
            if "sync" in pr:
                pr["sync"](e)
        e.wait_ge(*ready)
        e.dma_start(out[0].rearrange("(t p) d -> p t d", p=P), x[:]).then_inc(s_out, 16)
        e.wait_ge(s_out, 16)

    @block.tensor
    def _(e):
        e.wait_ge(s_const, 16)
        e.wait_ge(s_const2, 1)
        for pr in layers:
            pr["tensor"](e)

    @block.scalar
    def _(e):
        chains["act"] = Chain(e, chain_sems["act"])
        for pr in layers:
            pr["scalar"](e)

    @block.vector
    def _(e):
        chains["dve"] = Chain(e, chain_sems["dve"])
        e.wait_ge(s_const, 16)
        nc.vector.tensor_copy(ident_bf[:], ident[:]).then_inc(s_const2, 1)
        for pr in layers:
            pr["vector"](e)

    @block.gpsimd
    def _(e):
        chains["pool"] = Chain(e, chain_sems["pool"])
        for pr in layers:
            if "gpsimd" in pr:
                pr["gpsimd"](e)


def constants():
    f = np.float32
    c = {}
    c["ident"] = np.eye(P, dtype=f)
    c["iota_row"] = np.tile(TOKENS - np.arange(TOKENS // 2, dtype=f), (P, 1))
    c["key_off"] = np.where(np.arange(P) < EXPERTS, 0, -TOKENS // 2).astype(f).reshape(P, 1)
    c["iota_bf"] = np.tile(np.arange(P, dtype=f), (P, 1)).astype(mybir.dt.np(BF16))
    c["tile_off"] = np.tile(P * np.arange(TILES, dtype=f), (P, 1))
    c["mask32"] = (np.arange(P)[:, None] // LHD == np.arange(P // LHD)[None, :]).astype(f)
    c["mask16"] = (np.arange(P)[:, None] // HD == np.arange(P // HD)[None, :]).astype(f)
    c["iota8"] = np.tile(np.arange(MIX_EXPERTS, dtype=f), (P, 1))
    inv = (1.0 / np.float32(10000.0) ** (np.arange(0, DIM, 2, dtype=f) / f(DIM))).astype(f)
    angle = (np.arange(TOKENS, dtype=f)[None, :] * inv[:, None]).astype(f).astype(np.float64)
    c["rope"] = np.stack([np.cos(angle), np.sin(angle)]).astype(f)
    c["slot_mask"] = (np.arange(P)[:, None] // CAP == np.arange(EPG)[None, :]).astype(f)
    return c


def host_arrays(inputs):
    t = lambda w: np.ascontiguousarray(np.swapaxes(w, -1, -2))
    d = {k: np.asarray(v) for k, v in inputs.items()}
    d["gate_T"] = t(d.pop("L0_ffn_gate_w"))
    qkv = d.pop("L0_attn_w_qkv")
    d["wq_T"], d["wkv_T"] = t(qkv[:DIM]), t(qkv[DIM:])
    d["wproj_T"] = t(d.pop("L0_attn_w_proj"))
    for w in ("Wq", "Wk", "Wv", "Wo"):
        d[w + "_T"] = t(d.pop("L1_attn_" + w))
    d["w3_T"] = t(d.pop("L1_ffn_w3"))
    d["w1_T"], d["w2_T"] = t(d.pop("L1_ffn_w1")), t(d.pop("L1_ffn_w2"))
    d["b1_T"], d["b2_T"] = t(d.pop("L1_ffn_b1")), t(d.pop("L1_ffn_b2"))
    d.update(constants())
    return d


def kernel(stages=6, **inputs):
    import concourse.bacc as _bacc
    from concourse.bass_utils import run_bass_kernel_spmd as _run

    nc = _bacc.Bacc("TRN2", target_bir_lowering=False, num_devices=1)
    arrays, a = {}, {}
    for name, v in host_arrays(inputs).items():
        arrays[f"in_{name}"] = v
        a[name] = nc.dram_tensor(f"in_{name}", v.shape, mybir.dt.from_np(v.dtype), kind="ExternalInput").ap()
    out = nc.dram_tensor("out_0", (1, TOKENS, DIM), F32, kind="ExternalOutput").ap()
    build(nc, a, out, stages)
    r = _run(nc, [arrays], core_ids=[0])
    return r.results[0]["out_0"]
```

```python
from contextlib import ExitStack

import numpy as np

import concourse.bass as bass
from concourse import mybir

F32 = mybir.dt.float32
BF16 = mybir.dt.bfloat16
U32 = mybir.dt.uint32
ACT = mybir.ActivationFunctionType
ALU = mybir.AluOpType
AX_X = mybir.AxisListType.X

P = 128
TOKENS = 2048
DIM = 256
TILES = TOKENS // P
CHUNKS = DIM // P
EPS = 1e-5

EXPERTS = 64
TOPK = 6
UPFRONT = 6
PIECES = [("down", 2), ("down", 3), ("up", 6), ("up", 7), ("up", 8), ("down", 4), ("down", 5),
          ("up", 9), ("up", 10), ("up", 11), ("down", 6), ("down", 7)]
CAP = 32
INNER = 176
HALF = INNER // 2
SHARED = 352
EPG = P // CAP
GROUPS = EXPERTS // EPG
ROW = DIM + EXPERTS
SHARED_CHUNKS = [(0, 128), (128, 128), (256, 96)]
BIG = 3.0e38
WBUFS = 4

LHEADS, LHD = 8, 32
MIX_EXPERTS = 8
HEADS, HD = 16, 16
BLOCK = 512
BLOCKS = TOKENS // BLOCK
HPG = 4
HGROUPS = HEADS // HPG
STEPS = HGROUPS * BLOCKS
STACK = 6 * HD
STACK_M = STACK + 3
EARLY = 8
Q_PARTS = [0, 0, 1, 1, 0, 2]
K_PARTS = [0, 1, 0, 1, 2, 0]


class Chain:

    def __init__(self, eng, sem):
        self.eng, self.sem, self.n, self.turn = eng, sem, 0, None

    def at(self):
        return self.n if self.turn is None else self.n + self.turn[0] * self.turn[1]

    def __call__(self, ins):
        ins.then_inc(self.sem, 1)
        self.n += 1
        self.eng.wait_ge(self.sem, self.at())

    def enter(self, i, per):
        self.turn, self.start = (i, per), self.n

    def leave(self, trips):
        per = self.turn[1]
        assert self.n - self.start == per, (self.n - self.start, per)
        self.turn, self.n = None, self.start + per * trips


def build(nc, a, out, stages=6):
    ctx = ExitStack()
    with ctx:
        _program(nc, ctx, a, out, stages)


def _program(nc, ctx, a, out, stages):
    def sem(name):
        return ctx.enter_context(nc.semaphore(name))

    def sems(tag, names):
        return {n: sem(f"{tag}_{n}") for n in names.split()}

    made, calls = {}, {}

    def shared_sems(kind, totals):
        if kind not in made:
            made[kind] = sems(kind, " ".join(totals))
        n = calls[kind] = calls.get(kind, -1) + 1
        return made[kind], {k: n * v for k, v in totals.items()}

    def sb(name, shape, dt=F32):
        return ctx.enter_context(nc.sbuf_tensor(name, shape, dt))

    def dram(name, shape, dt=F32):
        return nc.dram_tensor(name, shape, dt, kind="Internal").ap()

    x = sb("x_res", [P, TILES, DIM])
    xn = sb("xn", [P, TILES, DIM])
    xnT = sb("xnT", [P, CHUNKS, TOKENS])
    stats = sb("stats", [P, TILES, 6])
    mv = sb("mv", [P, TILES, 2])
    rstd = sb("rstd", [P, 4, TILES])
    ident = sb("ident_sb", [P, P])
    ident_bf = sb("ident_bf", [P, P], BF16)
    AREA = 40400
    area = sb("area", [P, AREA])
    psum = ctx.enter_context(nc.psum_tensor("psum", [P, 8 * 512], F32))
    bank = [psum[:, 512 * i:512 * (i + 1)] for i in range(8)]

    class Carve:
        def __init__(self):
            self.at = 0

        def __call__(self, words, dt=F32, parts=P):
            v = area[0:parts, self.at:self.at + words]
            self.at += words
            assert self.at <= AREA, self.at
            return v if dt is F32 else v.bitcast(dt)

    s_const = sem("const_loaded")
    s_const2 = sem("const_made")
    s_x = sem("x_loaded")
    chain_sems = {e: sem(f"chain_{e}") for e in ("dve", "act", "pool")}
    chains = {}

    def layer_norm(s_ready, n_ready, have_stats):
        s, base = shared_sems("ln", dict(var=1, root=1, xn=TILES, tr=TILES // 2, xnT=TILES // 2))

        def dve(v):
            link = chains["dve"]
            v.wait_ge(s_ready, n_ready)
            for t in range(TILES - 1 if have_stats else 0, TILES):
                ins = nc.vector.bn_stats(stats[:, t, :], x[:, t, :])
            link(ins)
            for t in range(TILES):
                ins = nc.vector.bn_aggr(mv[:, t, :], stats[:, t, :])
            link(ins)
            var, r = rstd[:, 0, :], rstd[:, 2, :]
            nc.vector.tensor_scalar(var, mv[:, :, 1], EPS, None, ALU.add).then_inc(s["var"], 1)
            v.wait_ge(s["root"], base["root"] + 1)
            link(nc.vector.reciprocal(r, rstd[:, 1, :]))
            link(nc.vector.tensor_tensor(rstd[:, 3, :], r, r, ALU.mult))
            link(nc.vector.tensor_tensor(rstd[:, 3, :], rstd[:, 3, :], var, ALU.mult))
            link(nc.vector.tensor_scalar(rstd[:, 3, :], rstd[:, 3, :], -0.5, 1.5, ALU.mult, ALU.add))
            link(nc.vector.tensor_tensor(r, r, rstd[:, 3, :], ALU.mult))
            for t in range(TILES):
                nc.vector.tensor_scalar(xn[:, t, :], x[:, t, :], mv[:, t, 0:1], rstd[:, 2, t:t + 1],
                                        ALU.subtract, ALU.mult).then_inc(s["xn"], 1)

        def act(e):
            e.wait_ge(s["var"], base["var"] + 1)
            nc.scalar.activation(rstd[:, 1, :], rstd[:, 0, :], ACT.Sqrt).then_inc(s["root"], 1)
            for t2 in range(TILES // 2):
                e.wait_ge(s["tr"], base["tr"] + t2 + 1)
                nc.scalar.copy(xnT[:, :, 2 * P * t2:2 * P * (t2 + 1)].rearrange("p c (t n) -> p t c n", t=2),
                               bank[t2 % 2][:].rearrange("p (t c n) -> p t c n", t=2, c=CHUNKS)
                               ).then_inc(s["xnT"], 1)

        def pe(e):
            for t in range(TILES):
                e.wait_ge(s["xn"], base["xn"] + t + 1)
                if t % 2 == 0 and t >= 4:
                    e.wait_ge(s["xnT"], base["xnT"] + t // 2 - 1)
                for c in range(CHUNKS):
                    o = (t % 2) * 2 * P + c * P
                    ins = nc.tensor.transpose(bank[t // 2 % 2][:, o:o + P], xn[:, t, c * P:(c + 1) * P], ident[:])
                if t % 2:
                    ins.then_inc(s["tr"], 1)

        return (s, base), dve, act, pe

    table = dram("dispatch_table", [TOKENS + 1, ROW])
    slot_dram = dram("slot_tokens", [EXPERTS, CAP])

    def out_stats(v, s_out, at, t):
        if t >= 1:
            v.wait_ge(s_out, at + t)
            nc.vector.bn_stats(stats[:, t - 1, :], x[:, t - 1, :])

    def moe(tag, s_ready, n_ready, have_stats):
        (ln, ln_base), ln_dve, ln_act, ln_pe = layer_norm(s_ready, n_ready, have_stats)
        s, base = shared_sems("moe", dict(
            w=7 * 16, wsh=64, rows=32, halfin=16, tokrow=32, logit=4, shmm=12, mt=2, tokt=1, xgt=GROUPS, gu=GROUPS, ht=GROUPS,
            y=GROUPS, lgsb=5, exp=1, shg=12, shu=12, bufT=GROUPS, sg=GROUPS, hTsb=GROUPS, expin=1,
            msk=1, prob=2, key=2, half=1, tok=1, idx=1, sel=1, h=GROUPS, out=1, hs=12, ysplit=GROUPS,
            xrow=16, sdm=8, sdx=8, seen=1, seent=1, pairs=1, gat0=64, gat1=64, gat2=64, gat3=64,
            **{f"wb{b}": 48 * GROUPS // WBUFS for b in range(WBUFS)}))
        sl = sems(tag, "oneh mix done")
        s_w = [s[f"wb{b}"] for b in range(WBUFS)]
        s_gat = [s[f"gat{b}"] for b in range(4)]
        c = Carve()
        gu_w = [c(EPG * CHUNKS * SHARED).rearrange("p (e k i) -> p e k i", e=EPG, k=CHUNKS) for _ in range(WBUFS)]
        dn_w = [c(EPG * 2 * DIM).rearrange("p (e k d) -> p e k d", e=EPG, k=2) for _ in range(WBUFS)]
        hsT = xn[:].rearrange("p t d -> p (t d)")[:, 0:6 * BLOCK].rearrange("p (b c n) -> p b c n", b=2, c=3)
        top = c.at
        lg = c(TILES * 66).rearrange("p (t e) -> p t e", t=TILES)
        rep = c(TILES * 66).rearrange("p (t e) -> p t e", t=TILES)
        msk = c(TILES * EXPERTS).rearrange("p (t h e) -> p t h e", t=TILES // 2, h=2)
        keyA = c(TOKENS // 2)
        keyB = c(TOKENS // 2)
        end = c.at
        c.at = top
        yp = c(3 * GROUPS * DIM // 2, BF16).rearrange("p (k g d) -> p k g d", k=3, g=GROUPS)
        c.at = max(c.at, end)
        top = c.at
        xg = c(GROUPS * ROW).rearrange("p (g r) -> p g r", g=GROUPS)
        end = c.at
        c.at = top
        prob = c(TILES * EXPERTS).rearrange("p (t e) -> p t e", t=TILES)
        assert c.at <= end
        c.at = end
        sg_sh = [xn[:].rearrange("p t d -> p (t d)")[:, (6 + i) * BLOCK:(7 + i) * BLOCK] for i in range(2)]
        su_sh = [c(BLOCK) for _ in range(2)]
        top = c.at
        oneh = [c(GROUPS * P // 2, BF16).rearrange("p (g n) -> p g n", g=GROUPS) for _ in range(2)]
        c.at = top
        bufT = [c(DIM).rearrange("p (k n) -> p k n", k=2) for _ in range(2)]
        sg = [c(INNER) for _ in range(2)]
        hh = [c(INNER) for _ in range(2)]
        hT = [c(DIM).rearrange("p (k n) -> p k n", k=2) for _ in range(2)]
        yres = [c(DIM) for _ in range(2)]
        c.at = max(c.at, top + GROUPS * P)
        gate = c(2 * P).rearrange("p (k e) -> p k e", k=2)
        sh_w = c(CHUNKS * 2 * SHARED).rearrange("p (k g i) -> p k g i", k=CHUNKS, g=2)
        sh_d = c(3 * DIM).rearrange("p (c d) -> p c d", c=3)
        v8 = c(TILES * 8).rearrange("p (t e) -> p t e", t=TILES)
        r8 = c(TILES * 8).rearrange("p (t e) -> p t e", t=TILES)
        esum = c(TILES)
        einv = c(TILES)
        top32 = c(64)
        best = c(CAP)
        bestB = c(64)
        tok = c(CAP)
        tokrow = c(P, parts=GROUPS)
        tokp = c(GROUPS)
        idx = c(GROUPS, U32)
        rel = c((TILES + 1) * GROUPS // 2, BF16).rearrange("p (t g) -> p t g", t=TILES + 1)
        seen = c(GROUPS)
        last = c(1)
        lastT, reached = c(1, parts=1), c(8, parts=1)
        thresh = c(8, parts=1)
        pairs = c(1, U32, parts=1)
        wsel = c(GROUPS)
        junk = c(EPG)
        iota_n = c(TOKENS // 2)
        iota_bf = c(P // 2, BF16)
        tile_off = c(TILES + 1)
        key_off = c(1)
        jmask = c(EPG)
        zrow = c(ROW, parts=1)
        w_gate, w_up, w_down = a["L0_ffn_w_gate"], a["L0_ffn_w_up"], a["L0_ffn_w_down"]

        def load_group(e, g):
            b = g % WBUFS
            if g >= WBUFS:
                e.wait_ge(s["y"], base["y"] + g - WBUFS + 1)
            es = slice(EPG * g, EPG * (g + 1))
            e.dma_start(gu_w[b][:, :, :, 0:INNER], w_gate[es].rearrange("e (k p) i -> p e k i", p=P)).then_inc(s_w[b], 16)
            e.dma_start(gu_w[b][:, :, :, INNER:SHARED], w_up[es].rearrange("e (k p) i -> p e k i", p=P)).then_inc(s_w[b], 16)
            e.dma_start(dn_w[b][0:HALF], w_down[es].rearrange("e (k p) d -> p e k d", p=HALF)).then_inc(s_w[b], 16)

        first = base["y"] == 0

        def sync(e):
            if not first:
                e.wait_ge(s["y"], base["y"])
                for g in range(WBUFS):
                    load_group(e, g)
            e.wait_ge(s_ready, n_ready)
            e.dma_start(gate[:, :, 0:EXPERTS], a["gate_T"].rearrange("(k p) e -> p k e", p=P)).then_inc(s["w"], 16)
            for dst, src in ((iota_n, "iota_row"), (iota_bf, "iota_bf"), (tile_off, "tile_off"),
                             (key_off, "key_off"), (jmask, "slot_mask"), (thresh, "pair_starts")):
                e.dma_start(dst, a[src]).then_inc(s["w"], 16)
            e.dma_start(sh_w[:, :, 0, :], a["L0_ffn_sw_gate"].rearrange("(k p) i -> p k i", p=P)).then_inc(s["wsh"], 16)
            e.dma_start(sh_w[:, :, 1, :], a["L0_ffn_sw_up"].rearrange("(k p) i -> p k i", p=P)).then_inc(s["wsh"], 16)
            e.dma_start(sh_d[:, 0:2, :], a["L0_ffn_sw_down"][0:2 * P].rearrange("(c p) d -> p c d", p=P)).then_inc(s["wsh"], 16)
            e.dma_start(sh_d[0:96, 2, :], a["L0_ffn_sw_down"][2 * P:SHARED]).then_inc(s["wsh"], 16)
            if first:
                e.wait_ge(s["wsh"], base["wsh"] + 64)
                for g in range(WBUFS):
                    load_group(e, g)
            e.wait_ge(ln["xn"], ln_base["xn"] + TILES)
            body = table[0:TOKENS].rearrange("(t p) r -> p t r", p=P)
            e.dma_start(body[:, :, 0:DIM], xn[:]).then_inc(s["xrow"], 16)
            e.wait_ge(s["prob"], base["prob"] + 2)
            e.dma_start(body[:, :, DIM:ROW], prob).then_inc(s["rows"], 16)
            e.dma_start(table[TOKENS:TOKENS + 1], zrow).then_inc(s["rows"], 16)
            e.wait_ge(s["half"], base["half"] + 1)
            e.dma_start(top32[0:64, CAP:2 * CAP], top32[64:128, 0:CAP]).then_inc(s["halfin"], 16)
            e.wait_ge(s["tok"], base["tok"] + 1)
            e.dma_start(slot_dram, tok[0:EXPERTS]).then_inc(s["tokrow"], 16)
            e.wait_ge(s["tokrow"], base["tokrow"] + 16)
            e.dma_start(tokrow, slot_dram.rearrange("(g j) c -> g (j c)", j=EPG)).then_inc(s["tokrow"], 16)
            for g in range(WBUFS, GROUPS):
                load_group(e, g)

        def pe(e):
            ln_pe(e)
            e.wait_ge(s["w"], base["w"] + 7 * 16)
            e.wait_ge(s["lgsb"], base["lgsb"] + 1)
            for t in range(TILES):
                e.wait_ge(ln["xnT"], ln_base["xnT"] + t // 2 + 1)
                b = bank[2 + t // 4 % 2]
                if t % 4 == 0 and t >= 8:
                    e.wait_ge(s["lgsb"], base["lgsb"] + 1 + t // 4 - 1)
                for k in range(CHUNKS):
                    ins = nc.tensor.matmul(b[:, (t % 4) * P:(t % 4 + 1) * P], xnT[:, k, t * P:(t + 1) * P],
                                           gate[:, k, :], start=(k == 0), stop=(k == CHUNKS - 1))
                if t % 4 == 3:
                    ins.then_inc(s["logit"], 1)
            e.wait_ge(s["wsh"], base["wsh"] + 64)

            def shared_up(n):
                blk, ch = n // 3, n % 3
                lo, w = SHARED_CHUNKS[ch]
                pair = 4 + 2 * (n % 2 if n < UPFRONT else 0)
                if n >= 2:
                    e.wait_ge(s["shu"], base["shu"] + (n - 1 if n < UPFRONT else n))
                for gu in range(2):
                    for k in range(CHUNKS):
                        ins = nc.tensor.matmul(bank[pair + gu][0:w, :], sh_w[:, k, gu, lo:lo + w],
                                               xnT[:, k, blk * BLOCK:(blk + 1) * BLOCK],
                                               start=(k == 0), stop=(k == CHUNKS - 1))
                ins.then_inc(s["shmm"], 1)

            def shared_down(n):
                blk, h = n // 2, n % 2
                e.wait_ge(s["hs"], base["hs"] + 3 * blk + 3)
                if n >= 3:
                    e.wait_ge(s["sdx"], base["sdx"] + n)
                elif n == 2:
                    e.wait_ge(s["shu"], base["shu"] + UPFRONT)
                for q in range(2):
                    t = 2 * h + q
                    for ch, (lo, w) in enumerate(SHARED_CHUNKS):
                        ins = nc.tensor.matmul(bank[n if n < 2 else 7][:, q * DIM:(q + 1) * DIM],
                                               hsT[0:w, blk % 2, ch, t * P:(t + 1) * P], sh_d[0:w, ch, :],
                                               start=(ch == 0), stop=(ch == 2))
                ins.then_inc(s["sdm"], 1)

            shared_up(0)
            e.wait_ge(s["msk"], base["msk"] + 1)
            e.wait_ge(s["lgsb"], base["lgsb"] + 5)
            for i in range(TILES // 2):
                ins = nc.tensor.transpose(bank[2 + i // 4][:, (i % 4) * P:(i % 4 + 1) * P],
                                          msk[:, i, :, :].rearrange("p h e -> p (h e)"), ident[:])
                if i % 4 == 3:
                    ins.then_inc(s["mt"], 1)
            for n in range(1, 5):
                shared_up(n)
            shared_down(0)
            shared_down(1)
            e.wait_ge(s["tokrow"], base["tokrow"] + 32)
            e.wait_ge(s["key"], base["key"] + 2)
            nc.tensor.transpose(bank[2][:, 0:GROUPS], tokrow, ident[0:GROUPS, 0:GROUPS]).then_inc(s["tokt"], 1)
            shared_up(5)
            e.wait_ge(s["seen"], base["seen"] + 1)
            nc.tensor.transpose(bank[3][0:1, 0:P], last, ident[:]).then_inc(s["seent"], 1)

            def rows_T(g):
                e.wait_ge(s_gat[g // 4], base["gat0"] + 64)
                if g >= 1:
                    e.wait_ge(s["bufT"], base["bufT"] + g)
                else:
                    e.wait_ge(s["sdx"], base["sdx"] + 2)
                for k in range(CHUNKS):
                    ins = nc.tensor.transpose(bank[0][:, k * P:(k + 1) * P], xg[:, g, k * P:(k + 1) * P], ident[:])
                ins.then_inc(s["xgt"], 1)

            def gate_up(g):
                e.wait_ge(s_w[g % WBUFS], base[f"wb{g % WBUFS}"] + 48 * (g // WBUFS + 1))
                e.wait_ge(s["bufT"], base["bufT"] + g + 1)
                if g >= 2:
                    e.wait_ge(s["h"], base["h"] + g - 1)
                else:
                    e.wait_ge(s["pairs"], base["pairs"] + 1)
                for k in range(CHUNKS):
                    for j in range(EPG):
                        ins = nc.tensor.matmul(bank[2 + g % 2][CAP * j:CAP * (j + 1), 0:SHARED],
                                               bufT[g % 2][:, k, CAP * j:CAP * (j + 1)], gu_w[g % WBUFS][:, j, k, :],
                                               start=(k == 0), stop=(k == CHUNKS - 1))
                ins.then_inc(s["gu"], 1)

            def hidden_T(g):
                e.wait_ge(s["h"], base["h"] + g + 1)
                if g >= 1:
                    e.wait_ge(s["hTsb"], base["hTsb"] + g)
                for k in range(2):
                    ins = nc.tensor.transpose(bank[1][0:HALF, k * P:(k + 1) * P],
                                              hh[g % 2][:, k * HALF:(k + 1) * HALF], ident[:])
                ins.then_inc(s["ht"], 1)

            def down(g):
                e.wait_ge(s["hTsb"], base["hTsb"] + g + 1)
                if g >= 1:
                    e.wait_ge(s["ysplit"], base["ysplit"] + g)
                else:
                    e.wait_ge(s["shu"], base["shu"] + UPFRONT)
                for k in range(2):
                    for j in range(EPG):
                        ins = nc.tensor.matmul(bank[6][CAP * j:CAP * (j + 1), 0:DIM],
                                               hT[g % 2][0:HALF, k, CAP * j:CAP * (j + 1)],
                                               dn_w[g % WBUFS][0:HALF, j, k, :], start=(k == 0), stop=(k == 1))
                ins.then_inc(s["y"], 1)

            rows_T(0)
            for g in range(GROUPS + 1):
                if g < GROUPS:
                    gate_up(g)
                if g >= 1:
                    hidden_T(g - 1)
                if g + 1 < GROUPS:
                    rows_T(g + 1)
                if g >= 1:
                    down(g - 1)
                if g < len(PIECES):
                    kind, n = PIECES[g]
                    (shared_up if kind == "up" else shared_down)(n)
            e.wait_ge(s["pairs"], base["pairs"] + 1)
            n_pairs = e.value_load(pairs, min_val=1, max_val=TILES // 2)
            with e.Fori(0, n_pairs) as i:
                for r in range(2):
                    t = i * 2 + r
                    e.wait_ge(sl["oneh"], t + 1)
                    e.wait_ge(sl["done"], t + 1)
                    b = bank[r][:, 0:DIM]
                    for g in range(GROUPS):
                        for k in range(3):
                            ins = nc.tensor.matmul(b, oneh[r][:, g, :], yp[:, k, g, :], start=(g == 0 and k == 0),
                                                   stop=(g == GROUPS - 1 and k == 2))
                    ins.then_inc(sl["mix"], 1)

        def act(e):
            ln_act(e)
            for q in range(TILES // 4):
                e.wait_ge(s["logit"], base["logit"] + q + 1)
                nc.scalar.copy(lg[:, 4 * q:4 * q + 4, 0:EXPERTS],
                               bank[2 + q % 2][:].rearrange("p (t e) -> p t e", t=4)[:, :, 0:EXPERTS]
                               ).then_inc(s["lgsb"], 1)

            def shared(n):
                w = SHARED_CHUNKS[n % 3][1]
                pair = 4 + 2 * (n % 2 if n < UPFRONT else 0)
                e.wait_ge(s["shmm"], base["shmm"] + n + 1)
                if n >= 2:
                    e.wait_ge(s["hs"], base["hs"] + n - 1)
                nc.scalar.activation(sg_sh[n % 2][0:w], bank[pair][0:w, :], ACT.Silu).then_inc(s["shg"], 1)
                nc.scalar.copy(su_sh[n % 2][0:w], bank[pair + 1][0:w, :]).then_inc(s["shu"], 1)

            e.wait_ge(s["expin"], base["expin"] + 1)
            nc.scalar.activation(prob, prob, ACT.Exp).then_inc(s["exp"], 1)
            e.wait_ge(s["xrow"], base["xrow"] + 16)
            e.wait_ge(ln["xnT"], ln_base["xnT"] + TILES // 2)
            for n in range(UPFRONT):
                shared(n)
            for g in range(GROUPS + 1):
                if g < GROUPS:
                    e.wait_ge(s["xgt"], base["xgt"] + g + 1)
                    if g >= 2:
                        e.wait_ge(s["gu"], base["gu"] + g - 1)
                    nc.scalar.copy(bufT[g % 2], bank[0][:, 0:DIM].rearrange("p (k n) -> p k n", k=2)
                                   ).then_inc(s["bufT"], 1)
                    e.wait_ge(s["gu"], base["gu"] + g + 1)
                    if g >= 2:
                        e.wait_ge(s["h"], base["h"] + g - 1)
                    nc.scalar.activation(sg[g % 2], bank[2 + g % 2][:, 0:INNER], ACT.Silu).then_inc(s["sg"], 1)
                if g >= 1:
                    e.wait_ge(s["ht"], base["ht"] + g)
                    if g >= 3:
                        e.wait_ge(s["y"], base["y"] + g - 2)
                    nc.scalar.copy(hT[(g - 1) % 2][0:HALF], bank[1][0:HALF, 0:DIM]
                                   .rearrange("p (k n) -> p k n", k=2)).then_inc(s["hTsb"], 1)
                if 1 <= g <= len(PIECES) and PIECES[g - 1][0] == "up":
                    shared(PIECES[g - 1][1])

        def dve(v):
            link = chains["dve"]
            ln_dve(v)
            v.wait_ge(s_ready, n_ready)
            nc.vector.memset(gate[:, :, EXPERTS:P], 0.0)
            nc.vector.memset(lg[:, :, EXPERTS:66], -BIG)
            nc.vector.memset(zrow, 0.0)
            nc.vector.memset(r8[:, :, TOPK:8], -BIG).then_inc(s["lgsb"], 1)
            for t in range(TILES):
                if t % 4 == 0:
                    v.wait_ge(s["lgsb"], base["lgsb"] + 2 + t // 4)
                ins = nc.vector.max(v8[:, t, :], lg[:, t, 0:EXPERTS])
            link(ins)
            nc.vector.tensor_tensor(prob, lg[:, :, 0:EXPERTS], v8[:, :, 0:1].to_broadcast([P, TILES, EXPERTS]),
                                    ALU.subtract).then_inc(s["expin"], 1)
            link(nc.vector.tensor_copy(r8[:, :, 0:TOPK], v8[:, :, 0:TOPK]))
            for t in range(TILES):
                ins = nc.vector.match_replace(rep[:, t, :], r8[:, t, :], lg[:, t, :], BIG)
            link(ins)
            for h in range(2):
                ins = nc.vector.tensor_scalar(msk[:, :, h, :], rep[:, h * 8:(h + 1) * 8, 0:EXPERTS], 1.0e38, None, ALU.is_gt)
            ins.then_inc(s["msk"], 1)
            v.wait_ge(s["exp"], base["exp"] + 1)
            link(nc.vector.tensor_reduce(esum, prob, AX_X, ALU.add))
            link(nc.vector.reciprocal(einv, esum))
            nc.vector.tensor_tensor(prob, prob, einv.rearrange("p (t o) -> p t o", o=1).to_broadcast([P, TILES, EXPERTS]),
                                    ALU.mult).then_inc(s["prob"], 2)
            for i in range(2):
                v.wait_ge(s["mt"], base["mt"] + i + 1)
                ins = nc.vector.scalar_tensor_tensor(out=keyA[:, 512 * i:512 * (i + 1)], in0=iota_n[:, 512 * i:512 * (i + 1)],
                                                     scalar=key_off, in1=bank[2 + i][:], op0=ALU.add, op1=ALU.mult)
                ins.then_inc(s["key"], 1)
            v.wait_ge(s["key"], base["key"] + 2)
            src, dst = keyA, keyB
            for r in range(CAP // 8):
                ins = nc.vector.max(top32[:, 8 * r:8 * r + 8], src)
                if r == CAP // 8 - 1:
                    ins.then_inc(s["half"], 1)
                else:
                    link(ins)
                    link(nc.vector.match_replace(dst, top32[:, 8 * r:8 * r + 8], src, 0.0))
                    src, dst = dst, src
            v.wait_ge(s["halfin"], base["halfin"] + 16)
            v.wait_ge(s["half"], base["half"] + 1)
            src, dst = top32[0:EXPERTS], bestB[0:EXPERTS]
            for r in range(CAP // 8):
                link(nc.vector.max(best[0:EXPERTS, 8 * r:8 * r + 8], src))
                if r < CAP // 8 - 1:
                    link(nc.vector.match_replace(dst, best[0:EXPERTS, 8 * r:8 * r + 8], src, 0.0))
                    src, dst = dst, src
            nc.vector.tensor_scalar(tok[0:EXPERTS], best[0:EXPERTS], -1.0, float(TOKENS), ALU.mult, ALU.add
                                    ).then_inc(s["tok"], 1)

            def shared_add(n):
                v.wait_ge(s["sdm"], base["sdm"] + n + 1)
                xs = x[:, 2 * n:2 * n + 2, :]
                nc.vector.scalar_tensor_tensor(out=xs, in0=bank[n if n < 2 else 7].rearrange("p (t d) -> p t d", t=2),
                                               scalar=0.5, in1=xs, op0=ALU.mult, op1=ALU.add).then_inc(s["sdx"], 1)

            v.wait_ge(s["tokt"], base["tokt"] + 1)
            nc.vector.tensor_copy(tokp, bank[2][:, 0:GROUPS])
            nc.vector.tensor_copy(idx, bank[2][:, 0:GROUPS]).then_inc(s["idx"], 1)
            v.wait_ge(s["idx"], base["idx"] + 1)
            link(nc.vector.scalar_tensor_tensor(out=seen, in0=tokp, scalar=TOKENS - 0.5, in1=tokp, op0=ALU.is_lt, op1=ALU.mult))
            nc.vector.tensor_reduce(last, seen, AX_X, ALU.max).then_inc(s["seen"], 1)
            shared_add(0)
            shared_add(1)
            v.wait_ge(s["seent"], base["seent"] + 1)
            link(nc.vector.tensor_reduce(lastT, bank[3][0:1, 0:P], AX_X, ALU.max))
            link(nc.vector.tensor_scalar(reached, thresh, lastT, None, ALU.is_le))
            link(nc.vector.tensor_reduce(lastT, reached, AX_X, ALU.add))
            nc.vector.tensor_copy(pairs, lastT).then_inc(s["pairs"], 1)
            link(nc.vector.tensor_tensor(rel, tokp.rearrange("p (o g) -> p o g", o=1).to_broadcast([P, TILES + 1, GROUPS]),
                                         tile_off.rearrange("p (t o) -> p t o", o=1).to_broadcast([P, TILES + 1, GROUPS]),
                                         ALU.subtract))

            def slot_weights(q):
                v.wait_ge(s_gat[q], base["gat0"] + 64)
                for g in range(4 * q, 4 * q + 4):
                    o = DIM + EPG * g
                    link(nc.vector.tensor_tensor_reduce(out=junk, in0=xg[:, g, o:o + EPG], in1=jmask, scale=1.0,
                                                        scalar=0.0, op0=ALU.mult, op1=ALU.add, accum_out=wsel[:, g:g + 1]))

            def split(g):
                v.wait_ge(s["y"], base["y"] + g + 1)
                y, w, r = bank[6][:, 0:DIM], wsel[:, g:g + 1], yres[g % 2]
                link(nc.vector.tensor_scalar(yp[:, 0, g, :], y, w, None, ALU.mult))
                nc.vector.scalar_tensor_tensor(out=r, in0=y, scalar=w, in1=yp[:, 0, g, :], op0=ALU.mult, op1=ALU.subtract
                                               ).then_inc(s["ysplit"], 1)
                v.wait_ge(s["ysplit"], base["ysplit"] + g + 1)
                link(nc.vector.tensor_copy(yp[:, 1, g, :], r))
                link(nc.vector.tensor_tensor(yp[:, 2, g, :], r, yp[:, 1, g, :], ALU.subtract))

            for g in range(GROUPS + 1):
                if g < GROUPS:
                    if g % 4 == 0:
                        slot_weights(g // 4)
                    v.wait_ge(s["sg"], base["sg"] + g + 1)
                    if g >= 2:
                        v.wait_ge(s["ht"], base["ht"] + g - 1)
                    nc.vector.tensor_tensor(hh[g % 2], sg[g % 2], bank[2 + g % 2][:, INNER:SHARED], ALU.mult
                                            ).then_inc(s["h"], 1)
                if g >= 1:
                    split(g - 1)
                if g < len(PIECES) and PIECES[g][0] == "down":
                    shared_add(PIECES[g][1])
            v.wait_ge(s["ysplit"], base["ysplit"] + GROUPS)
            v.wait_ge(s["pairs"], base["pairs"] + 1)
            v.wait_ge(s["sdx"], base["sdx"] + 8)

            def one_hot(rel_t, r):
                nc.vector.tensor_tensor(oneh[r], rel_t.to_broadcast([P, GROUPS, P]),
                                        iota_bf.rearrange("p (o n) -> p o n", o=1).to_broadcast([P, GROUPS, P]),
                                        ALU.is_equal).then_inc(sl["oneh"], 1)

            nc.vector.memset(seen, 0.0).then_inc(sl["done"], 2)
            one_hot(rel[:, 0, :].rearrange("p (g o) -> p g o", o=1), 0)
            n_pairs = v.value_load(pairs, min_val=1, max_val=TILES // 2)
            with v.Fori(0, n_pairs) as i:
                for r in range(2):
                    t = i * 2 + r
                    one_hot(rel[:, bass.ds(t + 1, 1), :].rearrange("p o g -> p g o"), 1 - r)
                    v.wait_ge(sl["mix"], t + 1)
                    xt = x[:, bass.ds(t, 1), :].rearrange("p o d -> p (o d)")
                    nc.vector.scalar_tensor_tensor(out=xt, in0=bank[r][:, 0:DIM], scalar=0.5, in1=xt,
                                                   op0=ALU.mult, op1=ALU.add).then_inc(sl["done"], 1)
            v.wait_ge(sl["done"], n_pairs * 2 + 2)
            nc.vector.memset(seen, 0.0).then_inc(s["out"], 1)

        def pool(e):
            link = chains["pool"]
            def hidden(n):
                blk, ch = n // 3, n % 3
                w = SHARED_CHUNKS[ch][1]
                if n == 0:
                    e.wait_ge(s["xrow"], base["xrow"] + 16)
                    e.wait_ge(ln["xnT"], ln_base["xnT"] + TILES // 2)
                if blk >= 2 and ch == 0:
                    e.wait_ge(s["sdm"], base["sdm"] + 2 * blk - 2)
                e.wait_ge(s["shg"], base["shg"] + n + 1)
                e.wait_ge(s["shu"], base["shu"] + n + 1)
                nc.gpsimd.tensor_tensor(hsT[0:w, blk % 2, ch, :], sg_sh[n % 2][0:w], su_sh[n % 2][0:w],
                                        ALU.mult).then_inc(s["hs"], 1)
            for n in range(UPFRONT - 1):
                hidden(n)
            e.wait_ge(s["idx"], base["idx"] + 1)
            e.wait_ge(s["rows"], base["rows"] + 32)
            for g in range(GROUPS):
                e.indirect_dma_start(xg[:, g, :], None, table, bass.IndirectOffsetOnAxis(ap=idx[:, g:g + 1], axis=0)
                                     ).then_inc(s_gat[g // 4], 16)
            for n in range(UPFRONT - 1, 12):
                hidden(n)

        return (s["out"], base["out"] + 1), dict(sync=sync, tensor=pe, scalar=act, vector=dve, gpsimd=pool)

    def linear_attention(tag, s_ready, n_ready, have_stats):
        (ln, ln_base), ln_dve, ln_act, ln_pe = layer_norm(s_ready, n_ready, have_stats)
        s = sems(tag, "w kv kr vv vk mem qmm qT o on ot oT pj xb out")
        c = Carve()
        c.at = WBUFS * EPG * (CHUNKS * SHARED + 2 * DIM)
        wq = c(CHUNKS * DIM).rearrange("p (k e) -> p k e", k=CHUNKS)
        wkv = c(CHUNKS * 2 * DIM).rearrange("p (k e) -> p k e", k=CHUNKS)
        wp = c(CHUNKS * DIM).rearrange("p (k e) -> p k e", k=CHUNKS)
        bp = c(DIM)
        hmask = c(4)
        kr = [c(DIM) for _ in range(2)]
        vv = [c(2 * 129).rearrange("p (c n) -> p c n", c=2) for _ in range(2)]
        qT = c(CHUNKS * TOKENS).rearrange("p (c n) -> p c n", c=CHUNKS)
        W33 = 4 * (LHD + 1)
        mem = c(2 * W33).rearrange("p (c h n) -> p c h n", c=2, h=4)
        den = [c(LHEADS) for _ in range(2)]
        on = [c(DIM) for _ in range(2)]
        oT = [c(DIM).rearrange("p (c n) -> p c n", c=2) for _ in range(2)]

        def sync(e):
            e.wait_ge(s_ready, n_ready)
            e.dma_start(wkv, a["wkv_T"].rearrange("(k p) e -> p k e", p=P)).then_inc(s["w"], 16)
            e.dma_start(wq, a["wq_T"].rearrange("(k p) e -> p k e", p=P)).then_inc(s["w"], 16)
            e.dma_start(wp, a["wproj_T"].rearrange("(k p) e -> p k e", p=P)).then_inc(s["w"], 16)
            e.dma_start(hmask, a["mask32"]).then_inc(s["w"], 16)
            e.dma_start(bp, a["L0_attn_b_proj"].rearrange("(o d) -> o d", o=1).to_broadcast([P, DIM])).then_inc(s["w"], 16)

        def pe(e):
            ln_pe(e)
            e.wait_ge(s["w"], 80)
            for t in range(TILES):
                e.wait_ge(ln["xnT"], ln_base["xnT"] + t // 2 + 1)
                if t >= 2:
                    e.wait_ge(s["kr"], t - 1)
                    e.wait_ge(s["vv"], t - 1)
                for half in range(2):
                    for k in range(CHUNKS):
                        ins = nc.tensor.matmul(bank[2 + 4 * half + t % 2][:, 0:DIM], xnT[:, k, t * P:(t + 1) * P],
                                               wkv[:, k, half * DIM:(half + 1) * DIM], start=(k == 0), stop=(k == 1))
                ins.then_inc(s["kv"], 1)
                if t >= 1:
                    memory(e, t - 1)
            memory(e, TILES - 1)
            for n in range(CHUNKS * BLOCKS):
                ch, blk = n // BLOCKS, n % BLOCKS
                if n >= 2:
                    e.wait_ge(s["qT"], n - 1)
                for k in range(CHUNKS):
                    ins = nc.tensor.matmul(bank[6 + n % 2][:], wq[:, k, ch * P:(ch + 1) * P],
                                           xnT[:, k, blk * BLOCK:(blk + 1) * BLOCK], start=(k == 0), stop=(k == 1))
                ins.then_inc(s["qmm"], 1)
            e.wait_ge(s["qT"], CHUNKS * BLOCKS)
            e.wait_ge(s["mem"], 2)
            for t in range(TILES + 1):
                if t < TILES:
                    if t >= 2:
                        e.wait_ge(s["on"], t - 1)
                    for ch in range(CHUNKS):
                        ins = nc.tensor.matmul(bank[t % 2][:, ch * W33:(ch + 1) * W33], qT[:, ch, t * P:(t + 1) * P],
                                               mem[:, ch], start=True, stop=True)
                    ins.then_inc(s["o"], 1)
                if t >= 1:
                    u = t - 1
                    e.wait_ge(s["on"], u + 1)
                    if u >= 2:
                        e.wait_ge(s["oT"], u - 1)
                    for ch in range(CHUNKS):
                        ins = nc.tensor.transpose(bank[2 + u % 2][:, ch * P:(ch + 1) * P], on[u % 2][:, ch * P:(ch + 1) * P], ident[:])
                    ins.then_inc(s["ot"], 1)
                    e.wait_ge(s["oT"], u + 1)
                    if u >= 2:
                        e.wait_ge(s["out"], u - 1)
                    for ch in range(CHUNKS):
                        ins = nc.tensor.matmul(bank[6 + u % 2][:, 0:DIM], oT[u % 2][:, ch], wp[:, ch], start=(ch == 0), stop=(ch == 1))
                    ins.then_inc(s["pj"], 1)

        def memory(e, t):
            e.wait_ge(s["kr"], t + 1)
            e.wait_ge(s["vv"], t + 1)
            for ch in range(CHUNKS):
                ins = nc.tensor.matmul(bank[4 + ch][:, 0:129], kr[t % 2][:, ch * P:(ch + 1) * P], vv[t % 2][:, ch, :],
                                       start=(t == 0), stop=(t == TILES - 1))
            ins.then_inc(s["vk"], 1)

        def act(e):
            ln_act(e)
            for t in range(TILES):
                e.wait_ge(s["kv"], t + 1)
                if t >= 2:
                    e.wait_ge(s["vk"], t - 1)
                nc.scalar.activation(kr[t % 2], bank[2 + t % 2][:, 0:DIM], ACT.Relu).then_inc(s["kr"], 1)
            for n in range(CHUNKS * BLOCKS):
                ch, blk = n // BLOCKS, n % BLOCKS
                e.wait_ge(s["qmm"], n + 1)
                nc.scalar.activation(qT[:, ch, blk * BLOCK:(blk + 1) * BLOCK], bank[6 + n % 2][:], ACT.Relu).then_inc(s["qT"], 1)
            for u in range(TILES):
                e.wait_ge(s["ot"], u + 1)
                if u >= 2:
                    e.wait_ge(s["pj"], u - 1)
                nc.scalar.copy(oT[u % 2], bank[2 + u % 2][:, 0:DIM].rearrange("p (c n) -> p c n", c=2)).then_inc(s["oT"], 1)

        def dve(v):
            link = chains["dve"]
            ln_dve(v)
            nc.vector.memset(vv[0][:, :, P:P + 1], 1.0)
            link(nc.vector.memset(vv[1][:, :, P:P + 1], 1.0))
            for t in range(TILES):
                v.wait_ge(s["kv"], t + 1)
                if t >= 2:
                    v.wait_ge(s["vk"], t - 1)
                nc.vector.tensor_copy(vv[t % 2][:, :, 0:P], bank[6 + t % 2][:, 0:DIM].rearrange("p (c n) -> p c n", c=2)
                                      ).then_inc(s["vv"], 1)
            v.wait_ge(s["vk"], TILES)
            v.wait_ge(s["w"], 80)
            hm = hmask.rearrange("p (h o) -> p h o", o=1)
            for ch in range(CHUNKS):
                b = bank[4 + ch]
                nc.vector.tensor_tensor(mem[:, ch, :, 0:LHD], b[:, 0:P].rearrange("p (h n) -> p h n", h=4),
                                        hm.to_broadcast([P, 4, LHD]), ALU.mult)
                nc.vector.tensor_scalar(mem[:, ch, :, LHD], hmask, b[:, P:P + 1], None, ALU.mult).then_inc(s["mem"], 1)
            for t in range(TILES + 2):
                if t < TILES:
                    v.wait_ge(s["o"], t + 1)
                    o = bank[t % 2][:, 0:2 * W33].rearrange("p (h n) -> p h n", h=LHEADS)
                    link(nc.vector.tensor_scalar(den[t % 2], o[:, :, LHD], 1e-15, None, ALU.add))
                    link(nc.vector.reciprocal(den[t % 2], den[t % 2]))
                    if t >= 2:
                        v.wait_ge(s["ot"], t - 1)
                    nc.vector.tensor_tensor(on[t % 2].rearrange("p (h n) -> p h n", h=LHEADS), o[:, :, 0:LHD],
                                            den[t % 2].rearrange("p (h o) -> p h o", o=1).to_broadcast([P, LHEADS, LHD]),
                                            ALU.mult).then_inc(s["on"], 1)
                if t >= 2:
                    u = t - 2
                    if u == 0:
                        v.wait_ge(s["xb"], 1)
                    v.wait_ge(s["pj"], u + 1)
                    nc.vector.tensor_tensor(x[:, u, :], bank[6 + u % 2][:, 0:DIM], x[:, u, :], ALU.add).then_inc(s["out"], 1)
                    out_stats(v, s["out"], 0, u)

        def pool(e):
            e.wait_ge(ln["xn"], ln_base["xn"] + TILES)
            e.wait_ge(s["w"], 80)
            nc.gpsimd.tensor_tensor(x[:], x[:], bp.rearrange("p (o d) -> p o d", o=1).to_broadcast([P, TILES, DIM]),
                                    ALU.add).then_inc(s["xb"], 1)

        return (s["out"], TILES), dict(sync=sync, tensor=pe, scalar=act, vector=dve, gpsimd=pool)

    def head_mixer(tag, s_ready, n_ready, have_stats):
        (ln, ln_base), ln_dve, ln_act, ln_pe = layer_norm(s_ready, n_ready, have_stats)
        NW = 16 * (32 + 5)
        s, base = shared_sems("mix", dict(
            sw=16 * MIX_EXPERTS, w=NW, lg=1, h=16, o=8, f=TILES, ex=1, g=16, part=1, ein=1, wb=1, bd=4, z=8, out=TILES, xb=1))
        E = MIX_EXPERTS
        c = Carve()
        sw = c(E * 2 * DIM).rearrange("p (e c d) -> p e c d", e=E, c=2)
        w3 = c(CHUNKS * DIM).rearrange("p (k e) -> p k e", k=CHUNKS)
        b3 = c(DIM)
        w1 = c(E * HD).rearrange("p (e f) -> p e f", e=E)
        w2 = c(E * HD).rearrange("p (e f) -> p e f", e=E)
        b1, b2, sbias, iota8 = c(E), c(E), c(E), c(E)
        hmask = c(8)
        ones = c(P)
        junk = c(2 * DIM).rearrange("p (c d) -> p c d", c=2)
        part, logit, m8, e8, esum = c(E), c(E), c(E), c(E), c(1)
        mi = c(E, U32)
        mif = c(E)
        oh = c(4 * E).rearrange("p (k e) -> p k e", k=4)
        tmp = c(E * HD)
        sel = c(4 * HD).rearrange("p (k f) -> p k f", k=4)
        bsel = c(4)
        tmpb = c(4 * E).rearrange("p (k e) -> p k e", k=4)
        b2s = c(1)
        bd = [[c(P) for _ in range(2)] for _ in range(2)]
        ht = [c(BLOCK) for _ in range(4)]
        z = [c(CHUNKS * BLOCK).rearrange("p (c n) -> p c n", c=2) for _ in range(2)]

        def sync(e):
            e.wait_ge(s_ready, n_ready)
            for ex in range(E):
                e.dma_start(sw[:, ex], a["L1_ffn_switch_w"][ex:ex + 1].rearrange("e (c p d) -> p (e c) d", p=P, c=2)).then_inc(s["sw"], 16)
            for h in range(8):
                hp = slice(HD * h, HD * (h + 1))
                e.dma_start(w1[hp], a["w1_T"].rearrange("e d f -> d e f")).then_inc(s["w"], 16)
                e.dma_start(w2[hp], a["w2_T"].rearrange("e d f -> d e f")).then_inc(s["w"], 16)
                e.dma_start(b1[hp], a["b1_T"]).then_inc(s["w"], 16)
                e.dma_start(b2[hp], a["b2_T"]).then_inc(s["w"], 16)
            row = lambda v: v.rearrange("(o d) -> o d", o=1)
            e.dma_start(sbias, row(a["L1_ffn_switch_b"]).to_broadcast([P, E])).then_inc(s["w"], 16)
            e.dma_start(b3, row(a["L1_ffn_b3"]).to_broadcast([P, DIM])).then_inc(s["w"], 16)
            e.dma_start(iota8, a["iota8"]).then_inc(s["w"], 16)
            e.dma_start(hmask, a["mask16"]).then_inc(s["w"], 16)
            e.dma_start(w3, a["w3_T"].rearrange("(k p) e -> p k e", p=P)).then_inc(s["w"], 16)

        def pe(e):
            ln_pe(e)
            e.wait_ge(s["part"], base["part"] + 1)
            nc.tensor.matmul(bank[2][:, 0:E], ones, part, start=True, stop=True).then_inc(s["lg"], 1)
            e.wait_ge(s["bd"], base["bd"] + 4)
            e.wait_ge(ln["xnT"], ln_base["xnT"] + TILES // 2)
            U = 2 * BLOCKS

            def second(u):
                if u >= 2:
                    e.wait_ge(s["z"], base["z"] + u - 1)
                for k in range(2):
                    e.wait_ge(s["g"], base["g"] + 2 * u + k + 1)
                    ins = nc.tensor.matmul(bank[4 + u % 2][:], bd[1][k], ht[(2 * u + k) % 4], start=(k == 0), stop=(k == 1))
                ins.then_inc(s["o"], 1)

            def final(blk):
                e.wait_ge(s["z"], base["z"] + 2 * blk + 2)
                for q in range(4):
                    t = 4 * blk + q
                    if t >= 2:
                        e.wait_ge(s["out"], base["out"] + t - 1)
                    for k in range(CHUNKS):
                        ins = nc.tensor.matmul(bank[6 + t % 2][:, 0:DIM], z[blk % 2][:, k, q * P:(q + 1) * P], w3[:, k, :],
                                               start=(k == 0), stop=(k == 1))
                    ins.then_inc(s["f"], 1)

            for u in range(U):
                blk, ch = u // 2, u % 2
                for k in range(2):
                    n = 2 * u + k
                    if n >= 4:
                        e.wait_ge(s["g"], base["g"] + n - 3)
                    nc.tensor.matmul(bank[n % 4][:], bd[0][k], xnT[:, ch, blk * BLOCK:(blk + 1) * BLOCK],
                                     start=True, stop=True).then_inc(s["h"], 1)
                if u >= 1:
                    second(u - 1)
                if u >= 3 and u % 2:
                    final(u // 2 - 1)
            second(U - 1)
            final(BLOCKS - 1)

        def act(e):
            ln_act(e)
            e.wait_ge(s["ein"], base["ein"] + 1)
            nc.scalar.activation(e8, e8, ACT.Exp).then_inc(s["ex"], 1)
            e.wait_ge(s["wb"], base["wb"] + 1)
            for n in range(4 * BLOCKS):
                e.wait_ge(s["h"], base["h"] + n + 1)
                if n >= 4:
                    e.wait_ge(s["o"], base["o"] + n // 2 - 1)
                nc.scalar.activation(ht[n % 4], bank[n % 4][:], ACT.Gelu, bias=bsel[:, n % 2:n % 2 + 1]).then_inc(s["g"], 1)

        def dve(v):
            link = chains["dve"]
            ln_dve(v)
            v.wait_ge(ln["xn"], ln_base["xn"] + TILES)
            link(nc.vector.memset(ones, 1.0))
            v.wait_ge(s["sw"], base["sw"] + 16 * E)
            for ex in range(E):
                ins = nc.vector.tensor_tensor_reduce(out=junk, in0=xn[:, 0:2, :], in1=sw[:, ex], scale=1.0, scalar=0.0,
                                                     op0=ALU.mult, op1=ALU.add, accum_out=part[:, ex:ex + 1])
                if ex < E - 1:
                    link(ins)
            ins.then_inc(s["part"], 1)
            v.wait_ge(s["w"], base["w"] + NW)
            v.wait_ge(s["lg"], base["lg"] + 1)
            link(nc.vector.tensor_tensor(logit, bank[2][:, 0:E], sbias, ALU.add))
            link(nc.vector.max(m8, logit))
            nc.vector.max_index(mi, m8, logit)
            nc.vector.tensor_scalar(e8, m8, m8[:, 0:1], None, ALU.subtract).then_inc(s["ein"], 1)
            v.wait_ge(s["ein"], base["ein"] + 1)
            link(nc.vector.tensor_copy(mif, mi))
            for k in range(2):
                ins = nc.vector.tensor_scalar(oh[:, k, :], iota8, mif[:, k:k + 1], None, ALU.is_equal)
            link(ins)
            v.wait_ge(s["ex"], base["ex"] + 1)
            link(nc.vector.tensor_reduce(esum, e8, AX_X, ALU.add))
            link(nc.vector.reciprocal(esum, esum))
            link(nc.vector.tensor_scalar(e8, e8, esum, None, ALU.mult))
            for k in range(2):
                ins = nc.vector.tensor_scalar(oh[:, 2 + k, :], oh[:, k, :], e8[:, k:k + 1], None, ALU.mult)
            link(ins)
            for k in range(4):
                w, b = (w1, b1) if k < 2 else (w2, b2)
                t3 = tmp.rearrange("p (e f) -> p e f", e=E)
                link(nc.vector.tensor_tensor(t3, w, oh[:, k, :].rearrange("p (e o) -> p e o", o=1).to_broadcast([P, E, HD]), ALU.mult))
                link(nc.vector.tensor_reduce(sel[:, k, :], tmp.rearrange("p (e f) -> p f e", e=E), AX_X, ALU.add))
                link(nc.vector.tensor_tensor(tmpb[:, k, :], b, oh[:, k, :], ALU.mult))
                link(nc.vector.tensor_reduce(bsel[:, k:k + 1], tmpb[:, k, :], AX_X, ALU.add))
            nc.vector.tensor_tensor(b2s, bsel[:, 2:3], bsel[:, 3:4], ALU.add).then_inc(s["wb"], 1)
            v.wait_ge(s["wb"], base["wb"] + 1)
            for k in range(4):
                nc.vector.tensor_tensor(bd[k // 2][k % 2].rearrange("p (h f) -> p h f", h=8),
                                        sel[:, k, :].rearrange("p (o f) -> p o f", o=1).to_broadcast([P, 8, HD]),
                                        hmask.rearrange("p (h o) -> p h o", o=1).to_broadcast([P, 8, HD]),
                                        ALU.mult).then_inc(s["bd"], 1)
            v.wait_ge(s["xb"], base["xb"] + 1)
            v.wait_ge(ln["xnT"], ln_base["xnT"] + TILES // 2)

            def outs(blk):
                for q in range(4):
                    t = 4 * blk + q
                    v.wait_ge(s["f"], base["f"] + t + 1)
                    nc.vector.scalar_tensor_tensor(out=x[:, t, :], in0=bank[6 + t % 2][:, 0:DIM], scalar=0.5, in1=x[:, t, :],
                                                   op0=ALU.mult, op1=ALU.add).then_inc(s["out"], 1)
                    out_stats(v, s["out"], base["out"], t)
            for u in range(2 * BLOCKS):
                blk, ch = u // 2, u % 2
                v.wait_ge(s["o"], base["o"] + u + 1)
                if blk >= 2 and ch == 0:
                    v.wait_ge(s["f"], base["f"] + 4 * (blk - 1))
                nc.vector.scalar_tensor_tensor(out=z[blk % 2][:, ch, :], in0=bank[4 + u % 2][:], scalar=b2s,
                                               in1=xnT[:, ch, blk * BLOCK:(blk + 1) * BLOCK], op0=ALU.add, op1=ALU.add
                                               ).then_inc(s["z"], 1)
                if u >= 2 and u % 2 == 0:
                    outs(u // 2 - 1)
            outs(BLOCKS - 1)

        def pool(e):
            link = chains["pool"]
            e.wait_ge(ln["xn"], ln_base["xn"] + TILES)
            e.wait_ge(s["w"], base["w"] + NW)
            link(nc.gpsimd.tensor_scalar(b3, b3, 0.5, None, ALU.mult))
            nc.gpsimd.tensor_tensor(x[:], x[:], b3.rearrange("p (o d) -> p o d", o=1).to_broadcast([P, TILES, DIM]),
                                    ALU.add).then_inc(s["xb"], 1)

        return (s["out"], base["out"] + TILES), dict(sync=sync, tensor=pe, scalar=act, vector=dve, gpsimd=pool)
    q_dram = dram("q_parts", [3, DIM, TOKENS], BF16)
    k_dram = dram("k_parts", [3, DIM, TOKENS], BF16)
    v_dram = dram("v_ones", [P, HGROUPS * TILES, HPG * 2 * HD])

    def softmax_attention(tag, s_ready, n_ready, have_stats):
        (ln, ln_base), ln_dve, ln_act, ln_pe = layer_norm(s_ready, n_ready, have_stats)
        s = sems(tag, "w wg qk v va rm ra kf kfT kft mem memo comb gex split part2 part3 exk kmax qkd "
                 "vd onesr st exp pv raw mx mxd nm nmt nms mrow rt rc cadd ot oT pj out")
        s_ld = [sem(f"{tag}_step{b}") for b in range(3)]
        VW = 2 * HD
        MW = HD + 1
        c = Carve()
        wqk = c(2 * CHUNKS * DIM).rearrange("p (w k e) -> p w k e", w=2, k=CHUNKS)
        wv = c(CHUNKS * DIM).rearrange("p (k e) -> p k e", k=CHUNKS)
        cs = c(2 * TOKENS).rearrange("p (w n) -> p w n", w=2)
        va = c(TILES * HEADS * VW).rearrange("p (t h n) -> p t h n", t=TILES, h=HEADS)
        qk = [c(CHUNKS * TOKENS).rearrange("p (c n) -> p c n", c=CHUNKS) for _ in range(2)]
        rope = [c(4 * BLOCK).rearrange("p (u n) -> p u n", u=4) for _ in range(2)]
        parts = [c(CHUNKS * TOKENS // 2, BF16).rearrange("p (c n) -> p c n", c=CHUNKS) for _ in range(3)]
        end = c.at
        res = cs
        kfT = c(TILES * DIM).rearrange("p (t d) -> p t d", t=TILES)
        feat = rope[0]
        memb = c(CHUNKS * 8 * MW).rearrange("p (c h n) -> p c h n", c=CHUNKS, h=8)
        c = Carve()
        KS = [c(HPG * TOKENS // 2, BF16).rearrange("p (h n) -> p h n", h=HPG) for _ in range(3)]
        QS = [c(HPG * BLOCK // 2, BF16).rearrange("p (h n) -> p h n", h=HPG) for _ in range(3)]
        VS = [c(TILES * HPG * VW).rearrange("p (t n) -> p t n", t=TILES) for _ in range(3)]
        PT = [c(HPG * BLOCK).rearrange("p (h n) -> p h n", h=HPG) for _ in range(2)]
        raw = xnT[:].rearrange("p c n -> p (c n)")
        raw = c(STEPS * BLOCK).rearrange("p (s n) -> p s n", s=STEPS)
        mx = c(16 * 4).rearrange("p (i k) -> p i k", i=16)
        m16, mr, mr2 = c(16), c(16), c(16)
        nmx = c(P // 2, BF16)
        nm3 = nmx[:, 0:48].rearrange("p (r i) -> p r i", r=3)
        nmT = c(P // 2, BF16, parts=48)
        assert c.at <= AREA - 2000
        c.at = AREA - 2000
        hmask, gate, gexp, gp, omg = c(8), c(HEADS), c(HEADS), c(HEADS), c(HEADS)
        den = [c(HEADS) for _ in range(2)]
        wo = c(CHUNKS * DIM).rearrange("p (k e) -> p k e", k=CHUNKS)
        oT = [c(DIM).rearrange("p (c n) -> p c n", c=2) for _ in range(2)]
        tmp = [c(DIM).rearrange("p (t n) -> p t n", t=16) for _ in range(1)]
        comb = xn

        def sync(e):
            e.wait_ge(s_ready, n_ready)
            for w, name in enumerate(("Wq_T", "Wk_T")):
                e.dma_start(wqk[:, w], a[name].rearrange("(k p) e -> p k e", p=P)).then_inc(s["w"], 16)
            e.dma_start(wv, a["Wv_T"].rearrange("(k p) e -> p k e", p=P)).then_inc(s["w"], 16)
            e.dma_start(cs, a["rope"].rearrange("w p n -> p w n")).then_inc(s["w"], 16)
            e.dma_start(gate, a["L1_attn_gate"].rearrange("a h b c -> a (h b c)").to_broadcast([P, HEADS])).then_inc(s["wg"], 16)
            e.dma_start(hmask, a["mask16"]).then_inc(s["wg"], 16)
            e.dma_start(wo, a["Wo_T"].rearrange("(k p) e -> p k e", p=P)).then_inc(s["wg"], 16)
            e.wait_ge(s["va"], TILES)
            e.wait_ge(s["onesr"], 1)
            for g in range(HGROUPS):
                e.dma_start(v_dram[:, TILES * g:TILES * (g + 1), :],
                            va[:, :, HPG * g:HPG * (g + 1), :].rearrange("p t h n -> p t (h n)")).then_inc(s["vd"], 16)
            for w, d in enumerate((q_dram, k_dram)):
                for r, need in ((0, "split"), (1, "part2"), (2, "part3")):
                    e.wait_ge(s[need], w + 1)
                    e.dma_start(d[r].rearrange("(c p) n -> p c n", p=P), parts[r]).then_inc(s["qkd"], 16)
                e.wait_ge(s["qkd"], 48 * (w + 1))
            e.wait_ge(s["vd"], 16 * HGROUPS)

            def load(b, st):
                g, q = st // BLOCKS, st % BLOCKS
                rows, col, tile = g * HPG * HD, q * BLOCK, g * TILES
                for d, dst, ps, cols in ((q_dram, QS[b], Q_PARTS, bass.ds(col, BLOCK)),
                                         (k_dram, KS[b], K_PARTS, slice(0, TOKENS))):
                    for i, part in enumerate(ps):
                        src = d[part, bass.ds(rows, HPG * HD), cols].rearrange("(h r) n -> r h n", r=HD)
                        e.dma_start(dst[HD * i:HD * (i + 1)], src).then_inc(s_ld[b], 16)
                e.dma_start(VS[b], v_dram[:, bass.ds(tile, TILES), :]).then_inc(s_ld[b], 16)

            def store_max(b, st):
                e.wait_ge(s["nms"], st + 1)
                e.dma_start(QS[b][STACK:STACK_M].rearrange("r h n -> r (h n)").rearrange("r (i n) -> r i n", n=P),
                            nmT).then_inc(s["mrow"], 16)

            e.wait_ge(s["memo"], TILES)
            e.wait_ge(s["comb"], TILES)
            for b in range(3):
                load(b, b)
            store_max(0, 0)
            for st in range(STEPS - 1):
                store_max((st + 1) % 3, st + 1)
                if st + 3 < STEPS:
                    e.wait_ge(s["pv"], (st + 1) * 16)
                    load(st % 3, st + 3)

        def pe(e):
            ln_pe(e)
            e.wait_ge(s["w"], 64)
            e.wait_ge(ln["xnT"], ln_base["xnT"] + TILES // 2)
            for t in range(TILES):
                if t >= 2:
                    e.wait_ge(s["va"], t - 1)
                for k in range(CHUNKS):
                    ins = nc.tensor.matmul(bank[6 + t % 2][:, 0:DIM], xnT[:, k, t * P:(t + 1) * P], wv[:, k], start=(k == 0), stop=(k == 1))
                ins.then_inc(s["v"], 1)
                if t % 2 == 0:
                    n = t // 2
                    w, blk = n // BLOCKS, n % BLOCKS
                    if n >= 2:
                        e.wait_ge(s["rm"], n - 1)
                    for ch in range(CHUNKS):
                        for k in range(CHUNKS):
                            ins = nc.tensor.matmul(bank[2 + 2 * (n % 2) + ch][:], wqk[:, w, k, ch * P:(ch + 1) * P],
                                                   xnT[:, k, blk * BLOCK:(blk + 1) * BLOCK], start=(k == 0), stop=(k == 1))
                    ins.then_inc(s["qk"], 1)
            e.wait_ge(s["kf"], 2)
            for t in range(TILES):
                if t >= 2:
                    e.wait_ge(s["kfT"], t - 1)
                for ch in range(CHUNKS):
                    ins = nc.tensor.transpose(bank[t % 2][:, ch * P:(ch + 1) * P], qk[1][:, ch, t * P:(t + 1) * P], ident[:])
                ins.then_inc(s["kft"], 1)
            e.wait_ge(s["rm"], 2 * BLOCKS)
            for t in range(TILES):
                e.wait_ge(s["kfT"], t + 1)
                for ch in range(CHUNKS):
                    ins = nc.tensor.matmul(bank[4 + ch][:, 0:8 * MW], kfT[:, t, ch * P:(ch + 1) * P], va[:, t, 8 * ch:8 * ch + 8, 0:MW],
                                           start=(t == 0), stop=(t == TILES - 1))
            ins.then_inc(s["mem"], 1)
            e.wait_ge(s["kf"], 4)
            e.wait_ge(s["mem"], 2)
            for t in range(TILES):
                if t >= 2:
                    e.wait_ge(s["comb"], t - 1)
                else:
                    e.wait_ge(s["va"], TILES)
                for ch in range(CHUNKS):
                    ins = nc.tensor.matmul(bank[6 + t % 2][:, ch * 8 * MW:(ch + 1) * 8 * MW], qk[0][:, ch, t * P:(t + 1) * P],
                                           memb[:, ch], start=True, stop=True)
                ins.then_inc(s["memo"], 1)
            e.wait_ge(s["comb"], TILES)

            def max_scores(b, m, j):
                h, qt, kc = j // 16, j // 4 % 4, j % 4
                if j == 0:
                    e.wait_ge(s_ld[b], 208 * (m // 3 + 1) if isinstance(m, int) else turn_of(b))
                if j == EARLY and not (isinstance(m, int) and m == 0):
                    e.wait_ge(s["nms"], m)
                elif not (isinstance(m, int) and m == 0 and j < 3):
                    e.wait_ge(s["mxd"], m * 64 + (j - 2))
                nc.tensor.matmul(bank[5 + (b + j) % 3], QS[b][0:STACK, h, qt * P:(qt + 1) * P],
                                 KS[b][0:STACK, h, kc * BLOCK:(kc + 1) * BLOCK], start=True, stop=True).then_inc(s["mx"], 1)

            def max_rows(b, m):
                e.wait_ge(s["nm"], m + 1)
                if not (isinstance(m, int) and m == STEPS - 1):
                    e.wait_ge(s["mxd"], (m + 1) * 64 + (EARLY - 2))
                nc.tensor.transpose(bank[5 + (b + 1 + EARLY) % 3].bitcast(BF16)[:, 0:P], nmx, ident_bf[:]).then_inc(s["nmt"], 1)

            turn = [None]

            def turn_of(b):
                return (turn[0] + (1 if b == 2 else 2)) * 208

            def step(b, st):
                static = isinstance(st, int)
                ahead = [(st + 1, (b + 1) % 3, 16 + i) for i in range(48)] + [(st + 2, (b + 2) % 3, i) for i in range(16)]
                if static:
                    ahead = [w if w[0] < STEPS else None for w in ahead]

                def maxima(n):
                    for _ in range(n):
                        if w := ahead.pop(0):
                            max_scores(w[1], w[0], w[2])

                e.wait_ge(s["mrow"], (st + 1) * 16)
                for kt in range(TILES + 1):
                    if kt == 14 and not (static and st + 1 >= STEPS):
                        max_rows((b + 1) % 3, st + 1)
                    for pair in range(2):
                        if kt < TILES:
                            e.wait_ge(s["exp"], st * 32 + (2 * kt + pair + 1))
                            for h in (2 * pair, 2 * pair + 1):
                                ins = nc.tensor.matmul(bank[h], KS[b][0:STACK_M, h, kt * P:(kt + 1) * P],
                                                       QS[b][0:STACK_M, h, :], start=True, stop=True)
                            ins.then_inc(s["st"], 1)
                            maxima(2 - pair)
                    if kt >= 1:
                        if kt == 1:
                            e.wait_ge(s["raw"], st + 1)
                        e.wait_ge(s["exp"], st * 32 + (2 * kt + 2))
                        for h in range(HPG):
                            ins = nc.tensor.matmul(bank[4][VW * h:VW * (h + 1), :], VS[b][:, kt - 1, VW * h:VW * (h + 1)],
                                                   PT[(kt - 1) % 2][:, h, :], start=(kt == 1), stop=(kt == TILES))
                        ins.then_inc(s["pv"], 1)
                    if kt < TILES:
                        maxima(1)

            e.wait_ge(s["onesr"], 2)
            for j in range(64):
                max_scores(0, 0, j)
            for j in range(16):
                if j == EARLY:
                    max_rows(0, 0)
                max_scores(1, 1, j)
            with e.Fori(0, 4) as i:
                turn[0] = i
                for b in range(3):
                    step(b, i * 3 + b)
            for st in range(12, STEPS):
                step(st % 3, st)

            for st in range(STEPS):
                if st == 0:
                    e.wait_ge(s["exp"], 2 + 32 * STEPS)
                if st >= 2:
                    e.wait_ge(s["rc"], st - 1)
                e.wait_ge(s["raw"], st + 2)
                for q in range(4):
                    ins = nc.tensor.transpose(bank[st % 2][:, q * P:(q + 1) * P], raw[:, st, q * P:(q + 1) * P], ident[:])
                ins.then_inc(s["rt"], 1)
            e.wait_ge(s["cadd"], STEPS)
            e.wait_ge(s["wg"], 48)
            for t in range(TILES):
                if t >= 2:
                    e.wait_ge(s["oT"], t - 1)
                for ch in range(CHUNKS):
                    ins = nc.tensor.transpose(bank[2 + t % 2][:, ch * P:(ch + 1) * P], comb[:, t, ch * P:(ch + 1) * P], ident[:])
                ins.then_inc(s["ot"], 1)
                e.wait_ge(s["oT"], t + 1)
                if t >= 2:
                    e.wait_ge(s["out"], t - 1)
                for ch in range(CHUNKS):
                    ins = nc.tensor.matmul(bank[6 + t % 2][:, 0:DIM], oT[t % 2][:, ch], wo[:, ch], start=(ch == 0), stop=(ch == 1))
                ins.then_inc(s["pj"], 1)

        def act(e):
            ln_act(e)
            for t in range(TILES):
                e.wait_ge(s["v"], t + 1)
                nc.scalar.copy(va[:, t, :, 0:HD], bank[6 + t % 2][:, 0:DIM].rearrange("p (h n) -> p h n", h=HEADS)).then_inc(s["va"], 1)
            for w in range(2):
                e.wait_ge(s["ra"], BLOCKS * (w + 1))
                if w:
                    e.wait_ge(s["qkd"], 48)
                nc.scalar.activation(parts[0], qk[w], ACT.Copy, scale=(0.25 if w == 0 else 1.0)).then_inc(s["split"], 1)
                e.wait_ge(s["exk"], w + 1)
                nc.scalar.copy(parts[1], res).then_inc(s["part2"], 1)
            for n, w in enumerate((1, 0)):
                for ch in range(CHUNKS):
                    i = 2 * n + ch
                    if i >= 1:
                        e.wait_ge(s["kf"], i)
                    else:
                        e.wait_ge(s["part3"], 2)
                    nc.scalar.activation(feat, qk[w][:, ch, :].rearrange("p (u n) -> p u n", u=4), ACT.Exp).then_inc(s["kmax"], 1)
                if n == 0:
                    for t in range(TILES):
                        e.wait_ge(s["kft"], t + 1)
                        nc.scalar.copy(kfT[:, t, :], bank[t % 2][:, 0:DIM]).then_inc(s["kfT"], 1)
            e.wait_ge(s["wg"], 48)
            nc.scalar.activation(gexp, gate, ACT.Exp, scale=-1.0).then_inc(s["gex"], 1)
            e.wait_ge(s["gex"], 1)
            nc.scalar.copy(tmp[0][:, 0, 0:1], gexp[:, 0:1]).then_inc(s["exp"], 2)
            nc.scalar.copy(tmp[0][:, 1, 0:1], gexp[:, 0:1]).then_inc(s["raw"], 1)

            def step(st):
                for kt in range(TILES):
                    for pair in range(2):
                        e.wait_ge(s["st"], st * 32 + (2 * kt + pair + 1))
                        nc.scalar.activation(PT[kt % 2][:, 2 * pair:2 * pair + 2, :],
                                             psum[:, 2 * pair * 512:(2 * pair + 2) * 512].rearrange("p (h n) -> p h n", h=2),
                                             ACT.Exp).then_inc(s["exp"], 1)
                e.wait_ge(s["pv"], st * 16 + 16)
                nc.scalar.copy(raw[:, st, :] if isinstance(st, int) else raw[:, bass.ds(st, 1), :].rearrange("p s n -> p (s n)"),
                               bank[4][:]).then_inc(s["raw"], 1)

            with e.Fori(0, STEPS) as st:
                step(st)
            for t in range(TILES):
                e.wait_ge(s["ot"], t + 1)
                if t >= 2:
                    e.wait_ge(s["pj"], t - 1)
                nc.scalar.copy(oT[t % 2], bank[2 + t % 2][:, 0:DIM].rearrange("p (c n) -> p c n", c=2)).then_inc(s["oT"], 1)

        def dve(v):
            link = chains["dve"]
            ln_dve(v)
            v.wait_ge(s["w"], 64)
            for n in range(2 * BLOCKS):
                blk = n % BLOCKS
                v.wait_ge(s["qk"], n + 1)
                if n >= 2:
                    v.wait_ge(s["ra"], n - 1)
                cols = slice(blk * BLOCK, (blk + 1) * BLOCK)
                for u, (ch, w) in enumerate(((0, 0), (1, 1), (1, 0), (0, 1))):
                    ins = nc.vector.tensor_tensor(rope[n % 2][:, u, :], bank[2 + 2 * (n % 2) + ch][:], cs[:, w, cols], ALU.mult)
                ins.then_inc(s["rm"], 1)
            v.wait_ge(s["ra"], 2 * BLOCKS)
            for w in range(2):
                v.wait_ge(s["split"], w + 1)
                nc.vector.scalar_tensor_tensor(out=res, in0=qk[w], scalar=(0.25 if w == 0 else 1.0), in1=parts[0],
                                               op0=ALU.mult, op1=ALU.subtract).then_inc(s["exk"], 1)
                v.wait_ge(s["part2"], w + 1)
                nc.vector.tensor_tensor(parts[2], res, parts[1], ALU.subtract).then_inc(s["part3"], 1)
            v.wait_ge(s["part3"], 2)
            for i in range(4):
                w, ch = 1 - i // 2, i % 2
                if i == 2:
                    memory_mask(v)
                v.wait_ge(s["kmax"], i + 1)
                f = qk[w][:, ch, :]
                link(nc.vector.tensor_scalar(f, f, 0.0, None, ALU.max))
                nc.vector.scalar_tensor_tensor(out=f, in0=feat.rearrange("p u n -> p (u n)"), scalar=1.0, in1=f,
                                               op0=ALU.min, op1=ALU.add).then_inc(s["kf"], 1)
            v.wait_ge(s["gex"], 1)
            link(nc.vector.tensor_scalar(gp, gexp, 1.0, None, ALU.add))
            link(nc.vector.reciprocal(gp, gp))
            link(nc.vector.tensor_scalar(omg, gp, -1.0, 1.0, ALU.mult, ALU.add))
            for t in range(TILES):
                v.wait_ge(s["memo"], t + 1)
                o = bank[6 + t % 2][:, 0:HEADS * MW].rearrange("p (h n) -> p h n", h=HEADS)
                link(nc.vector.reciprocal(den[t % 2], o[:, :, HD]))
                link(nc.vector.tensor_tensor(den[t % 2], den[t % 2], gp, ALU.mult))
                nc.vector.tensor_tensor(comb[:, t, :].rearrange("p (h n) -> p h n", h=HEADS), o[:, :, 0:HD],
                                        den[t % 2].rearrange("p (h o) -> p h o", o=1).to_broadcast([P, HEADS, HD]),
                                        ALU.mult).then_inc(s["comb"], 1)
            v.wait_ge(s["comb"], TILES)
            v.wait_ge(s["qkd"], 96)
            v.wait_ge(s["vd"], 16 * HGROUPS)
            nc.vector.memset(nmx, 0.0)
            for b in range(3):
                ins = nc.vector.memset(KS[b][STACK:STACK_M], 1.0)
            ins.then_inc(s["onesr"], 1)

            def maxima(m, js, r):
                for j in js:
                    v.wait_ge(s["mx"], m * 64 + (j + 1))
                    nc.vector.tensor_reduce(mx[:, j // 4, j % 4:j % 4 + 1], bank[5 + (r + j) % 3], AX_X, ALU.max).then_inc(s["mxd"], 1)

            def negated(m):
                v.wait_ge(s["mxd"], m * 64 + 64)
                link(nc.vector.tensor_reduce(m16, mx, AX_X, ALU.max))
                link(nc.vector.tensor_scalar(nm3[:, 0, :], m16, -1.0, None, ALU.mult))
                link(nc.vector.scalar_tensor_tensor(out=mr, in0=m16, scalar=-1.0, in1=nm3[:, 0, :], op0=ALU.mult, op1=ALU.subtract))
                link(nc.vector.tensor_copy(nm3[:, 1, :], mr))
                link(nc.vector.tensor_tensor(mr2, mr, nm3[:, 1, :], ALU.subtract))
                nc.vector.tensor_copy(nm3[:, 2, :], mr2).then_inc(s["nm"], 1)

            def rows(m, r):
                v.wait_ge(s["nmt"], m + 1)
                if not (isinstance(m, int) and m == 0):
                    v.wait_ge(s["mrow"], m * 16)
                nc.vector.tensor_copy(nmT, bank[5 + (r + 1 + EARLY) % 3].bitcast(BF16)[0:48, 0:P]).then_inc(s["nms"], 1)

            def turn(m, r):
                maxima(m, range(EARLY if r else 0, 64), r % 3)
                negated(m)
                maxima(m + 1, range(EARLY), (r + 1) % 3)
                rows(m, r % 3)

            turn(0, 0)
            with v.Fori(0, 4) as i:
                link.enter(i, 15)
                for r in (1, 2, 3):
                    turn(i * 3 + r, r)
                link.leave(4)
            for m in (13, 14):
                turn(m, m)
            maxima(STEPS - 1, range(EARLY, 64), (STEPS - 1) % 3)
            negated(STEPS - 1)
            rows(STEPS - 1, (STEPS - 1) % 3)
            for st in range(STEPS):
                g, qb = st // BLOCKS, st % BLOCKS
                v.wait_ge(s["rt"], st + 1)
                o = bank[st % 2][:].rearrange("p (q h n) -> p q h n", q=4, h=HPG)
                d = den[st % 2].rearrange("p (q h) -> p q h", q=4)
                if st >= 1:
                    v.wait_ge(s["cadd"], st)
                link(nc.vector.reciprocal(d, o[:, :, :, HD]))
                link(nc.vector.tensor_tensor(d, d, omg[:, HPG * g:HPG * (g + 1)].rearrange("p (o h) -> p o h", o=1).to_broadcast([P, 4, HPG]), ALU.mult))
                t4 = tmp[0].rearrange("p (q h) n -> p q h n", q=4)
                for q in range(4):
                    ins = nc.vector.tensor_tensor(t4[:, q], o[:, q, :, 0:HD],
                                                  d[:, q, :].rearrange("p (h o) -> p h o", o=1).to_broadcast([P, HPG, HD]), ALU.mult)
                ins.then_inc(s["rc"], 1)
                v.wait_ge(s["rc"], st + 1)
                cv = comb[:, 4 * qb:4 * qb + 4, HPG * HD * g:HPG * HD * (g + 1)]
                nc.vector.tensor_tensor(cv, cv, tmp[0].rearrange("p (q h) n -> p q (h n)", q=4), ALU.add).then_inc(s["cadd"], 1)
            for t in range(TILES):
                v.wait_ge(s["pj"], t + 1)
                nc.vector.tensor_tensor(x[:, t, :], bank[6 + t % 2][:, 0:DIM], x[:, t, :], ALU.add).then_inc(s["out"], 1)
                out_stats(v, s["out"], 0, t)

        def memory_mask(v):
            v.wait_ge(s["mem"], 1)
            v.wait_ge(s["wg"], 48)
            for ch in range(CHUNKS):
                ins = nc.vector.tensor_tensor(memb[:, ch], bank[4 + ch][:, 0:8 * MW].rearrange("p (h n) -> p h n", h=8),
                                              hmask.rearrange("p (h o) -> p h o", o=1).to_broadcast([P, 8, MW]), ALU.mult)
            ins.then_inc(s["mem"], 1)

        def pool(e):
            e.wait_ge(s["w"], 64)
            e.wait_ge(s_ready, n_ready)
            nc.gpsimd.memset(va[:, :, :, HD:VW], 1.0).then_inc(s["onesr"], 1)
            for n in range(2 * BLOCKS):
                w, blk = n // BLOCKS, n % BLOCKS
                cols = slice(blk * BLOCK, (blk + 1) * BLOCK)
                e.wait_ge(s["rm"], n + 1)
                r = rope[n % 2]
                nc.gpsimd.tensor_tensor(qk[w][:, 0, cols], r[:, 0, :], r[:, 1, :], ALU.subtract)
                nc.gpsimd.tensor_tensor(qk[w][:, 1, cols], r[:, 2, :], r[:, 3, :], ALU.add).then_inc(s["ra"], 1)

        return (s["out"], TILES), dict(sync=sync, tensor=pe, scalar=act, vector=dve, gpsimd=pool)

    layers = []
    ready, have_stats = (s_x, 16), False
    makers = [moe, linear_attention, moe, head_mixer, softmax_attention, head_mixer]
    from_ = [m for m in makers]
    for n, mk in enumerate(from_[:stages]):
        ready, progs = mk(f"l{n}", *ready, have_stats)
        have_stats = mk is not moe
        layers.append(progs)

    block = ctx.enter_context(nc.Block())
    s_out = sem("stored")

    @block.sync
    def _(e):
        e.dma_start(x[:], a["L0_attn_x"][0].rearrange("(t p) d -> p t d", p=P)).then_inc(s_x, 16)
        e.dma_start(ident[:], a["ident"]).then_inc(s_const, 16)
        for pr in layers:
            if "sync" in pr:
                pr["sync"](e)
        e.wait_ge(*ready)
        e.dma_start(out[0].rearrange("(t p) d -> p t d", p=P), x[:]).then_inc(s_out, 16)
        e.wait_ge(s_out, 16)

    @block.tensor
    def _(e):
        e.wait_ge(s_const, 16)
        e.wait_ge(s_const2, 1)
        for pr in layers:
            pr["tensor"](e)

    @block.scalar
    def _(e):
        chains["act"] = Chain(e, chain_sems["act"])
        for pr in layers:
            pr["scalar"](e)

    @block.vector
    def _(e):
        chains["dve"] = Chain(e, chain_sems["dve"])
        e.wait_ge(s_const, 16)
        nc.vector.tensor_copy(ident_bf[:], ident[:]).then_inc(s_const2, 1)
        for pr in layers:
            pr["vector"](e)

    @block.gpsimd
    def _(e):
        chains["pool"] = Chain(e, chain_sems["pool"])
        for pr in layers:
            if "gpsimd" in pr:
                pr["gpsimd"](e)


def constants():
    f = np.float32
    c = {}
    c["ident"] = np.eye(P, dtype=f)
    c["iota_row"] = np.tile(TOKENS - np.arange(TOKENS // 2, dtype=f), (P, 1))
    c["key_off"] = np.where(np.arange(P) < EXPERTS, 0, -TOKENS // 2).astype(f).reshape(P, 1)
    c["iota_bf"] = np.tile(np.arange(P, dtype=f), (P, 1)).astype(mybir.dt.np(BF16))
    c["tile_off"] = np.tile(P * np.arange(TILES + 1, dtype=f), (P, 1))
    c["pair_starts"] = (2 * P * np.arange(TILES // 2, dtype=f)).reshape(1, -1)
    c["mask32"] = (np.arange(P)[:, None] // LHD == np.arange(P // LHD)[None, :]).astype(f)
    c["mask16"] = (np.arange(P)[:, None] // HD == np.arange(P // HD)[None, :]).astype(f)
    c["iota8"] = np.tile(np.arange(MIX_EXPERTS, dtype=f), (P, 1))
    inv = (1.0 / np.float32(10000.0) ** (np.arange(0, DIM, 2, dtype=f) / f(DIM))).astype(f)
    angle = (np.arange(TOKENS, dtype=f)[None, :] * inv[:, None]).astype(f).astype(np.float64)
    c["rope"] = np.stack([np.cos(angle), np.sin(angle)]).astype(f)
    c["slot_mask"] = (np.arange(P)[:, None] // CAP == np.arange(EPG)[None, :]).astype(f)
    return c


def host_arrays(inputs):
    t = lambda w: np.ascontiguousarray(np.swapaxes(w, -1, -2))
    d = {k: np.asarray(v) for k, v in inputs.items()}
    d["gate_T"] = t(d.pop("L0_ffn_gate_w"))
    qkv = d.pop("L0_attn_w_qkv")
    d["wq_T"], d["wkv_T"] = t(qkv[:DIM]), t(qkv[DIM:])
    d["wproj_T"] = t(d.pop("L0_attn_w_proj"))
    for w in ("Wq", "Wk", "Wv", "Wo"):
        d[w + "_T"] = t(d.pop("L1_attn_" + w))
    d["w3_T"] = t(d.pop("L1_ffn_w3"))
    d["w1_T"], d["w2_T"] = t(d.pop("L1_ffn_w1")), t(d.pop("L1_ffn_w2"))
    d["b1_T"], d["b2_T"] = t(d.pop("L1_ffn_b1")), t(d.pop("L1_ffn_b2"))
    d.update(constants())
    return d


def kernel(stages=6, **inputs):
    import concourse.bacc as _bacc
    from concourse.bass_utils import run_bass_kernel_spmd as _run

    nc = _bacc.Bacc("TRN2", target_bir_lowering=False, num_devices=1)
    arrays, a = {}, {}
    for name, v in host_arrays(inputs).items():
        arrays[f"in_{name}"] = v
        a[name] = nc.dram_tensor(f"in_{name}", v.shape, mybir.dt.from_np(v.dtype), kind="ExternalInput").ap()
    out = nc.dram_tensor("out_0", (1, TOKENS, DIM), F32, kind="ExternalOutput").ap()
    build(nc, a, out, stages)
    r = _run(nc, [arrays], core_ids=[0])
    return r.results[0]["out_0"]
```

```python
from contextlib import ExitStack

import numpy as np

import concourse.bass as bass
from concourse import mybir

F32 = mybir.dt.float32
BF16 = mybir.dt.bfloat16
U32 = mybir.dt.uint32
ACT = mybir.ActivationFunctionType
ALU = mybir.AluOpType
AX_X = mybir.AxisListType.X

P = 128
TOKENS = 2048
DIM = 256
TILES = TOKENS // P
CHUNKS = DIM // P
EPS = 1e-5
RSQRT_BITS = float(0x5F3759DF)
NEWTON = 3
STORES = [(0, 8), (8, 12), (12, 14), (14, TILES)]

EXPERTS = 64
TOPK = 6
UPFRONT = 6
PIECES = [None, None, ("down", 2), ("down", 3), ("up", 8), ("down", 4), ("down", 5),
          ("up", 9), ("up", 10), None, None, ("up", 11), ("down", 6), ("down", 7)]
CAP = 32
INNER = 176
HALF = INNER // 2
SHARED = 2 * INNER
EPG = P // CAP
GROUPS = EXPERTS // EPG
ROW = DIM + EXPERTS
SHARED_CHUNKS = [(0, 128), (128, 128), (256, 96)]
BIG = 3.0e38
WBUFS = 4
GATHERS = [(0, 1), (1, 4), (4, 8), (8, 16)]

LHEADS, LHD = 8, 32
MIX_EXPERTS = 8
HEADS, HD = 16, 16
BLOCK = 512
BLOCKS = TOKENS // BLOCK
HPG = 4
HGROUPS = HEADS // HPG
STEPS = HGROUPS * BLOCKS
STEP_OPERANDS = 3 * (HPG * TOKENS // 2 + HPG * BLOCK // 2 + (TOKENS // P) * HPG * 2 * HD)
STACK = 6 * HD
STACK_M = STACK + 3
EARLY = 8
Q_PARTS = [0, 0, 1, 1, 0, 2]
K_PARTS = [0, 1, 0, 1, 2, 0]
FEAT = 2
LATE_FACTORS = (2, 8)
KEYS_AT = 18
RECALL_AT = 54


class Chain:

    def __init__(self, eng, sem):
        self.eng, self.sem, self.n, self.turn = eng, sem, 0, None

    def at(self):
        return self.n if self.turn is None else self.n + self.turn[0] * self.turn[1]

    def __call__(self, ins):
        ins.then_inc(self.sem, 1)
        self.n += 1
        self.eng.wait_ge(self.sem, self.at())

    def enter(self, i, per):
        self.turn, self.start = (i, per), self.n

    def leave(self, trips):
        per = self.turn[1]
        assert self.n - self.start == per, (self.n - self.start, per)
        self.turn, self.n = None, self.start + per * trips


def build(nc, a, out, stages=6):
    ctx = ExitStack()
    with ctx:
        _program(nc, ctx, a, out, stages)


def _program(nc, ctx, a, out, stages):
    def sem(name):
        return ctx.enter_context(nc.semaphore(name))

    def sems(tag, names):
        return {n: sem(f"{tag}_{n}") for n in names.split()}

    made, calls = {}, {}

    def shared_sems(kind, totals):
        if kind not in made:
            made[kind] = sems(kind, " ".join(totals))
        n = calls[kind] = calls.get(kind, -1) + 1
        return made[kind], {k: n * v for k, v in totals.items()}

    def sb(name, shape, dt=F32):
        return ctx.enter_context(nc.sbuf_tensor(name, shape, dt))

    def dram(name, shape, dt=F32):
        return nc.dram_tensor(name, shape, dt, kind="Internal").ap()

    x = sb("x_res", [P, TILES, DIM])
    xn = sb("xn", [P, TILES, DIM])
    xnT = sb("xnT", [P, CHUNKS, TOKENS])
    stats = sb("stats", [P, TILES, 6])
    mv = sb("mv", [P, TILES, 2])
    rstd = sb("rstd", [P, 4, TILES])
    ident = sb("ident_sb", [P, P])
    ident_bf = sb("ident_bf", [P, P], BF16)
    AREA = 39200
    area = sb("area", [P, AREA])
    psum = ctx.enter_context(nc.psum_tensor("psum", [P, 8 * 512], F32))
    bank = [psum[:, 512 * i:512 * (i + 1)] for i in range(8)]

    class Carve:
        def __init__(self):
            self.at = 0

        def __call__(self, words, dt=F32, parts=P):
            v = area[0:parts, self.at:self.at + words]
            self.at += words
            assert self.at <= AREA, self.at
            return v if dt is F32 else v.bitcast(dt)

    s_const = sem("const_loaded")
    s_const2 = sem("const_made")
    s_x = [sem(f"x_loaded{i}") for i in range(4)]
    chain_sems = {e: sem(f"chain_{e}") for e in ("dve", "act", "pool")}
    chains = {}

    followed = {}
    AHEAD = TILES - 2
    s_stats, s_agg, s_scale = sem("ln_stats"), sem("ln_agg"), sem("ln_scale")

    def statistics(lo, hi):
        for t in range(lo, hi):
            ins = nc.vector.bn_stats(stats[:, t, :], x[:, t, :])
        return ins

    def aggregates(lo, hi):
        for t in range(lo, hi):
            ins = nc.vector.bn_aggr(mv[:, t, :], stats[:, t, :])
        return ins

    def roots(eng, link, lo, hi, between=lambda: None):
        var, r, e1, e2 = (rstd[:, i, lo:hi] for i in range(4))

        def then(ins):
            between()
            link(ins)

        then(eng.tensor_scalar(var, mv[:, lo:hi, 1], EPS, None, ALU.add))
        then(eng.tensor_scalar(r.bitcast(U32), var.bitcast(U32), -0.5, RSQRT_BITS, ALU.mult, ALU.add))
        for _ in range(NEWTON):
            if eng is nc.vector:
                then(eng.scalar_tensor_tensor(out=e1, in0=r, scalar=-0.5, in1=r, op0=ALU.mult, op1=ALU.mult))
                then(eng.tensor_tensor(e2, e1, var, ALU.mult))
                then(eng.scalar_tensor_tensor(out=r, in0=e2, scalar=1.5, in1=r, op0=ALU.add, op1=ALU.mult))
                continue
            then(eng.tensor_tensor(e1, r, r, ALU.mult))
            then(eng.tensor_tensor(e2, e1, var, ALU.mult))
            then(eng.tensor_scalar(e1, e2, -0.5, 1.5, ALU.mult, ALU.add))
            then(eng.tensor_tensor(r, r, e1, ALU.mult))

    def layer_norm(s_ready, n_ready, before):
        s, base = shared_sems("ln", dict(xn=TILES, tr=TILES // 2, xnT=TILES // 2))
        turn = None if before in (None, "moe") else len(followed)

        def normed(lo, hi):
            for t in range(lo, hi):
                nc.vector.tensor_scalar(xn[:, t, :], x[:, t, :], mv[:, t, 0:1], rstd[:, 1, t:t + 1],
                                        ALU.subtract, ALU.mult).then_inc(s["xn"], 1)

        def normed_ahead(v, t):
            if t >= 12:
                v.wait_ge(s_scale, 2 * turn + 1)
                normed(2 * (t - 12), 2 * (t - 11))

        if turn is not None:
            followed[before] = (turn, normed_ahead)

        def pool(e):
            if turn is not None:
                for i, (lo, hi) in enumerate(((0, 8), (8, AHEAD))):
                    e.wait_ge(s_agg, turn * AHEAD + hi)
                    roots(nc.gpsimd, chains["pool"], lo, hi)
                    nc.gpsimd.memset(rstd[:, 2, lo:lo + 1], 0.0).then_inc(s_scale, 1)

        def dve(v):
            link = chains["dve"]
            v.wait_ge(s_ready, n_ready)

            if turn is not None:
                link(statistics(TILES - 1, TILES))
                link(aggregates(AHEAD, TILES))
                v.wait_ge(s_scale, 2 * turn + 2)
                left = iter(range(8, AHEAD))

                def norm_one():
                    t = next(left, None)
                    if t is not None:
                        normed(t, t + 1)
                roots(nc.vector, link, AHEAD, TILES, norm_one)
                normed(AHEAD, TILES)
                return
            if before is None:
                for i in range(4):
                    v.wait_ge(s_x[i], 16)
                    ins = statistics(4 * i, 4 * i + 4)
                link(ins)
            link(aggregates(0, TILES))
            roots(nc.vector, link, 0, TILES)
            normed(0, TILES)

        def act(e):
            for t2 in range(TILES // 2):
                e.wait_ge(s["tr"], base["tr"] + t2 + 1)
                nc.scalar.copy(xnT[:, :, 2 * P * t2:2 * P * (t2 + 1)].rearrange("p c (t n) -> p t c n", t=2),
                               bank[t2 % 2][:].rearrange("p (t c n) -> p t c n", t=2, c=CHUNKS)
                               ).then_inc(s["xnT"], 1)

        def pe(e):
            for t in range(TILES):
                e.wait_ge(s["xn"], base["xn"] + t + 1)
                if t % 2 == 0 and t >= 4:
                    e.wait_ge(s["xnT"], base["xnT"] + t // 2 - 1)
                for c in range(CHUNKS):
                    o = (t % 2) * 2 * P + c * P
                    ins = nc.tensor.transpose(bank[t // 2 % 2][:, o:o + P], xn[:, t, c * P:(c + 1) * P], ident[:])
                if t % 2:
                    ins.then_inc(s["tr"], 1)

        return (s, base), dve, act, pe, pool

    def out_stats(v, s_out, at, t, tag):
        if tag not in followed or t == 0:
            return
        turn, normed_ahead = followed[tag]
        v.wait_ge(s_out, at + t)
        nc.vector.bn_stats(stats[:, t - 1, :], x[:, t - 1, :]).then_inc(s_stats, 1)
        if t >= 2:
            v.wait_ge(s_stats, turn * (TILES - 1) + t - 1)
            nc.vector.bn_aggr(mv[:, t - 2, :], stats[:, t - 2, :]).then_inc(s_agg, 1)
        normed_ahead(v, t)

    table = dram("dispatch_table", [TOKENS + 1, ROW])
    slot_dram = dram("slot_tokens", [EXPERTS, CAP])

    def moe(tag, s_ready, n_ready, before):
        (ln, ln_base), ln_dve, ln_act, ln_pe, ln_pool = layer_norm(s_ready, n_ready, before)
        s, base = shared_sems("moe", dict(
            w=7 * 16, wsh=64, rows=32, halfin=16, tokrow=32, logit=4, shmm=12, mt=2, tokt=1, xgt=GROUPS, gu=GROUPS, ht=GROUPS,
            y=GROUPS, lgsb=5, exp=1, shg=12, shu=12, bufT=GROUPS, sg=GROUPS, hTsb=GROUPS, expin=1,
            msk=1, prob=2, key=2, half=1, tok=1, idx=1, h=GROUPS, out=1, hs=12, ysplit=GROUPS, yparts=GROUPS,
            xrow=16, sdm=8, sdx=8, seen=1, seent=1, pairs=1, **{f"gat{i}": 16 * (hi - lo) for i, (lo, hi) in enumerate(GATHERS)},
            **{f"wb{b}": 48 * GROUPS // WBUFS for b in range(WBUFS)}))
        sl = sems(tag, "oneh mix done")
        s_w = [s[f"wb{b}"] for b in range(WBUFS)]

        def gathered(g):
            i = [lo <= g < hi for lo, hi in GATHERS].index(True)
            return s[f"gat{i}"], base[f"gat{i}"] + 16 * (GATHERS[i][1] - GATHERS[i][0])

        c = Carve()
        gu_w = [c(EPG * CHUNKS * SHARED).rearrange("p (e k i) -> p e k i", e=EPG, k=CHUNKS) for _ in range(WBUFS)]
        dn_w = [c(EPG * 2 * DIM).rearrange("p (e k d) -> p e k d", e=EPG, k=2) for _ in range(WBUFS)]
        hsT = xn[:].rearrange("p t d -> p (t d)")[:, 0:6 * BLOCK].rearrange("p (b c n) -> p b c n", b=2, c=3)
        top = c.at
        lg = c(TILES * 66).rearrange("p (t e) -> p t e", t=TILES)
        rep = c(TILES * 66).rearrange("p (t e) -> p t e", t=TILES)
        msk = c(TILES * EXPERTS).rearrange("p (t h e) -> p t h e", t=TILES // 2, h=2)
        keyA = c(TOKENS // 2)
        keyB = c(TOKENS // 2)
        end = c.at
        c.at = top
        yp = c(3 * GROUPS * DIM // 2, BF16).rearrange("p (k g d) -> p k g d", k=3, g=GROUPS)
        c.at = max(c.at, end)
        top = c.at
        xg = c(GROUPS * ROW).rearrange("p (g r) -> p g r", g=GROUPS)
        end = c.at
        c.at = top
        prob = c(TILES * EXPERTS).rearrange("p (t e) -> p t e", t=TILES)
        assert c.at <= end
        c.at = end
        sg_sh = [xn[:].rearrange("p t d -> p (t d)")[:, (6 + i) * BLOCK:(7 + i) * BLOCK] for i in range(2)]
        su_sh = [c(BLOCK) for _ in range(2)]
        oneh = [xnT[:].rearrange("p c n -> p (c n)")[:, i * GROUPS * P // 2:(i + 1) * GROUPS * P // 2].bitcast(BF16)
                .rearrange("p (g n) -> p g n", g=GROUPS) for i in range(2)]
        bufT = [c(DIM).rearrange("p (k n) -> p k n", k=2) for _ in range(2)]
        sg = [c(INNER) for _ in range(2)]
        hh = [c(INNER) for _ in range(2)]
        hT = [c(DIM).rearrange("p (k n) -> p k n", k=2) for _ in range(2)]
        yres = [c(DIM) for _ in range(2)]
        gate = c(2 * P).rearrange("p (k e) -> p k e", k=2)
        sh_w = c(CHUNKS * 2 * SHARED).rearrange("p (k g i) -> p k g i", k=CHUNKS, g=2)
        sh_d = c(3 * DIM).rearrange("p (c d) -> p c d", c=3)
        v8 = c(TILES * 8).rearrange("p (t e) -> p t e", t=TILES)
        r8 = c(TILES * 8).rearrange("p (t e) -> p t e", t=TILES)
        esum = c(TILES)
        einv = c(TILES)
        top32 = c(64)
        best = c(CAP)
        bestB = c(64)
        tok = c(CAP)
        tokrow = c(P, parts=GROUPS)
        tokp = c(GROUPS)
        idx = c(GROUPS, U32)
        rel = c((TILES + 1) * GROUPS // 2, BF16).rearrange("p (t g) -> p t g", t=TILES + 1)
        seen = c(GROUPS)
        last = c(1)
        lastT, reached = c(1, parts=1), c(8, parts=1)
        thresh = c(8, parts=1)
        pairs = c(1, U32, parts=1)
        wsel = c(GROUPS)
        junk = c(EPG)
        iota_n = c(TOKENS // 2)
        iota_bf = c(P // 2, BF16)
        tile_off = c(TILES + 1)
        key_off = c(1)
        jmask = c(EPG)
        zrow = c(ROW, parts=1)
        w_gate, w_up, w_down = a["L0_ffn_w_gate"], a["L0_ffn_w_up"], a["L0_ffn_w_down"]

        def load_group(e, g):
            b = g % WBUFS
            if g >= WBUFS:
                e.wait_ge(s["y"], base["y"] + g - WBUFS + 1)
            es = slice(EPG * g, EPG * (g + 1))
            e.dma_start(gu_w[b][:, :, :, 0:INNER], w_gate[es].rearrange("e (k p) i -> p e k i", p=P)).then_inc(s_w[b], 16)
            e.dma_start(gu_w[b][:, :, :, INNER:SHARED], w_up[es].rearrange("e (k p) i -> p e k i", p=P)).then_inc(s_w[b], 16)
            e.dma_start(dn_w[b][0:HALF], w_down[es].rearrange("e (k p) d -> p e k d", p=HALF)).then_inc(s_w[b], 16)

        first = base["y"] == 0

        def sync(e):
            if not first:
                e.wait_ge(s["y"], base["y"])
                for g in range(WBUFS):
                    load_group(e, g)
            e.wait_ge(s_ready, n_ready)
            e.dma_start(gate[:, :, 0:EXPERTS], a["gate_T"].rearrange("(k p) e -> p k e", p=P)).then_inc(s["w"], 16)
            for dst, src in ((iota_n, "iota_row"), (iota_bf, "iota_bf"), (tile_off, "tile_off"),
                             (key_off, "key_off"), (jmask, "slot_mask"), (thresh, "pair_starts")):
                e.dma_start(dst, a[src]).then_inc(s["w"], 16)
            e.dma_start(sh_w[:, :, 0, :], a["L0_ffn_sw_gate"].rearrange("(k p) i -> p k i", p=P)).then_inc(s["wsh"], 16)
            e.dma_start(sh_w[:, :, 1, :], a["L0_ffn_sw_up"].rearrange("(k p) i -> p k i", p=P)).then_inc(s["wsh"], 16)
            e.dma_start(sh_d[:, 0:2, :], a["L0_ffn_sw_down"][0:2 * P].rearrange("(c p) d -> p c d", p=P)).then_inc(s["wsh"], 16)
            e.dma_start(sh_d[0:96, 2, :], a["L0_ffn_sw_down"][2 * P:SHARED]).then_inc(s["wsh"], 16)
            e.wait_ge(ln["xn"], ln_base["xn"] + TILES)
            body = table[0:TOKENS].rearrange("(t p) r -> p t r", p=P)
            e.dma_start(body[:, :, 0:DIM], xn[:]).then_inc(s["xrow"], 16)
            if first:
                for g in range(2):
                    load_group(e, g)
            e.wait_ge(s["prob"], base["prob"] + 2)
            e.dma_start(body[:, :, DIM:ROW], prob).then_inc(s["rows"], 16)
            e.dma_start(table[TOKENS:TOKENS + 1], zrow).then_inc(s["rows"], 16)
            if first:
                for g in range(2, 4):
                    load_group(e, g)
            e.wait_ge(s["half"], base["half"] + 1)
            e.dma_start(top32[0:64, CAP:2 * CAP], top32[64:128, 0:CAP]).then_inc(s["halfin"], 16)
            e.wait_ge(s["tok"], base["tok"] + 1)
            e.dma_start(slot_dram, tok[0:EXPERTS]).then_inc(s["tokrow"], 16)
            e.wait_ge(s["tokrow"], base["tokrow"] + 16)
            e.dma_start(tokrow, slot_dram.rearrange("(g j) c -> g (j c)", j=EPG)).then_inc(s["tokrow"], 16)
            for g in range(4 if first else WBUFS, GROUPS):
                load_group(e, g)

        def pe(e):
            ln_pe(e)
            e.wait_ge(s["w"], base["w"] + 7 * 16)
            e.wait_ge(s["lgsb"], base["lgsb"] + 1)
            for t in range(TILES):
                e.wait_ge(ln["xnT"], ln_base["xnT"] + t // 2 + 1)
                b = bank[2 + t // 4 % 2]
                if t % 4 == 0 and t >= 8:
                    e.wait_ge(s["lgsb"], base["lgsb"] + 1 + t // 4 - 1)
                for k in range(CHUNKS):
                    ins = nc.tensor.matmul(b[:, (t % 4) * P:(t % 4 + 1) * P], xnT[:, k, t * P:(t + 1) * P],
                                           gate[:, k, :], start=(k == 0), stop=(k == CHUNKS - 1))
                if t % 4 == 3:
                    ins.then_inc(s["logit"], 1)
            e.wait_ge(s["wsh"], base["wsh"] + 64)

            def shared_up(n):
                blk, ch = n // 3, n % 3
                lo, w = SHARED_CHUNKS[ch]
                pair = 4 + 2 * (n % 2 if n < UPFRONT else 0)
                if n >= 2:
                    e.wait_ge(s["shu"], base["shu"] + (n - 1 if n < UPFRONT else n))
                for gu in range(2):
                    for k in range(CHUNKS):
                        ins = nc.tensor.matmul(bank[pair + gu][0:w, :], sh_w[:, k, gu, lo:lo + w],
                                               xnT[:, k, blk * BLOCK:(blk + 1) * BLOCK],
                                               start=(k == 0), stop=(k == CHUNKS - 1))
                ins.then_inc(s["shmm"], 1)

            def shared_down(n):
                blk, h = n // 2, n % 2
                e.wait_ge(s["hs"], base["hs"] + 3 * blk + 3)
                if n >= 3:
                    e.wait_ge(s["sdx"], base["sdx"] + n)
                elif n == 2:
                    e.wait_ge(s["shu"], base["shu"] + UPFRONT)
                for q in range(2):
                    t = 2 * h + q
                    for ch, (lo, w) in enumerate(SHARED_CHUNKS):
                        ins = nc.tensor.matmul(bank[n if n < 2 else 7][:, q * DIM:(q + 1) * DIM],
                                               hsT[0:w, blk % 2, ch, t * P:(t + 1) * P], sh_d[0:w, ch, :],
                                               start=(ch == 0), stop=(ch == 2))
                ins.then_inc(s["sdm"], 1)

            shared_up(0)
            e.wait_ge(s["msk"], base["msk"] + 1)
            e.wait_ge(s["lgsb"], base["lgsb"] + 5)
            for i in range(TILES // 2):
                ins = nc.tensor.transpose(bank[2 + i // 4][:, (i % 4) * P:(i % 4 + 1) * P],
                                          msk[:, i, :, :].rearrange("p h e -> p (h e)"), ident[:])
                if i % 4 == 3:
                    ins.then_inc(s["mt"], 1)
            for n in range(1, UPFRONT):
                shared_up(n)
            shared_down(0)
            shared_down(1)
            shared_up(UPFRONT)
            e.wait_ge(s["tokrow"], base["tokrow"] + 32)
            e.wait_ge(s["key"], base["key"] + 2)
            nc.tensor.transpose(bank[2][:, 0:GROUPS], tokrow, ident[0:GROUPS, 0:GROUPS]).then_inc(s["tokt"], 1)
            e.wait_ge(s["seen"], base["seen"] + 1)
            nc.tensor.transpose(bank[3][0:1, 0:P], last, ident[:]).then_inc(s["seent"], 1)
            shared_up(UPFRONT + 1)

            def rows_T(g):
                e.wait_ge(*gathered(g))
                if g >= 1:
                    e.wait_ge(s["bufT"], base["bufT"] + g)
                else:
                    e.wait_ge(s["sdx"], base["sdx"] + 2)
                for k in range(CHUNKS):
                    ins = nc.tensor.transpose(bank[0][:, k * P:(k + 1) * P], xg[:, g, k * P:(k + 1) * P], ident[:])
                ins.then_inc(s["xgt"], 1)

            def gate_up(g):
                e.wait_ge(s_w[g % WBUFS], base[f"wb{g % WBUFS}"] + 48 * (g // WBUFS + 1))
                e.wait_ge(s["bufT"], base["bufT"] + g + 1)
                if g >= 2:
                    e.wait_ge(s["h"], base["h"] + g - 1)
                else:
                    e.wait_ge(s["pairs"], base["pairs"] + 1)
                for k in range(CHUNKS):
                    for j in range(EPG):
                        ins = nc.tensor.matmul(bank[2 + g % 2][CAP * j:CAP * (j + 1), 0:SHARED],
                                               bufT[g % 2][:, k, CAP * j:CAP * (j + 1)], gu_w[g % WBUFS][:, j, k, :],
                                               start=(k == 0), stop=(k == CHUNKS - 1))
                ins.then_inc(s["gu"], 1)

            def hidden_T(g):
                e.wait_ge(s["h"], base["h"] + g + 1)
                if g >= 1:
                    e.wait_ge(s["hTsb"], base["hTsb"] + g)
                for k in range(2):
                    ins = nc.tensor.transpose(bank[1][0:HALF, k * P:(k + 1) * P],
                                              hh[g % 2][:, k * HALF:(k + 1) * HALF], ident[:])
                ins.then_inc(s["ht"], 1)

            def down(g):
                e.wait_ge(s["hTsb"], base["hTsb"] + g + 1)
                if g >= 1:
                    e.wait_ge(s["ysplit"], base["ysplit"] + g)
                else:
                    e.wait_ge(s["shu"], base["shu"] + UPFRONT)
                for k in range(2):
                    for j in range(EPG):
                        ins = nc.tensor.matmul(bank[6][CAP * j:CAP * (j + 1), 0:DIM],
                                               hT[g % 2][0:HALF, k, CAP * j:CAP * (j + 1)],
                                               dn_w[g % WBUFS][0:HALF, j, k, :], start=(k == 0), stop=(k == 1))
                ins.then_inc(s["y"], 1)

            rows_T(0)
            for g in range(GROUPS + 1):
                if g < GROUPS:
                    gate_up(g)
                if g >= 1:
                    hidden_T(g - 1)
                if g + 1 < GROUPS:
                    rows_T(g + 1)
                if g >= 1:
                    down(g - 1)
                if g < len(PIECES) and PIECES[g]:
                    kind, n = PIECES[g]
                    (shared_up if kind == "up" else shared_down)(n)
            e.wait_ge(s["pairs"], base["pairs"] + 1)
            n_pairs = e.value_load(pairs, min_val=1, max_val=TILES // 2)
            with e.Fori(0, n_pairs) as i:
                for r in range(2):
                    t = i * 2 + r
                    e.wait_ge(sl["oneh"], t + 1)
                    e.wait_ge(sl["done"], t + 1)
                    b = bank[r][:, 0:DIM]
                    for g in range(GROUPS):
                        if g == 0:
                            e.wait_ge(s["yparts"], base["yparts"] + GROUPS - 2)
                        elif g >= GROUPS - 2:
                            e.wait_ge(s["yparts"], base["yparts"] + g + 1)
                        for k in range(3):
                            ins = nc.tensor.matmul(b, oneh[r][:, g, :], yp[:, k, g, :], start=(g == 0 and k == 0),
                                                   stop=(g == GROUPS - 1 and k == 2))
                    ins.then_inc(sl["mix"], 1)

        def act(e):
            ln_act(e)
            for q in range(TILES // 4):
                e.wait_ge(s["logit"], base["logit"] + q + 1)
                nc.scalar.copy(lg[:, 4 * q:4 * q + 4, 0:EXPERTS],
                               bank[2 + q % 2][:].rearrange("p (t e) -> p t e", t=4)[:, :, 0:EXPERTS]
                               ).then_inc(s["lgsb"], 1)

            def shared(n):
                w = SHARED_CHUNKS[n % 3][1]
                pair = 4 + 2 * (n % 2 if n < UPFRONT else 0)
                e.wait_ge(s["shmm"], base["shmm"] + n + 1)
                if n >= 2:
                    e.wait_ge(s["hs"], base["hs"] + n - 1)
                nc.scalar.activation(sg_sh[n % 2][0:w], bank[pair][0:w, :], ACT.Silu).then_inc(s["shg"], 1)
                nc.scalar.copy(su_sh[n % 2][0:w], bank[pair + 1][0:w, :]).then_inc(s["shu"], 1)

            e.wait_ge(s["expin"], base["expin"] + 1)
            nc.scalar.activation(prob, prob, ACT.Exp).then_inc(s["exp"], 1)
            e.wait_ge(s["xrow"], base["xrow"] + 16)
            e.wait_ge(ln["xnT"], ln_base["xnT"] + TILES // 2)
            for n in range(UPFRONT + 2):
                shared(n)
            for g in range(GROUPS + 1):
                if g < GROUPS:
                    e.wait_ge(s["xgt"], base["xgt"] + g + 1)
                    if g >= 2:
                        e.wait_ge(s["gu"], base["gu"] + g - 1)
                    nc.scalar.copy(bufT[g % 2], bank[0][:, 0:DIM].rearrange("p (k n) -> p k n", k=2)
                                   ).then_inc(s["bufT"], 1)
                    e.wait_ge(s["gu"], base["gu"] + g + 1)
                    if g >= 2:
                        e.wait_ge(s["h"], base["h"] + g - 1)
                    nc.scalar.activation(sg[g % 2], bank[2 + g % 2][:, 0:INNER], ACT.Silu).then_inc(s["sg"], 1)
                if g >= 1:
                    e.wait_ge(s["ht"], base["ht"] + g)
                    if g >= 3:
                        e.wait_ge(s["y"], base["y"] + g - 2)
                    nc.scalar.copy(hT[(g - 1) % 2][0:HALF], bank[1][0:HALF, 0:DIM]
                                   .rearrange("p (k n) -> p k n", k=2)).then_inc(s["hTsb"], 1)
                if 1 <= g <= len(PIECES) and PIECES[g - 1] and PIECES[g - 1][0] == "up":
                    shared(PIECES[g - 1][1])

        def dve(v):
            link = chains["dve"]
            ln_dve(v)
            v.wait_ge(s_ready, n_ready)
            nc.vector.memset(gate[:, :, EXPERTS:P], 0.0)
            nc.vector.memset(lg[:, :, EXPERTS:66], -BIG)
            nc.vector.memset(zrow, 0.0)
            nc.vector.memset(r8[:, :, TOPK:8], -BIG).then_inc(s["lgsb"], 1)
            for t in range(TILES):
                if t % 4 == 0:
                    v.wait_ge(s["lgsb"], base["lgsb"] + 2 + t // 4)
                ins = nc.vector.max(v8[:, t, :], lg[:, t, 0:EXPERTS])
            link(ins)
            nc.vector.tensor_tensor(prob, lg[:, :, 0:EXPERTS], v8[:, :, 0:1].to_broadcast([P, TILES, EXPERTS]),
                                    ALU.subtract).then_inc(s["expin"], 1)
            link(nc.vector.tensor_copy(r8[:, :, 0:TOPK], v8[:, :, 0:TOPK]))
            for t in range(TILES):
                ins = nc.vector.match_replace(rep[:, t, :], r8[:, t, :], lg[:, t, :], BIG)
            link(ins)
            for h in range(2):
                ins = nc.vector.tensor_scalar(msk[:, :, h, :], rep[:, h * 8:(h + 1) * 8, 0:EXPERTS], 1.0e38, None, ALU.is_gt)
            ins.then_inc(s["msk"], 1)
            v.wait_ge(s["exp"], base["exp"] + 1)
            link(nc.vector.tensor_reduce(esum, prob, AX_X, ALU.add))
            link(nc.vector.reciprocal(einv, esum))
            nc.vector.tensor_tensor(prob, prob, einv.rearrange("p (t o) -> p t o", o=1).to_broadcast([P, TILES, EXPERTS]),
                                    ALU.mult).then_inc(s["prob"], 2)
            for i in range(2):
                v.wait_ge(s["mt"], base["mt"] + i + 1)
                ins = nc.vector.scalar_tensor_tensor(out=keyA[:, 512 * i:512 * (i + 1)], in0=iota_n[:, 512 * i:512 * (i + 1)],
                                                     scalar=key_off, in1=bank[2 + i][:], op0=ALU.add, op1=ALU.mult)
                ins.then_inc(s["key"], 1)
            v.wait_ge(s["key"], base["key"] + 2)
            src, dst = keyA, keyB
            for r in range(CAP // 8):
                ins = nc.vector.max(top32[:, 8 * r:8 * r + 8], src)
                if r == CAP // 8 - 1:
                    ins.then_inc(s["half"], 1)
                else:
                    link(ins)
                    link(nc.vector.match_replace(dst, top32[:, 8 * r:8 * r + 8], src, 0.0))
                    src, dst = dst, src
            v.wait_ge(s["halfin"], base["halfin"] + 16)
            v.wait_ge(s["half"], base["half"] + 1)
            src, dst = top32[0:EXPERTS], bestB[0:EXPERTS]
            for r in range(CAP // 8):
                link(nc.vector.max(best[0:EXPERTS, 8 * r:8 * r + 8], src))
                if r < CAP // 8 - 1:
                    link(nc.vector.match_replace(dst, best[0:EXPERTS, 8 * r:8 * r + 8], src, 0.0))
                    src, dst = dst, src
            nc.vector.tensor_scalar(tok[0:EXPERTS], best[0:EXPERTS], -1.0, float(TOKENS), ALU.mult, ALU.add
                                    ).then_inc(s["tok"], 1)

            def shared_add(n):
                v.wait_ge(s["sdm"], base["sdm"] + n + 1)
                xs = x[:, 2 * n:2 * n + 2, :]
                nc.vector.scalar_tensor_tensor(out=xs, in0=bank[n if n < 2 else 7].rearrange("p (t d) -> p t d", t=2),
                                               scalar=0.5, in1=xs, op0=ALU.mult, op1=ALU.add).then_inc(s["sdx"], 1)
                if n >= 1:
                    pair_stats(n - 1)

            def pair_stats(n):
                v.wait_ge(s["sdx"], base["sdx"] + n + 1)
                statistics(2 * n, 2 * n + 2)

            v.wait_ge(s["tokt"], base["tokt"] + 1)
            nc.vector.tensor_copy(tokp, bank[2][:, 0:GROUPS])
            nc.vector.tensor_copy(idx, bank[2][:, 0:GROUPS]).then_inc(s["idx"], 1)
            v.wait_ge(s["idx"], base["idx"] + 1)
            link(nc.vector.scalar_tensor_tensor(out=seen, in0=tokp, scalar=TOKENS - 0.5, in1=tokp, op0=ALU.is_lt, op1=ALU.mult))
            nc.vector.tensor_reduce(last, seen, AX_X, ALU.max).then_inc(s["seen"], 1)
            shared_add(0)
            shared_add(1)
            v.wait_ge(s["seent"], base["seent"] + 1)
            link(nc.vector.tensor_reduce(lastT, bank[3][0:1, 0:P], AX_X, ALU.max))
            link(nc.vector.tensor_scalar(reached, thresh, lastT, None, ALU.is_le))
            link(nc.vector.tensor_reduce(lastT, reached, AX_X, ALU.add))
            nc.vector.tensor_copy(pairs, lastT).then_inc(s["pairs"], 1)
            link(nc.vector.tensor_tensor(rel, tokp.rearrange("p (o g) -> p o g", o=1).to_broadcast([P, TILES + 1, GROUPS]),
                                         tile_off.rearrange("p (t o) -> p t o", o=1).to_broadcast([P, TILES + 1, GROUPS]),
                                         ALU.subtract))

            def slot_weights(q):
                for g in range(4 * q, 4 * q + 4):
                    v.wait_ge(*gathered(g))
                    o = DIM + EPG * g
                    link(nc.vector.tensor_tensor_reduce(out=junk, in0=xg[:, g, o:o + EPG], in1=jmask, scale=1.0,
                                                        scalar=0.0, op0=ALU.mult, op1=ALU.add, accum_out=wsel[:, g:g + 1]))

            def split(g):
                v.wait_ge(s["y"], base["y"] + g + 1)
                y, w, r = bank[6][:, 0:DIM], wsel[:, g:g + 1], yres[g % 2]
                link(nc.vector.tensor_scalar(yp[:, 0, g, :], y, w, None, ALU.mult))
                nc.vector.scalar_tensor_tensor(out=r, in0=y, scalar=w, in1=yp[:, 0, g, :], op0=ALU.mult, op1=ALU.subtract
                                               ).then_inc(s["ysplit"], 1)
                v.wait_ge(s["ysplit"], base["ysplit"] + g + 1)
                link(nc.vector.tensor_copy(yp[:, 1, g, :], r))
                nc.vector.tensor_tensor(yp[:, 2, g, :], r, yp[:, 1, g, :], ALU.subtract).then_inc(s["yparts"], 1)

            def one_hot(rel_t, r):
                nc.vector.tensor_tensor(oneh[r], rel_t.to_broadcast([P, GROUPS, P]),
                                        iota_bf.rearrange("p (o n) -> p o n", o=1).to_broadcast([P, GROUPS, P]),
                                        ALU.is_equal).then_inc(sl["oneh"], 1)

            for g in range(GROUPS + 1):
                if g < GROUPS:
                    if g % 4 == 0:
                        slot_weights(g // 4)
                    v.wait_ge(s["sg"], base["sg"] + g + 1)
                    if g >= 2:
                        v.wait_ge(s["ht"], base["ht"] + g - 1)
                    nc.vector.tensor_tensor(hh[g % 2], sg[g % 2], bank[2 + g % 2][:, INNER:SHARED], ALU.mult
                                            ).then_inc(s["h"], 1)
                if g >= 1:
                    split(g - 1)
                if g < len(PIECES) and PIECES[g] and PIECES[g][0] == "down":
                    shared_add(PIECES[g][1])
                if g == GROUPS - 2:
                    pair_stats(7)
                    v.wait_ge(s["shmm"], base["shmm"] + 12)
                    one_hot(rel[:, 0, :].rearrange("p (g o) -> p g o", o=1), 0)
                    nc.vector.memset(seen, 0.0).then_inc(sl["done"], 2)
            v.wait_ge(s["pairs"], base["pairs"] + 1)
            v.wait_ge(s["sdx"], base["sdx"] + 8)
            n_pairs = v.value_load(pairs, min_val=1, max_val=TILES // 2)
            with v.Fori(0, n_pairs) as i:
                for r in range(2):
                    t = i * 2 + r
                    one_hot(rel[:, bass.ds(t + 1, 1), :].rearrange("p o g -> p g o"), 1 - r)
                    v.wait_ge(sl["mix"], t + 1)
                    xt = x[:, bass.ds(t, 1), :].rearrange("p o d -> p (o d)")
                    nc.vector.scalar_tensor_tensor(out=xt, in0=bank[r][:, 0:DIM], scalar=0.5, in1=xt,
                                                   op0=ALU.mult, op1=ALU.add).then_inc(sl["done"], 1)
                    v.wait_ge(sl["done"], t + 3)
                    nc.vector.bn_stats(stats[:, bass.ds(t, 1), :].rearrange("p o c -> p (o c)"), xt)
            nc.vector.memset(seen, 0.0).then_inc(s["out"], 1)

        def pool(e):
            link = chains["pool"]
            ln_pool(e)
            def hidden(n):
                blk, ch = n // 3, n % 3
                w = SHARED_CHUNKS[ch][1]
                if n == 0:
                    e.wait_ge(s["xrow"], base["xrow"] + 16)
                    e.wait_ge(ln["xnT"], ln_base["xnT"] + TILES // 2)
                if blk >= 2 and ch == 0:
                    e.wait_ge(s["sdm"], base["sdm"] + 2 * blk - 2)
                e.wait_ge(s["shg"], base["shg"] + n + 1)
                e.wait_ge(s["shu"], base["shu"] + n + 1)
                nc.gpsimd.tensor_tensor(hsT[0:w, blk % 2, ch, :], sg_sh[n % 2][0:w], su_sh[n % 2][0:w],
                                        ALU.mult).then_inc(s["hs"], 1)
            for n in range(UPFRONT):
                hidden(n)
            e.wait_ge(s["idx"], base["idx"] + 1)
            e.wait_ge(s["rows"], base["rows"] + 32)
            for g in range(GROUPS):
                e.indirect_dma_start(xg[:, g, :], None, table, bass.IndirectOffsetOnAxis(ap=idx[:, g:g + 1], axis=0)
                                     ).then_inc(gathered(g)[0], 16)
            for n in range(UPFRONT, 12):
                hidden(n)

        room_free = (s["y"], base["y"] + GROUPS)
        return (s["out"], base["out"] + 1), dict(room_free=room_free, sync=sync, tensor=pe, scalar=act, vector=dve, gpsimd=pool)

    E = MIX_EXPERTS
    w3 = sb("w3", [P, CHUNKS, DIM])
    b3 = sb("b3", [P, DIM])
    w1, w2 = sb("w1", [P, E, HD]), sb("w2", [P, E, HD])
    b1, b2, sbias, iota8, hmask16 = (sb(n, [P, 8]) for n in ("b1", "b2", "switch_bias", "iota8_sb", "mask16_sb"))
    s_mixw = sem("mixer_weights")

    def load_mixer_weights(e):
        row = lambda v: v.rearrange("(o d) -> o d", o=1)
        for dst, src in ((w1, a["w1_rep"]), (w2, a["w2_rep"]), (b1, a["b1_rep"]), (b2, a["b2_rep"]),
                         (sbias, row(a["L1_ffn_switch_b"]).to_broadcast([P, E])), (b3, row(a["L1_ffn_b3"]).to_broadcast([P, DIM])),
                         (iota8, a["iota8"]), (hmask16, a["mask16"]), (w3, a["w3_T"].rearrange("(k p) e -> p k e", p=P))):
            e.dma_start(dst[:], src).then_inc(s_mixw, 16)

    def linear_attention(tag, s_ready, n_ready, before):
        (ln, ln_base), ln_dve, ln_act, ln_pe, ln_pool = layer_norm(s_ready, n_ready, before)
        s = sems(tag, "w kv kr vv vk mem qmm qT o on ot oT pj xb out")
        c = Carve()
        c.at = WBUFS * EPG * (CHUNKS * SHARED + 2 * DIM)
        wq = c(CHUNKS * DIM).rearrange("p (k e) -> p k e", k=CHUNKS)
        wkv = c(CHUNKS * 2 * DIM).rearrange("p (k e) -> p k e", k=CHUNKS)
        wp = c(CHUNKS * DIM).rearrange("p (k e) -> p k e", k=CHUNKS)
        bp = c(DIM)
        hmask = c(4)
        kr = [c(DIM) for _ in range(2)]
        vv = [c(2 * 129).rearrange("p (c n) -> p c n", c=2) for _ in range(2)]
        qT = c(CHUNKS * TOKENS).rearrange("p (c n) -> p c n", c=CHUNKS)
        W33 = 4 * (LHD + 1)
        mem = c(2 * W33).rearrange("p (c h n) -> p c h n", c=2, h=4)
        den = [c(LHEADS) for _ in range(2)]
        on = [c(DIM) for _ in range(2)]
        oT = [c(DIM).rearrange("p (c n) -> p c n", c=2) for _ in range(2)]

        def sync(e):
            e.wait_ge(s_ready, n_ready)
            e.dma_start(wkv, a["wkv_T"].rearrange("(k p) e -> p k e", p=P)).then_inc(s["w"], 16)
            e.dma_start(wq, a["wq_T"].rearrange("(k p) e -> p k e", p=P)).then_inc(s["w"], 16)
            e.dma_start(wp, a["wproj_T"].rearrange("(k p) e -> p k e", p=P)).then_inc(s["w"], 16)
            e.dma_start(hmask, a["mask32"]).then_inc(s["w"], 16)
            e.dma_start(bp, a["L0_attn_b_proj"].rearrange("(o d) -> o d", o=1).to_broadcast([P, DIM])).then_inc(s["w"], 16)
            load_mixer_weights(e)

        def pe(e):
            ln_pe(e)
            e.wait_ge(s["w"], 80)
            for t in range(TILES):
                e.wait_ge(ln["xnT"], ln_base["xnT"] + t // 2 + 1)
                if t >= 2:
                    e.wait_ge(s["kr"], t - 1)
                    e.wait_ge(s["vv"], t - 1)
                for half in range(2):
                    for k in range(CHUNKS):
                        ins = nc.tensor.matmul(bank[2 + 4 * half + t % 2][:, 0:DIM], xnT[:, k, t * P:(t + 1) * P],
                                               wkv[:, k, half * DIM:(half + 1) * DIM], start=(k == 0), stop=(k == 1))
                ins.then_inc(s["kv"], 1)
                if t >= 1:
                    memory(e, t - 1)
            memory(e, TILES - 1)
            for n in range(CHUNKS * BLOCKS):
                ch, blk = n // BLOCKS, n % BLOCKS
                if n >= 2:
                    e.wait_ge(s["qT"], n - 1)
                for k in range(CHUNKS):
                    ins = nc.tensor.matmul(bank[6 + n % 2][:], wq[:, k, ch * P:(ch + 1) * P],
                                           xnT[:, k, blk * BLOCK:(blk + 1) * BLOCK], start=(k == 0), stop=(k == 1))
                ins.then_inc(s["qmm"], 1)
            e.wait_ge(s["qT"], CHUNKS * BLOCKS)
            e.wait_ge(s["mem"], 2)
            for t in range(TILES + 2):
                if t < TILES:
                    if t >= 2:
                        e.wait_ge(s["on"], t - 1)
                    for ch in range(CHUNKS):
                        ins = nc.tensor.matmul(bank[t % 2][:, ch * W33:(ch + 1) * W33], qT[:, ch, t * P:(t + 1) * P],
                                               mem[:, ch], start=True, stop=True)
                    ins.then_inc(s["o"], 1)
                if 1 <= t <= TILES:
                    u = t - 1
                    e.wait_ge(s["on"], u + 1)
                    if u >= 2:
                        e.wait_ge(s["oT"], u - 1)
                    for ch in range(CHUNKS):
                        ins = nc.tensor.transpose(bank[2 + u % 2][:, ch * P:(ch + 1) * P], on[u % 2][:, ch * P:(ch + 1) * P], ident[:])
                    ins.then_inc(s["ot"], 1)
                if t >= 2:
                    u = t - 2
                    e.wait_ge(s["oT"], u + 1)
                    if u >= 2:
                        e.wait_ge(s["out"], u - 1)
                    for ch in range(CHUNKS):
                        ins = nc.tensor.matmul(bank[6 + u % 2][:, 0:DIM], oT[u % 2][:, ch], wp[:, ch], start=(ch == 0), stop=(ch == 1))
                    ins.then_inc(s["pj"], 1)

        def memory(e, t):
            e.wait_ge(s["kr"], t + 1)
            e.wait_ge(s["vv"], t + 1)
            for ch in range(CHUNKS):
                ins = nc.tensor.matmul(bank[4 + ch][:, 0:129], kr[t % 2][:, ch * P:(ch + 1) * P], vv[t % 2][:, ch, :],
                                       start=(t == 0), stop=(t == TILES - 1))
            ins.then_inc(s["vk"], 1)

        def act(e):
            ln_act(e)
            for t in range(TILES):
                e.wait_ge(s["kv"], t + 1)
                if t >= 2:
                    e.wait_ge(s["vk"], t - 1)
                nc.scalar.activation(kr[t % 2], bank[2 + t % 2][:, 0:DIM], ACT.Relu).then_inc(s["kr"], 1)
            for n in range(CHUNKS * BLOCKS):
                ch, blk = n // BLOCKS, n % BLOCKS
                e.wait_ge(s["qmm"], n + 1)
                nc.scalar.activation(qT[:, ch, blk * BLOCK:(blk + 1) * BLOCK], bank[6 + n % 2][:], ACT.Relu).then_inc(s["qT"], 1)
            for u in range(TILES):
                e.wait_ge(s["ot"], u + 1)
                if u >= 2:
                    e.wait_ge(s["pj"], u - 1)
                nc.scalar.copy(oT[u % 2], bank[2 + u % 2][:, 0:DIM].rearrange("p (c n) -> p c n", c=2)).then_inc(s["oT"], 1)

        def dve(v):
            link = chains["dve"]
            ln_dve(v)
            nc.vector.memset(vv[0][:, :, P:P + 1], 1.0)
            link(nc.vector.memset(vv[1][:, :, P:P + 1], 1.0))
            for t in range(TILES):
                v.wait_ge(s["kv"], t + 1)
                if t >= 2:
                    v.wait_ge(s["vk"], t - 1)
                nc.vector.tensor_copy(vv[t % 2][:, :, 0:P], bank[6 + t % 2][:, 0:DIM].rearrange("p (c n) -> p c n", c=2)
                                      ).then_inc(s["vv"], 1)
            v.wait_ge(s["vk"], TILES)
            v.wait_ge(s["w"], 80)
            hm = hmask.rearrange("p (h o) -> p h o", o=1)
            for ch in range(CHUNKS):
                b = bank[4 + ch]
                nc.vector.tensor_tensor(mem[:, ch, :, 0:LHD], b[:, 0:P].rearrange("p (h n) -> p h n", h=4),
                                        hm.to_broadcast([P, 4, LHD]), ALU.mult)
                nc.vector.tensor_scalar(mem[:, ch, :, LHD], hmask, b[:, P:P + 1], None, ALU.mult).then_inc(s["mem"], 1)
            for t in range(TILES + 2):
                if t < TILES:
                    v.wait_ge(s["o"], t + 1)
                    o = bank[t % 2][:, 0:2 * W33].rearrange("p (h n) -> p h n", h=LHEADS)
                    link(nc.vector.tensor_scalar(den[t % 2], o[:, :, LHD], 1e-15, None, ALU.add))
                    link(nc.vector.reciprocal(den[t % 2], den[t % 2]))
                    if t >= 2:
                        v.wait_ge(s["ot"], t - 1)
                    nc.vector.tensor_tensor(on[t % 2].rearrange("p (h n) -> p h n", h=LHEADS), o[:, :, 0:LHD],
                                            den[t % 2].rearrange("p (h o) -> p h o", o=1).to_broadcast([P, LHEADS, LHD]),
                                            ALU.mult).then_inc(s["on"], 1)
                if t >= 2:
                    u = t - 2
                    if u == 0:
                        v.wait_ge(s["xb"], 1)
                    v.wait_ge(s["pj"], u + 1)
                    nc.vector.tensor_tensor(x[:, u, :], bank[6 + u % 2][:, 0:DIM], x[:, u, :], ALU.add).then_inc(s["out"], 1)
                    out_stats(v, s["out"], 0, u, tag)

        def pool(e):
            ln_pool(e)
            e.wait_ge(ln["xn"], ln_base["xn"] + TILES)
            e.wait_ge(s["w"], 80)
            nc.gpsimd.tensor_tensor(x[:], x[:], bp.rearrange("p (o d) -> p o d", o=1).to_broadcast([P, TILES, DIM]),
                                    ALU.add).then_inc(s["xb"], 1)

        return (s["out"], TILES), dict(sync=sync, tensor=pe, scalar=act, vector=dve, gpsimd=pool)

    def head_mixer(tag, s_ready, n_ready, before, room_free):
        (ln, ln_base), ln_dve, ln_act, ln_pe, ln_pool = layer_norm(s_ready, n_ready, before)
        s, base = shared_sems("mix", dict(
            sw=16 * MIX_EXPERTS, lg=1, h=16, o=8, f=TILES, ex=1, g=16, part=1, ein=1, bd=4, z=8, out=TILES, xb=1))
        c = Carve()
        sw = c(E * 2 * DIM).rearrange("p (e c d) -> p e c d", e=E, c=2)
        c.at = STEP_OPERANDS - TILES * HPG * 2 * HD * 2
        ones = c(P)
        junk = c(E * 2 * DIM).rearrange("p (e c d) -> p e c d", e=E, c=2)
        part, logit, m8, e8, esum = c(E), c(E), c(E), c(E), c(1)
        mi = c(E, U32)
        mif = c(E)
        oh = c(4 * E).rearrange("p (k e) -> p k e", k=4)
        tmp = c(4 * E * HD).rearrange("p (k e f) -> p k e f", k=4, e=E)
        sel = c(4 * HD).rearrange("p (k f) -> p k f", k=4)
        bsel = c(4)
        tmpb = c(4 * E).rearrange("p (k e) -> p k e", k=4)
        b2s = c(1)
        bd = [[c(P) for _ in range(2)] for _ in range(2)]
        ht = [c(BLOCK) for _ in range(4)]
        z = [c(CHUNKS * BLOCK).rearrange("p (c n) -> p c n", c=2) for _ in range(2)]

        def sync(e):
            e.wait_ge(*room_free)
            for ex in range(E):
                e.dma_start(sw[:, ex], a["L1_ffn_switch_w"][ex:ex + 1].rearrange("e (c p d) -> p (e c) d", p=P, c=2)).then_inc(s["sw"], 16)

        def pe(e):
            ln_pe(e)
            e.wait_ge(s["part"], base["part"] + 1)
            nc.tensor.matmul(bank[2][:, 0:E], ones, part, start=True, stop=True).then_inc(s["lg"], 1)
            e.wait_ge(s["bd"], base["bd"] + 4)
            e.wait_ge(ln["xnT"], ln_base["xnT"] + TILES // 2)
            U = 2 * BLOCKS

            def second(u):
                if u >= 2:
                    e.wait_ge(s["z"], base["z"] + u - 1)
                for k in range(2):
                    e.wait_ge(s["g"], base["g"] + 2 * u + k + 1)
                    ins = nc.tensor.matmul(bank[4 + u % 2][:], bd[1][k], ht[(2 * u + k) % 4], start=(k == 0), stop=(k == 1))
                ins.then_inc(s["o"], 1)

            def final(blk):
                e.wait_ge(s["z"], base["z"] + 2 * blk + 2)
                for q in range(4):
                    t = 4 * blk + q
                    if t >= 2:
                        e.wait_ge(s["out"], base["out"] + t - 1)
                    for k in range(CHUNKS):
                        ins = nc.tensor.matmul(bank[6 + t % 2][:, 0:DIM], z[blk % 2][:, k, q * P:(q + 1) * P], w3[:, k, :],
                                               start=(k == 0), stop=(k == 1))
                    ins.then_inc(s["f"], 1)

            for u in range(U):
                blk, ch = u // 2, u % 2
                for k in range(2):
                    n = 2 * u + k
                    if n >= 4:
                        e.wait_ge(s["g"], base["g"] + n - 3)
                    nc.tensor.matmul(bank[n % 4][:], bd[0][k], xnT[:, ch, blk * BLOCK:(blk + 1) * BLOCK],
                                     start=True, stop=True).then_inc(s["h"], 1)
                if u >= 1:
                    second(u - 1)
                if u >= 3 and u % 2:
                    final(u // 2 - 1)
            second(U - 1)
            final(BLOCKS - 1)

        def act(e):
            ln_act(e)
            e.wait_ge(s["ein"], base["ein"] + 1)
            nc.scalar.activation(e8, e8, ACT.Exp).then_inc(s["ex"], 1)
            for n in range(4 * BLOCKS):
                e.wait_ge(s["h"], base["h"] + n + 1)
                if n >= 4:
                    e.wait_ge(s["o"], base["o"] + n // 2 - 1)
                nc.scalar.activation(ht[n % 4], bank[n % 4][:], ACT.Gelu, bias=bsel[:, n % 2:n % 2 + 1]).then_inc(s["g"], 1)

        def dve(v):
            link = chains["dve"]
            ln_dve(v)
            v.wait_ge(ln["xn"], ln_base["xn"] + TILES)
            link(nc.vector.memset(ones, 1.0))
            v.wait_ge(s["sw"], base["sw"] + 16 * E)
            for ex in range(E):
                ins = nc.vector.tensor_tensor_reduce(out=junk[:, ex], in0=xn[:, 0:2, :], in1=sw[:, ex], scale=1.0, scalar=0.0,
                                                     op0=ALU.mult, op1=ALU.add, accum_out=part[:, ex:ex + 1])
            ins.then_inc(s["part"], 1)
            v.wait_ge(s_mixw, 16 * 9)
            v.wait_ge(s["lg"], base["lg"] + 1)
            link(nc.vector.tensor_tensor(logit, bank[2][:, 0:E], sbias[:], ALU.add))
            link(nc.vector.max(m8, logit))
            nc.vector.max_index(mi, m8, logit)
            nc.vector.tensor_scalar(e8, m8, m8[:, 0:1], None, ALU.subtract).then_inc(s["ein"], 1)
            v.wait_ge(s["ein"], base["ein"] + 1)
            link(nc.vector.tensor_copy(mif, mi))
            for k in range(2):
                ins = nc.vector.tensor_scalar(oh[:, k, :], iota8[:], mif[:, k:k + 1], None, ALU.is_equal)
            link(ins)
            v.wait_ge(s["ex"], base["ex"] + 1)
            link(nc.vector.tensor_reduce(esum, e8, AX_X, ALU.add))
            link(nc.vector.reciprocal(esum, esum))
            link(nc.vector.tensor_scalar(e8, e8, esum, None, ALU.mult))
            for k in range(2):
                ins = nc.vector.tensor_scalar(oh[:, 2 + k, :], oh[:, k, :], e8[:, k:k + 1], None, ALU.mult)
            link(ins)
            for k in range(4):
                nc.vector.tensor_tensor(tmp[:, k], (w1, w2)[k // 2][:], oh[:, k, :].rearrange("p (e o) -> p e o", o=1)
                                        .to_broadcast([P, E, HD]), ALU.mult)
            for layer, b in enumerate((b1, b2)):
                ks = slice(2 * layer, 2 * layer + 2)
                ins = nc.vector.tensor_tensor(tmpb[:, ks], oh[:, ks], b[:].rearrange("p (o e) -> p o e", o=1)
                                              .to_broadcast([P, 2, E]), ALU.mult)
            link(ins)
            nc.vector.tensor_reduce(bsel, tmpb, AX_X, ALU.add)
            for k in range(4):
                ins = nc.vector.tensor_reduce(sel[:, k, :], tmp[:, k].rearrange("p e f -> p f e"), AX_X, ALU.add)
            link(ins)
            nc.vector.tensor_tensor(b2s, bsel[:, 2:3], bsel[:, 3:4], ALU.add)
            for k in range(4):
                nc.vector.tensor_tensor(bd[k // 2][k % 2].rearrange("p (h f) -> p h f", h=8),
                                        sel[:, k, :].rearrange("p (o f) -> p o f", o=1).to_broadcast([P, 8, HD]),
                                        hmask16[:].rearrange("p (h o) -> p h o", o=1).to_broadcast([P, 8, HD]),
                                        ALU.mult).then_inc(s["bd"], 1)
            v.wait_ge(ln["xnT"], ln_base["xnT"] + TILES // 2)

            def outs(blk):
                for q in range(4):
                    t = 4 * blk + q
                    if t == 0:
                        v.wait_ge(s["xb"], base["xb"] + 1)
                    v.wait_ge(s["f"], base["f"] + t + 1)
                    nc.vector.scalar_tensor_tensor(out=x[:, t, :], in0=bank[6 + t % 2][:, 0:DIM], scalar=0.5, in1=x[:, t, :],
                                                   op0=ALU.mult, op1=ALU.add).then_inc(s["out"], 1)
                    out_stats(v, s["out"], base["out"], t, tag)
            for u in range(2 * BLOCKS):
                blk, ch = u // 2, u % 2
                v.wait_ge(s["o"], base["o"] + u + 1)
                if blk >= 2 and ch == 0:
                    v.wait_ge(s["f"], base["f"] + 4 * (blk - 1))
                nc.vector.scalar_tensor_tensor(out=z[blk % 2][:, ch, :], in0=bank[4 + u % 2][:], scalar=b2s,
                                               in1=xnT[:, ch, blk * BLOCK:(blk + 1) * BLOCK], op0=ALU.add, op1=ALU.add
                                               ).then_inc(s["z"], 1)
                if u >= 2 and u % 2 == 0:
                    outs(u // 2 - 1)
            outs(BLOCKS - 1)

        def pool(e):
            link = chains["pool"]
            ln_pool(e)
            e.wait_ge(ln["xn"], ln_base["xn"] + TILES)
            if base["xb"] == 0:
                e.wait_ge(s_mixw, 16 * 9)
                link(nc.gpsimd.tensor_scalar(b3[:], b3[:], 0.5, None, ALU.mult))
            nc.gpsimd.tensor_tensor(x[:], x[:], b3[:].rearrange("p (o d) -> p o d", o=1).to_broadcast([P, TILES, DIM]),
                                    ALU.add).then_inc(s["xb"], 1)

        return (s["out"], base["out"] + TILES), dict(sync=sync, tensor=pe, scalar=act, vector=dve, gpsimd=pool)
    q_dram = dram("q_parts", [3, DIM, TOKENS], BF16)
    k_dram = dram("k_parts", [3, DIM, TOKENS], BF16)
    v_dram = dram("v_ones", [P, HGROUPS * TILES, HPG * 2 * HD])

    def softmax_attention(tag, s_ready, n_ready, before):
        (ln, ln_base), ln_dve, ln_act, ln_pe, ln_pool = layer_norm(s_ready, n_ready, before)
        s = sems(tag, "w cs wg wo qk v va vd rm ra split exk part2 part3e part3o kd qd0 qd onesr keyones kexp qexp kf qf kft kfT mem memc memb "
                      "memo mden comb gex st exp pv raw rt rawT rden used mx mxd nm nmt nms mrow ot oT pj out")
        s_ld = [sem(f"{tag}_step{b}") for b in range(3)]
        s_lv = [sem(f"{tag}_values{b}") for b in range(3)]
        VW = 2 * HD
        MW = HD + 1
        SPLITS = 2 * BLOCKS
        PBUFS = BLOCKS + 1
        c = Carve()
        KS = [c(HPG * TOKENS // 2, BF16).rearrange("p (h n) -> p h n", h=HPG) for _ in range(3)]
        QS = [c(HPG * BLOCK // 2, BF16).rearrange("p (h n) -> p h n", h=HPG) for _ in range(3)]
        VS = [c(TILES * HPG * VW).rearrange("p (t n) -> p t n", t=TILES) for _ in range(3)]
        PT = [c(HPG * BLOCK).rearrange("p (h n) -> p h n", h=HPG) for _ in range(2)]
        qk = [c(CHUNKS * TOKENS).rearrange("p (c n) -> p c n", c=CHUNKS) for _ in range(2)]
        rope = [c(4 * BLOCK).rearrange("p (u n) -> p u n", u=4) for _ in range(2)]
        feat = [r.rearrange("p (w u) n -> p w (u n)", w=2) for r in rope]
        raw, rawT = rope[0][:, 0, :], rope[1][:, 0, :]
        mx = c(16 * 4).rearrange("p (i k) -> p i k", i=16)
        m16, mr, mr2 = c(16), c(16), c(16)
        nmx = c(P // 2, BF16)
        nm3 = nmx[:, 0:48].rearrange("p (r i) -> p r i", r=3)
        nmT = c(P // 2, BF16, parts=48)
        hmask, gate, gexp, gp, omg = c(8), c(HEADS), c(HEADS), c(HEADS), c(HEADS)
        mden = c(TILES * HEADS).rearrange("p (t h) -> p t h", t=TILES)
        memb = c(CHUNKS * 8 * MW).rearrange("p (c h n) -> p c h n", c=CHUNKS, h=8)
        rden = c(HEADS)
        flat = xnT[:].rearrange("p c n -> p (c n)")
        wo = flat[:, 0:CHUNKS * DIM].rearrange("p (k e) -> p k e", k=CHUNKS)
        oT = [flat[:, (CHUNKS + i) * DIM:(CHUNKS + i + 1) * DIM].rearrange("p (c n) -> p c n", c=2) for i in range(2)]
        tmp = c(DIM).rearrange("p (t n) -> p t n", t=16)
        comb = xn
        kfT = xnT[:].rearrange("p c n -> p (c n)").rearrange("p (t d) -> p t d", t=TILES)
        k_room, q_room = HPG * TOKENS // 2, HPG * BLOCK // 2
        v_at = 3 * (k_room + q_room)
        PARTS = 3 * CHUNKS * BLOCK // 2
        in_parts = lambda v: v.rearrange("p (r c n) -> p r c n", r=3, c=CHUNKS)
        c = Carve()
        c.at = k_room
        cs = c(2 * TOKENS).rearrange("p (w n) -> p w n", w=2)
        assert c.at == 2 * k_room
        parts = [in_parts(c(PARTS, BF16)) for _ in range(2)]
        wqk = c(2 * CHUNKS * DIM).rearrange("p (w k e) -> p w k e", w=2, k=CHUNKS)
        assert c.at <= 3 * k_room
        c.at = 3 * k_room + q_room
        parts.append(in_parts(c(PARTS, BF16)))
        wv = c(CHUNKS * DIM).rearrange("p (k e) -> p k e", k=CHUNKS)
        assert c.at <= v_at
        parts.append(in_parts(c(PARTS, BF16)))
        c.at = v_at + TILES * HPG * VW
        va = c(TILES * HEADS * VW).rearrange("p (t h n) -> p t h n", t=TILES, h=HEADS)
        xflat = xn[:].rearrange("p t d -> p (t d)")
        parts.append(in_parts(xflat[:, 0:PARTS].bitcast(BF16)))
        parts += parts[0:SPLITS - PBUFS]
        res = [xflat[:, PARTS + i * CHUNKS * BLOCK:PARTS + (i + 1) * CHUNKS * BLOCK].rearrange("p (c n) -> p c n", c=CHUNKS)
               for i in range(2)]

        def split_source(n):
            w, blk = 1 - n // BLOCKS, n % BLOCKS
            return qk[w][:, :, blk * BLOCK:(blk + 1) * BLOCK], (0.25 if w == 0 else 1.0)

        def third_made(n):
            return s[("part3e", "part3o")[n % 2]], n // 2 + 1

        def half_chunk(i):
            w, ch, half = 1 - i // 4, i // 2 % 2, i % 2
            return qk[w][:, ch, half * (TOKENS // 2):(half + 1) * (TOKENS // 2)]

        def sync(e):
            for w, name in enumerate(("Wq_T", "Wk_T")):
                e.dma_start(wqk[:, w], a[name].rearrange("(k p) e -> p k e", p=P)).then_inc(s["w"], 16)
            e.dma_start(wv, a["Wv_T"].rearrange("(k p) e -> p k e", p=P)).then_inc(s["w"], 16)
            e.dma_start(cs, a["rope"].rearrange("w p n -> p w n")).then_inc(s["cs"], 16)
            e.wait_ge(s_ready, n_ready)
            e.dma_start(gate, a["L1_attn_gate"].rearrange("a h b c -> a (h b c)").to_broadcast([P, HEADS])).then_inc(s["wg"], 16)
            e.dma_start(hmask, a["mask16"]).then_inc(s["wg"], 16)

            def store_parts(n, stored):
                w, blk = 1 - n // BLOCKS, n % BLOCKS
                e.wait_ge(*third_made(n))
                d = (q_dram, k_dram)[w]
                for ch in range(CHUNKS):
                    e.dma_start(d[:, ch * P:(ch + 1) * P, blk * BLOCK:(blk + 1) * BLOCK].rearrange("r p n -> p r n"),
                                parts[n][:, :, ch, :]).then_inc(stored, 16)

            def load(b, st):
                q, g = st // HGROUPS, st % HGROUPS
                rows, col = g * HPG * HD, q * BLOCK
                for d, dst, ps, cols in ((q_dram, QS[b], Q_PARTS, bass.ds(col, BLOCK)),
                                         (k_dram, KS[b], K_PARTS, slice(0, TOKENS))):
                    for i, part in enumerate(ps):
                        src = d[part, bass.ds(rows, HPG * HD), cols].rearrange("(h r) n -> r h n", r=HD)
                        e.dma_start(dst[HD * i:HD * (i + 1)], src).then_inc(s_ld[b], 16)

            def load_values(b, st):
                tile = st % HGROUPS * TILES
                e.dma_start(VS[b], v_dram[:, bass.ds(tile, TILES), :]).then_inc(s_lv[b], 16)

            def store_max(b, st):
                e.wait_ge(s["nms"], st + 1)
                e.dma_start(QS[b][STACK:STACK_M].rearrange("r h n -> r (h n)").rearrange("r (i n) -> r i n", n=P),
                            nmT).then_inc(s["mrow"], 16)

            for n in range(BLOCKS):
                store_parts(n, s["kd"])
            store_parts(BLOCKS, s["qd0"])
            e.wait_ge(s["kd"], 16 * CHUNKS * BLOCKS)
            e.wait_ge(s["qd0"], 16 * CHUNKS)
            load(0, 0)
            for n in range(PBUFS, SPLITS):
                store_parts(n, s["qd"])
            e.wait_ge(s["va"], TILES)
            e.wait_ge(s["onesr"], 1)
            for g in range(HGROUPS):
                e.dma_start(v_dram[:, TILES * g:TILES * (g + 1), :],
                            va[:, :, HPG * g:HPG * (g + 1), :].rearrange("p t h n -> p t (h n)")).then_inc(s["vd"], 16)
            e.wait_ge(s["qd"], 16 * CHUNKS * (BLOCKS - 1))
            e.wait_ge(s["vd"], 16 * HGROUPS)
            for ks in KS:
                e.dma_start(ks[STACK:STACK_M].rearrange("r h n -> r (h n)"), a["ones_rows"]).then_inc(s["keyones"], 16)
            load_values(0, 0)
            load(1, 1)
            load(2, 2)
            e.wait_ge(s["mem"], 1)
            e.dma_start(wo, a["Wo_T"].rearrange("(k p) e -> p k e", p=P)).then_inc(s["wo"], 16)
            load_values(1, 1)
            load_values(2, 2)
            store_max(0, 0)
            for st in range(STEPS - 1):
                store_max((st + 1) % 3, st + 1)
                if st + 3 < STEPS:
                    e.wait_ge(s["pv"], (st + 1) * 16)
                    load(st % 3, st + 3)
                    load_values(st % 3, st + 3)

        def pe(e):
            ln_pe(e)
            e.wait_ge(s["w"], 48)
            e.wait_ge(ln["xnT"], ln_base["xnT"] + TILES // 2)
            for n in range(SPLITS):
                w, blk = 1 - n // BLOCKS, n % BLOCKS
                if n >= 2:
                    e.wait_ge(s["rm"], n - 1)
                for ch in range(CHUNKS):
                    for k in range(CHUNKS):
                        ins = nc.tensor.matmul(bank[2 + 2 * (n % 2) + ch][:], wqk[:, w, k, ch * P:(ch + 1) * P],
                                               xnT[:, k, blk * BLOCK:(blk + 1) * BLOCK], start=(k == 0), stop=(k == 1))
                ins.then_inc(s["qk"], 1)
                values(e, n)
            for t in range(SPLITS, TILES):
                values(e, t)

            def key_rows(t):
                if t == 0:
                    e.wait_ge(s["kf"], 4)
                    e.wait_ge(s["va"], TILES)
                if t >= 2:
                    e.wait_ge(s["kfT"], t - 1)
                for ch in range(CHUNKS):
                    ins = nc.tensor.transpose(bank[t % 2][:, ch * P:(ch + 1) * P], qk[1][:, ch, t * P:(t + 1) * P], ident[:])
                ins.then_inc(s["kft"], 1)

            def memory(t):
                e.wait_ge(s["kfT"], t + 1)
                for ch in range(CHUNKS):
                    ins = nc.tensor.matmul(bank[2 + ch][:, 0:8 * MW], kfT[:, t, ch * P:(ch + 1) * P], va[:, t, 8 * ch:8 * ch + 8, 0:MW],
                                           start=(t == 0), stop=(t == TILES - 1))
                if t == TILES - 1:
                    ins.then_inc(s["mem"], 1)

            def recall(t):
                if t == 0:
                    e.wait_ge(s["qf"], 4)
                    e.wait_ge(s["memb"], 1)
                if t >= 2:
                    e.wait_ge(s["comb"], t - 1)
                for ch in range(CHUNKS):
                    ins = nc.tensor.matmul(bank[t % 2][:, ch * 8 * MW:(ch + 1) * 8 * MW], qk[0][:, ch, t * P:(t + 1) * P],
                                           memb[:, ch], start=True, stop=True)
                ins.then_inc(s["memo"], 1)

            def max_scores(b, m, j):
                h, qt, kc = j // 16, j // 4 % 4, j % 4
                if j == 0:
                    e.wait_ge(s_ld[b], 192 * (m // 3 + 1) if isinstance(m, int) else turn_of(b))
                if j == EARLY and not (isinstance(m, int) and m == 0):
                    e.wait_ge(s["nms"], m)
                elif not (isinstance(m, int) and m == 0 and j < 3):
                    e.wait_ge(s["mxd"], m * 64 + (j - 2))
                nc.tensor.matmul(bank[5 + (b + j) % 3], QS[b][0:STACK, h, qt * P:(qt + 1) * P],
                                 KS[b][0:STACK, h, kc * BLOCK:(kc + 1) * BLOCK], start=True, stop=True).then_inc(s["mx"], 1)

            def max_rows(b, m):
                e.wait_ge(s["nm"], m + 1)
                if not (isinstance(m, int) and m == STEPS - 1):
                    e.wait_ge(s["mxd"], (m + 1) * 64 + (EARLY - 2))
                nc.tensor.transpose(bank[5 + (b + 1 + EARLY) % 3].bitcast(BF16)[:, 0:P], nmx, ident_bf[:]).then_inc(s["nmt"], 1)

            def rows_of_sums(st):
                e.wait_ge(s["raw"], st + 2)
                for q in range(4):
                    ins = nc.tensor.transpose(bank[4][:, q * P:(q + 1) * P], raw[:, q * P:(q + 1) * P], ident[:])
                ins.then_inc(s["rt"], 1)

            turn = [None]

            def turn_of(b):
                return (turn[0] + 2) * 192

            def step(b, st, values_turn, first=False):
                static = isinstance(st, int)
                ahead = [(st + 1, (b + 1) % 3, 16 + i) for i in range(48)] + [(st + 2, (b + 2) % 3, i) for i in range(16)]
                if static:
                    ahead = [w if w[0] < STEPS else None for w in ahead]

                def maxima(n):
                    for _ in range(n):
                        if w := ahead.pop(0):
                            max_scores(w[1], w[0], w[2])

                e.wait_ge(s["mrow"], (st + 1) * 16)
                e.wait_ge(s["keyones"], 48)
                for kt in range(TILES + 1):
                    if kt == 12 + EARLY // 4 and not (static and st + 1 >= STEPS):
                        max_rows((b + 1) % 3, st + 1)
                    for pair in range(2):
                        if kt < TILES:
                            e.wait_ge(s["exp"], st * 32 + (2 * kt + pair + 1))
                            for h in (2 * pair, 2 * pair + 1):
                                ins = nc.tensor.matmul(bank[h], KS[b][0:STACK_M, h, kt * P:(kt + 1) * P],
                                                       QS[b][0:STACK_M, h, :], start=True, stop=True)
                            ins.then_inc(s["st"], 1)
                            maxima(2 - pair)
                    if kt == 0 and not first:
                        rows_of_sums(st - 1)
                    if kt >= 1:
                        if kt == 1:
                            e.wait_ge(s["rawT"], st + 1)
                            e.wait_ge(s_lv[b], values_turn)
                        e.wait_ge(s["exp"], st * 32 + (2 * kt + 2))
                        for h in range(HPG):
                            ins = nc.tensor.matmul(bank[4][VW * h:VW * (h + 1), :], VS[b][:, kt - 1, VW * h:VW * (h + 1)],
                                                   PT[(kt - 1) % 2][:, h, :], start=(kt == 1), stop=(kt == TILES))
                        ins.then_inc(s["pv"], 1)
                    if kt < TILES:
                        maxima(1)

            e.wait_ge(s["rm"], SPLITS)
            among = {KEYS_AT + t: (key_rows, t) for t in range(TILES)}
            among.update({KEYS_AT + TILES + t: (memory, t) for t in range(TILES)})
            among.update({RECALL_AT + t: (recall, t) for t in range(TILES)})
            for j in range(80):
                if j - 64 == EARLY:
                    max_rows(0, 0)
                max_scores(j // 64, j // 64, j % 64)
                if j in among:
                    do, t = among[j]
                    do(t)
            e.wait_ge(s["comb"], TILES)
            step(0, 0, 16, first=True)
            with e.Fori(0, 4) as i:
                turn[0] = i
                for r in (1, 2, 3):
                    step(r % 3, i * 3 + r, (i + (1 + r // 3)) * 16)
            for st in range(13, STEPS):
                step(st % 3, st, (st // 3 + 1) * 16)
            rows_of_sums(STEPS - 1)

            for q in range(BLOCKS):
                e.wait_ge(s["used"], HGROUPS * (q + 1))
                e.wait_ge(s["wo"], 16)
                for t in range(4 * q, 4 * q + 4):
                    for ch in range(CHUNKS):
                        ins = nc.tensor.transpose(bank[2 + t % 2][:, ch * P:(ch + 1) * P], comb[:, t, ch * P:(ch + 1) * P], ident[:])
                    ins.then_inc(s["ot"], 1)
                    if t >= 1:
                        project(e, t - 1)
            project(e, TILES - 1)

        def values(e, t):
            if t >= 2:
                e.wait_ge(s["va"], t - 1)
            for k in range(CHUNKS):
                ins = nc.tensor.matmul(bank[t % 2][:, 0:DIM], xnT[:, k, t * P:(t + 1) * P], wv[:, k], start=(k == 0), stop=(k == 1))
            ins.then_inc(s["v"], 1)

        def project(e, t):
            e.wait_ge(s["oT"], t + 1)
            if t >= 2:
                e.wait_ge(s["out"], t - 1)
            for ch in range(CHUNKS):
                ins = nc.tensor.matmul(bank[6 + t % 2][:, 0:DIM], oT[t % 2][:, ch], wo[:, ch], start=(ch == 0), stop=(ch == 1))
            ins.then_inc(s["pj"], 1)

        def act(e):
            ln_act(e)

            def first_part(n):
                src, scale = split_source(n)
                e.wait_ge(s["ra"], n + 1)
                if n >= PBUFS:
                    e.wait_ge(s["kd"], 16 * CHUNKS * BLOCKS)
                nc.scalar.activation(parts[n][:, 0], src, ACT.Copy, scale=scale).then_inc(s["split"], 1)

            def second_part(n):
                e.wait_ge(s["exk"], n + 1)
                nc.scalar.copy(parts[n][:, 1], res[n % 2]).then_inc(s["part2"], 1)

            def values(t):
                e.wait_ge(s["v"], t + 1)
                nc.scalar.copy(va[:, t, :, 0:HD], bank[t % 2][:, 0:DIM].rearrange("p (h n) -> p h n", h=HEADS)).then_inc(s["va"], 1)

            for n in range(SPLITS):
                values(n)
                if n >= 1:
                    first_part(n - 1)
                    second_part(n - 1)
            values(SPLITS)
            values(SPLITS + 1)
            first_part(SPLITS - 1)
            values(SPLITS + 2)
            values(SPLITS + 3)
            second_part(SPLITS - 1)
            for t in range(SPLITS + 4, TILES):
                values(t)
            e.wait_ge(s["wg"], 32)
            nc.scalar.activation(gexp, gate, ACT.Exp, scale=-1.0).then_inc(s["gex"], 1)
            def feature_factors(i):
                src, (made, used) = half_chunk(i), (("kexp", "kf"), ("qexp", "qf"))[i // 4]
                if i >= 2:
                    before = i - 1
                    e.wait_ge(s["kf"], min(before, 4))
                    if before > 4:
                        e.wait_ge(s["qf"], before - 4)
                nc.scalar.activation(feat[i % 2][:, 0], src, ACT.Exp)
                nc.scalar.activation(feat[i % 2][:, 1], src, ACT.Relu).then_inc(s[made], 1)

            for i in range(6):
                feature_factors(i)
            e.wait_ge(s["gex"], 1)
            nc.scalar.copy(tmp[:, 0, 0:1], gexp[:, 0:1]).then_inc(s["exp"], 2)
            nc.scalar.copy(tmp[:, 1, 0:1], gexp[:, 0:1]).then_inc(s["raw"], 1)
            nc.scalar.copy(tmp[:, 2, 0:1], gexp[:, 0:1]).then_inc(s["rawT"], 1)
            for t in range(TILES):
                e.wait_ge(s["kft"], t + 1)
                nc.scalar.copy(kfT[:, t, :], bank[t % 2][:, 0:DIM]).then_inc(s["kfT"], 1)
                if t in LATE_FACTORS:
                    feature_factors(6 + LATE_FACTORS.index(t))
            e.wait_ge(s["mem"], 1)
            nc.scalar.copy(memb, psum[:, 2 * 512:4 * 512].rearrange("p (c n) -> p c n", c=2)[:, :, 0:8 * MW]
                           .rearrange("p c (h n) -> p c h n", h=8)).then_inc(s["memc"], 1)
            for t in range(TILES):
                e.wait_ge(s["memo"], t + 1)
                o = bank[t % 2][:, 0:HEADS * MW].rearrange("p (h n) -> p h n", h=HEADS)
                nc.scalar.copy(mden[:, t, :], o[:, :, HD])
                nc.scalar.copy(comb[:, t, :].rearrange("p (h n) -> p h n", h=HEADS), o[:, :, 0:HD]).then_inc(s["comb"], 1)

            def step(st, first=False):
                for kt in range(TILES):
                    for pair in range(2):
                        e.wait_ge(s["st"], st * 32 + (2 * kt + pair + 1))
                        nc.scalar.activation(PT[kt % 2][:, 2 * pair:2 * pair + 2, :],
                                             psum[:, 2 * pair * 512:(2 * pair + 2) * 512].rearrange("p (h n) -> p h n", h=2),
                                             ACT.Exp).then_inc(s["exp"], 1)
                    if kt == 0 and not first:
                        rows_of_sums(st - 1)
                e.wait_ge(s["pv"], st * 16 + 16)
                nc.scalar.copy(raw, bank[4][:]).then_inc(s["raw"], 1)

            def rows_of_sums(st):
                e.wait_ge(s["rt"], st + 1)
                if not (isinstance(st, int) and st == 0):
                    e.wait_ge(s["used"], st)
                nc.scalar.copy(rawT, bank[4][:]).then_inc(s["rawT"], 1)

            step(0, first=True)
            step(1)
            with e.Fori(2, STEPS) as st:
                step(st)
            rows_of_sums(STEPS - 1)
            for t in range(TILES):
                e.wait_ge(s["ot"], t + 1)
                if t >= 2:
                    e.wait_ge(s["pj"], t - 1)
                nc.scalar.copy(oT[t % 2], bank[2 + t % 2][:, 0:DIM].rearrange("p (c n) -> p c n", c=2)).then_inc(s["oT"], 1)

        def dve(v):
            link = chains["dve"]
            ln_dve(v)

            def residue(n):
                src, scale = split_source(n)
                v.wait_ge(s["split"], n + 1)
                if n >= 2:
                    v.wait_ge(*third_made(n - 2))
                nc.vector.scalar_tensor_tensor(out=res[n % 2], in0=src, scalar=scale, in1=parts[n][:, 0],
                                               op0=ALU.mult, op1=ALU.subtract).then_inc(s["exk"], 1)

            def third_part(n):
                v.wait_ge(s["part2"], n + 1)
                nc.vector.tensor_tensor(parts[n][:, 2], res[n % 2], parts[n][:, 1], ALU.subtract).then_inc(s["part3e"], 1)

            v.wait_ge(s["cs"], 16)
            for n in range(SPLITS):
                blk = n % BLOCKS
                v.wait_ge(s["qk"], n + 1)
                if n >= 2:
                    v.wait_ge(s["ra"], n - 1)
                cols = slice(blk * BLOCK, (blk + 1) * BLOCK)
                for u, (ch, w) in enumerate(((0, 0), (1, 1), (1, 0), (0, 1))):
                    ins = nc.vector.tensor_tensor(rope[n % 2][:, u, :], bank[2 + 2 * (n % 2) + ch][:], cs[:, w, cols], ALU.mult)
                ins.then_inc(s["rm"], 1)
                if n >= 2 and n % 2 == 0:
                    third_part(n - 2)
                if n >= 1:
                    residue(n - 1)
            third_part(SPLITS - 2)
            residue(SPLITS - 1)
            nc.vector.memset(nmx, 0.0)

            def key_features(i):
                v.wait_ge(s["kexp"], i + 1)
                nc.vector.scalar_tensor_tensor(out=half_chunk(i), in0=feat[i % 2][:, 0], scalar=1.0, in1=feat[i % 2][:, 1],
                                               op0=ALU.min, op1=ALU.add).then_inc(s["kf"], 1)

            def maxima(m, js, r):
                for j in js:
                    v.wait_ge(s["mx"], m * 64 + (j + 1))
                    nc.vector.tensor_reduce(mx[:, j // 4, j % 4:j % 4 + 1], bank[5 + (r + j) % 3], AX_X, ALU.max).then_inc(s["mxd"], 1)

            def negated(m):
                v.wait_ge(s["mxd"], m * 64 + 64)
                link(nc.vector.tensor_reduce(m16, mx, AX_X, ALU.max))
                link(nc.vector.tensor_scalar(nm3[:, 0, :], m16, -1.0, None, ALU.mult))
                link(nc.vector.scalar_tensor_tensor(out=mr, in0=m16, scalar=-1.0, in1=nm3[:, 0, :], op0=ALU.mult, op1=ALU.subtract))
                link(nc.vector.tensor_copy(nm3[:, 1, :], mr))
                link(nc.vector.tensor_tensor(mr2, mr, nm3[:, 1, :], ALU.subtract))
                nc.vector.tensor_copy(nm3[:, 2, :], mr2).then_inc(s["nm"], 1)

            def rows(m, r):
                v.wait_ge(s["nmt"], m + 1)
                if not (isinstance(m, int) and m == 0):
                    v.wait_ge(s["mrow"], m * 16)
                nc.vector.tensor_copy(nmT, bank[5 + (r + 1 + EARLY) % 3].bitcast(BF16)[0:48, 0:P]).then_inc(s["nms"], 1)

            def denominators(st):
                v.wait_ge(s["rawT"], st + 2)
                if not (isinstance(st, int) and st == 0):
                    v.wait_ge(s["used"], st)
                nc.vector.reciprocal(rden, rawT.rearrange("p (i n) -> p i n", n=VW)[:, :, HD]).then_inc(s["rden"], 1)

            def turn(m, r):
                maxima(m, range(EARLY if r else 0, 64), r % 3)
                if r >= 2:
                    denominators(m - 2)
                negated(m)
                maxima(m + 1, range(EARLY), (r + 1) % 3)
                rows(m, r % 3)

            for i in range(4):
                maxima(0, range(FEAT * i, FEAT * (i + 1)), 0)
                key_features(i)
            v.wait_ge(s["gex"], 1)
            link(nc.vector.tensor_scalar(gp, gexp, 1.0, None, ALU.add))
            link(nc.vector.reciprocal(gp, gp))
            link(nc.vector.tensor_scalar(omg, gp, -1.0, 1.0, ALU.mult, ALU.add))
            maxima(0, range(4 * FEAT, 64), 0)
            negated(0)
            maxima(1, range(EARLY), 1)
            rows(0, 0)
            v.wait_ge(s["comb"], TILES)
            link(nc.vector.reciprocal(mden, mden))
            nc.vector.tensor_tensor(mden, mden, gp.rearrange("p (o h) -> p o h", o=1).to_broadcast([P, TILES, HEADS]),
                                    ALU.mult).then_inc(s["mden"], 1)
            turn(1, 1)
            turn(2, 2)
            with v.Fori(0, 4) as i:
                link.enter(i, 15)
                for r in (3, 4, 5):
                    turn(i * 3 + r, r)
                link.leave(4)
            maxima(STEPS - 1, range(EARLY, 64), (STEPS - 1) % 3)
            denominators(STEPS - 3)
            negated(STEPS - 1)
            rows(STEPS - 1, (STEPS - 1) % 3)
            denominators(STEPS - 2)
            denominators(STEPS - 1)
            for t in range(TILES):
                v.wait_ge(s["pj"], t + 1)
                nc.vector.tensor_tensor(x[:, t, :], bank[6 + t % 2][:, 0:DIM], x[:, t, :], ALU.add).then_inc(s["out"], 1)
                out_stats(v, s["out"], 0, t, tag)

        def pool(e):
            link = chains["pool"]
            ln_pool(e)
            e.wait_ge(s_ready, n_ready)
            nc.gpsimd.memset(va[:, :, :, HD:VW], 1.0).then_inc(s["onesr"], 1)

            def third_part(n):
                e.wait_ge(s["part2"], n + 1)
                nc.gpsimd.tensor_tensor(parts[n][:, 2], res[n % 2], parts[n][:, 1], ALU.subtract).then_inc(s["part3o"], 1)

            for n in range(SPLITS):
                w, blk = 1 - n // BLOCKS, n % BLOCKS
                cols = slice(blk * BLOCK, (blk + 1) * BLOCK)
                e.wait_ge(s["rm"], n + 1)
                r = rope[n % 2]
                nc.gpsimd.tensor_tensor(qk[w][:, 0, cols], r[:, 0, :], r[:, 1, :], ALU.subtract)
                nc.gpsimd.tensor_tensor(qk[w][:, 1, cols], r[:, 2, :], r[:, 3, :], ALU.add).then_inc(s["ra"], 1)
                if n >= 2 and n % 2 == 0:
                    third_part(n - 1)
            third_part(SPLITS - 1)
            for i in range(4, 8):
                e.wait_ge(s["qexp"], i - 3)
                link(nc.gpsimd.tensor_scalar(feat[i % 2][:, 0], feat[i % 2][:, 0], 1.0, None, ALU.min))
                nc.gpsimd.tensor_tensor(half_chunk(i), feat[i % 2][:, 0], feat[i % 2][:, 1], ALU.add).then_inc(s["qf"], 1)
            e.wait_ge(s["memc"], 1)
            e.wait_ge(s["wg"], 32)
            for ch in range(CHUNKS):
                ins = nc.gpsimd.tensor_tensor(memb[:, ch], memb[:, ch],
                                              hmask.rearrange("p (h o) -> p h o", o=1).to_broadcast([P, 8, MW]), ALU.mult)
            ins.then_inc(s["memb"], 1)
            e.wait_ge(s["mden"], 1)
            for q in range(4):
                v = comb[:, 4 * q:4 * q + 4, :].rearrange("p t d -> p (t d)").rearrange("p (i n) -> p i n", n=HD)
                d = mden[:, 4 * q:4 * q + 4, :].rearrange("p t h -> p (t h)").rearrange("p (i o) -> p i o", o=1)
                ins = nc.gpsimd.tensor_tensor(v, v, d.to_broadcast([P, 4 * HEADS, HD]), ALU.mult)
            link(ins)
            with e.Fori(0, BLOCKS) as q:
                link.enter(q, 2 * HGROUPS)
                for g in range(HGROUPS):
                    e.wait_ge(s["rawT"], q * HGROUPS + (g + 2))
                    o = rawT.rearrange("p (i n) -> p i n", n=VW)
                    e.wait_ge(s["rden"], q * HGROUPS + (g + 1))
                    rd = rden.rearrange("p (q h) -> p q h", h=HPG)
                    link(nc.gpsimd.tensor_tensor(rd, rd, omg[:, HPG * g:HPG * (g + 1)].rearrange("p (o h) -> p o h", o=1).to_broadcast([P, 4, HPG]),
                                                 ALU.mult))
                    link(nc.gpsimd.tensor_tensor(tmp, o[:, :, 0:HD], rden.rearrange("p (i o) -> p i o", o=1).to_broadcast([P, 16, HD]), ALU.mult))
                    cv = comb[:, bass.ds(q * 4, 4), HPG * HD * g:HPG * HD * (g + 1)]
                    nc.gpsimd.tensor_tensor(cv, cv, tmp.rearrange("p (q h) n -> p q (h n)", q=4), ALU.add).then_inc(s["used"], 1)
                link.leave(BLOCKS)

        room_free = (s["pv"], 16 * STEPS)
        return (s["out"], TILES), dict(room_free=room_free, sync=sync, tensor=pe, scalar=act, vector=dve, gpsimd=pool)

    layers = []
    ready, before = (s_x[0], 16), None
    makers = [moe, linear_attention, moe, head_mixer, softmax_attention, head_mixer]
    for n, mk in enumerate(makers[:stages]):
        more = (layers[-1]["room_free"],) if mk is head_mixer else ()
        ready, progs = mk(f"l{n}", *ready, before, *more)
        before = "moe" if mk is moe else f"l{n}"
        layers.append(progs)

    block = ctx.enter_context(nc.Block())
    s_out = sem("stored")

    @block.sync
    def _(e):
        e.dma_start(ident[:], a["ident"]).then_inc(s_const, 16)
        src = a["L0_attn_x"][0].rearrange("(t p) d -> p t d", p=P)
        for i in range(4):
            e.dma_start(x[:, 4 * i:4 * i + 4], src[:, 4 * i:4 * i + 4]).then_inc(s_x[i], 16)
        for pr in layers:
            if "sync" in pr:
                pr["sync"](e)
        done, count = ready
        dst = out[0].rearrange("(t p) d -> p t d", p=P)
        for lo, hi in STORES:
            e.wait_ge(done, count - (TILES - hi) if stages == 6 else count)
            e.dma_start(dst[:, lo:hi], x[:, lo:hi]).then_inc(s_out, 16)
        e.wait_ge(s_out, 16 * len(STORES))

    @block.tensor
    def _(e):
        e.wait_ge(s_const, 16)
        e.wait_ge(s_const2, 1)
        for pr in layers:
            pr["tensor"](e)

    @block.scalar
    def _(e):
        chains["act"] = Chain(e, chain_sems["act"])
        for pr in layers:
            pr["scalar"](e)

    @block.vector
    def _(e):
        chains["dve"] = Chain(e, chain_sems["dve"])
        e.wait_ge(s_const, 16)
        nc.vector.tensor_copy(ident_bf[:], ident[:]).then_inc(s_const2, 1)
        for pr in layers:
            pr["vector"](e)

    @block.gpsimd
    def _(e):
        chains["pool"] = Chain(e, chain_sems["pool"])
        for pr in layers:
            if "gpsimd" in pr:
                pr["gpsimd"](e)


def constants():
    f = np.float32
    c = {}
    c["ident"] = np.eye(P, dtype=f)
    c["iota_row"] = np.tile(TOKENS - np.arange(TOKENS // 2, dtype=f), (P, 1))
    c["key_off"] = np.where(np.arange(P) < EXPERTS, 0, -TOKENS // 2).astype(f).reshape(P, 1)
    c["ones_rows"] = np.ones((3, HPG * TOKENS), dtype=mybir.dt.np(BF16))
    c["iota_bf"] = np.tile(np.arange(P, dtype=f), (P, 1)).astype(mybir.dt.np(BF16))
    c["tile_off"] = np.tile(P * np.arange(TILES + 1, dtype=f), (P, 1))
    c["pair_starts"] = (2 * P * np.arange(TILES // 2, dtype=f)).reshape(1, -1)
    c["mask32"] = (np.arange(P)[:, None] // LHD == np.arange(P // LHD)[None, :]).astype(f)
    c["mask16"] = (np.arange(P)[:, None] // HD == np.arange(P // HD)[None, :]).astype(f)
    c["iota8"] = np.tile(np.arange(MIX_EXPERTS, dtype=f), (P, 1))
    inv = (1.0 / np.float32(10000.0) ** (np.arange(0, DIM, 2, dtype=f) / f(DIM))).astype(f)
    angle = (np.arange(TOKENS, dtype=f)[None, :] * inv[:, None]).astype(f).astype(np.float64)
    c["rope"] = np.stack([np.cos(angle), np.sin(angle)]).astype(f)
    c["slot_mask"] = (np.arange(P)[:, None] // CAP == np.arange(EPG)[None, :]).astype(f)
    return c


def host_arrays(inputs):
    t = lambda w: np.ascontiguousarray(np.swapaxes(w, -1, -2))
    d = {k: np.asarray(v) for k, v in inputs.items()}
    d["gate_T"] = t(d.pop("L0_ffn_gate_w"))
    qkv = d.pop("L0_attn_w_qkv")
    d["wq_T"], d["wkv_T"] = t(qkv[:DIM]), t(qkv[DIM:])
    d["wproj_T"] = t(d.pop("L0_attn_w_proj"))
    for w in ("Wq", "Wk", "Wv", "Wo"):
        d[w + "_T"] = t(d.pop("L1_attn_" + w))
    d["w3_T"] = t(d.pop("L1_ffn_w3"))
    for w in ("w1", "w2"):
        v = np.transpose(d.pop("L1_ffn_" + w), (2, 0, 1))
        d[w + "_rep"] = np.ascontiguousarray(np.tile(v, (P // HD, 1, 1)))
    for b in ("b1", "b2"):
        d[b + "_rep"] = np.ascontiguousarray(np.tile(d.pop("L1_ffn_" + b).T, (P // HD, 1)))
    d.update(constants())
    return d


def kernel(stages=6, **inputs):
    import concourse.bacc as _bacc
    from concourse.bass_utils import run_bass_kernel_spmd as _run

    nc = _bacc.Bacc("TRN2", target_bir_lowering=False, num_devices=1)
    arrays, a = {}, {}
    for name, v in host_arrays(inputs).items():
        arrays[f"in_{name}"] = v
        a[name] = nc.dram_tensor(f"in_{name}", v.shape, mybir.dt.from_np(v.dtype), kind="ExternalInput").ap()
    out = nc.dram_tensor("out_0", (1, TOKENS, DIM), F32, kind="ExternalOutput").ap()
    build(nc, a, out, stages)
    r = _run(nc, [arrays], core_ids=[0])
    return r.results[0]["out_0"]
```
